# Optimizing a Trainium2 kernel written in Bass

```python
import numpy as np
import jax
import jax.numpy as jnp

def _softmax(x, axis=-1):
    return jax.nn.softmax(x, axis=axis)

def _gelu(x):
    return jax.nn.gelu(x, approximate=True)

def _silu(x):
    return jax.nn.silu(x)

def _sigmoid(x):
    return jax.nn.sigmoid(x)

def _layernorm(x, axis=-1, eps=1e-05):
    m = jnp.mean(x, axis=axis, keepdims=True)
    v = jnp.var(x, axis=axis, keepdims=True)
    return (x - m) / jnp.sqrt(v + eps)

def _scatter_add(tgt, idx, src, axis=0):
    return tgt.at[idx].add(src)

def _segment_sum(src, seg, n):
    return jax.ops.segment_sum(src, seg, n)
kernel_name = 'mk_gps_d1_gnn_r8_4fe827'

def setup_inputs(seed: int=0):
    np.random.seed(seed)
    _w = jnp.asarray

    def _rec_inputs():
        import jax
        import jax.numpy as jnp
        _gk = jax.random.key(seed)
        x = -0.0002117 + 1 * jax.random.normal(jax.random.fold_in(_gk, 1), (6250, 512), jnp.float32)
        src = jax.random.randint(jax.random.fold_in(_gk, 2), (100000,), 0, 6250, jnp.int32)
        dst = jnp.minimum((6250 * jax.random.uniform(jax.random.fold_in(_gk, 3), (100000,)) ** 2.0).astype(jnp.int32), 49999)
        _o = jnp.argsort(dst, stable=True)
        src = src[_o]
        dst = dst[_o]
        return (x, src, dst)
    x, src, dst = _rec_inputs()

    def _L0_gnn_setup():
        import jax, jax.numpy as jnp
        import numpy as np
        N_NODES = 6250
        D_IN = 512
        D_OUT = 512
        N_EDGES = 100000
        key = jax.random.key(seed)
        kx, ke, k1, k2, k3, k4 = jax.random.split(key, 6)
        x = jax.random.normal(kx, (N_NODES, D_IN), dtype=jnp.float32)
        edge_index = jax.random.randint(ke, (2, N_EDGES), 0, N_NODES, dtype=jnp.int64)
        b1lim = 1.0 / np.sqrt(D_IN)
        b2lim = 1.0 / np.sqrt(D_OUT)
        W1 = jax.random.uniform(k1, (D_IN, D_OUT), jnp.float32, -b1lim, b1lim)
        b1 = jax.random.uniform(k2, (D_OUT,), jnp.float32, -b1lim, b1lim)
        W2 = jax.random.uniform(k3, (D_OUT, D_OUT), jnp.float32, -b2lim, b2lim)
        b2 = jax.random.uniform(k4, (D_OUT,), jnp.float32, -b2lim, b2lim)
        return {'x': x, 'edge_index': edge_index, 'W1': W1, 'b1': b1, 'W2': W2, 'b2': b2}
    _L0_gnn_all = _L0_gnn_setup()
    _L0_gnn_in = {k: v for k, v in _L0_gnn_all.items() if k in ('W1', 'b1', 'W2', 'b2')}
    del _L0_gnn_all

    def _L0_mix_setup():
        import jax, jax.numpy as jnp
        import numpy as np
        NUM_HEADS = 8
        key = jax.random.key(seed)
        k1, k2, k3 = jax.random.split(key, 3)
        B, N, C = (4, 512, 512)
        x = jax.random.normal(k1, (B, N, C), dtype=jnp.float32)
        w_qkv = jax.random.normal(k2, (C, 3 * C), dtype=jnp.float32) * (1.0 / np.sqrt(C))
        w_proj = jax.random.normal(k3, (C, C), dtype=jnp.float32) * (1.0 / np.sqrt(C))
        b_proj = jnp.zeros((C,), dtype=jnp.float32)
        return {'x': x, 'w_qkv': w_qkv, 'w_proj': w_proj, 'b_proj': b_proj}
    _L0_mix_all = _L0_mix_setup()
    _L0_mix_in = {k: v for k, v in _L0_mix_all.items() if k in ('w_qkv', 'w_proj', 'b_proj')}
    del _L0_mix_all

    def _L0_ffn_setup():
        import math
        import jax, jax.numpy as jnp
        import numpy as np
        B, T, D, FF, E = (32, 1024, 512, 256, 8)
        CAPACITY_FACTOR = 1.25
        CAP = int(math.ceil(CAPACITY_FACTOR * B * T / E))

        def _bank_residual(x2, Wr, br, W1, b1, W2, b2):
            N, d = x2.shape
            e = Wr.shape[1]
            logits = x2 @ Wr + br
            probs = jax.nn.softmax(logits, axis=-1)
            expert = jnp.argmax(probs, axis=-1)
            gate = jnp.take_along_axis(probs, expert[:, None], axis=-1)[:, 0]
            oneh = jax.nn.one_hot(expert, e, dtype=x2.dtype)
            pos = (jnp.cumsum(oneh, axis=0) * oneh).sum(-1).astype(jnp.int32) - 1
            keep = pos < CAP
            slot = expert.astype(jnp.int32) * CAP + jnp.minimum(pos, CAP - 1)
            xd = jnp.where(keep[:, None], x2, 0.0)
            buf = jnp.zeros((e * CAP, d), x2.dtype).at[slot].add(xd)
            buf = buf.reshape(e, CAP, d)
            h = jax.nn.gelu(jnp.einsum('ecd,edf->ecf', buf, W1) + b1[:, None, :], approximate=False)
            out = jnp.einsum('ecf,efd->ecd', h, W2) + b2[:, None, :]
            y = out.reshape(e * CAP, d)[slot]
            return y * (gate * keep.astype(x2.dtype))[:, None]
        key = jax.random.key(seed)
        ks = jax.random.split(key, 18)
        s = 0.02
        inp = {'x': jax.random.normal(ks[0], (B, T, D), dtype=jnp.float32), 'Wr_sp': jax.random.normal(ks[1], (D, E)) * s, 'br_sp': jnp.zeros((E,), jnp.float32), 'Wr_fq': jax.random.normal(ks[2], (D, E)) * s, 'br_fq': jnp.zeros((E,), jnp.float32), 'Ws1': jax.random.normal(ks[3], (D, FF)) * s, 'bs1': jnp.zeros((FF,), jnp.float32), 'Ws2': jax.random.normal(ks[4], (FF, D)) * s, 'bs2': jnp.zeros((D,), jnp.float32), 'W1_sp': jax.random.normal(ks[5], (E, D, FF)) * s, 'b1_sp': jnp.zeros((E, FF), jnp.float32), 'W2_sp': jax.random.normal(ks[6], (E, FF, D)) * s, 'b2_sp': jnp.zeros((E, D), jnp.float32), 'W1_fq': jax.random.normal(ks[7], (E, D, FF)) * s, 'b1_fq': jnp.zeros((E, FF), jnp.float32), 'W2_fq': jax.random.normal(ks[8], (E, FF, D)) * s, 'b2_fq': jnp.zeros((E, D), jnp.float32)}
        return inp
    _L0_ffn_all = _L0_ffn_setup()
    _L0_ffn_in = {k: v for k, v in _L0_ffn_all.items() if k in ('Wr_sp', 'br_sp', 'Wr_fq', 'br_fq', 'Ws1', 'bs1', 'Ws2', 'bs2', 'W1_sp', 'b1_sp', 'W2_sp', 'b2_sp', 'W1_fq', 'b1_fq', 'W2_fq', 'b2_fq')}
    del _L0_ffn_all
    return {'x': x, 'src': src, 'dst': dst, 'L0_gnn_W1': _L0_gnn_in['W1'], 'L0_gnn_b1': _L0_gnn_in['b1'], 'L0_gnn_W2': _L0_gnn_in['W2'], 'L0_gnn_b2': _L0_gnn_in['b2'], 'L0_mix_w_qkv': _L0_mix_in['w_qkv'], 'L0_mix_w_proj': _L0_mix_in['w_proj'], 'L0_mix_b_proj': _L0_mix_in['b_proj'], 'L0_ffn_Wr_sp': _L0_ffn_in['Wr_sp'], 'L0_ffn_br_sp': _L0_ffn_in['br_sp'], 'L0_ffn_Wr_fq': _L0_ffn_in['Wr_fq'], 'L0_ffn_br_fq': _L0_ffn_in['br_fq'], 'L0_ffn_Ws1': _L0_ffn_in['Ws1'], 'L0_ffn_bs1': _L0_ffn_in['bs1'], 'L0_ffn_Ws2': _L0_ffn_in['Ws2'], 'L0_ffn_bs2': _L0_ffn_in['bs2'], 'L0_ffn_W1_sp': _L0_ffn_in['W1_sp'], 'L0_ffn_b1_sp': _L0_ffn_in['b1_sp'], 'L0_ffn_W2_sp': _L0_ffn_in['W2_sp'], 'L0_ffn_b2_sp': _L0_ffn_in['b2_sp'], 'L0_ffn_W1_fq': _L0_ffn_in['W1_fq'], 'L0_ffn_b1_fq': _L0_ffn_in['b1_fq'], 'L0_ffn_W2_fq': _L0_ffn_in['W2_fq'], 'L0_ffn_b2_fq': _L0_ffn_in['b2_fq']}

def reference(x, src, dst, L0_gnn_W1, L0_gnn_b1, L0_gnn_W2, L0_gnn_b2, L0_mix_w_qkv, L0_mix_w_proj, L0_mix_b_proj, L0_ffn_Wr_sp, L0_ffn_br_sp, L0_ffn_Wr_fq, L0_ffn_br_fq, L0_ffn_Ws1, L0_ffn_bs1, L0_ffn_Ws2, L0_ffn_bs2, L0_ffn_W1_sp, L0_ffn_b1_sp, L0_ffn_W2_sp, L0_ffn_b2_sp, L0_ffn_W1_fq, L0_ffn_b1_fq, L0_ffn_W2_fq, L0_ffn_b2_fq):
    import jax
    import jax.numpy as jnp

    def _L0_gnn_ref(x, edge_index, W1, b1, W2, b2):
        import jax, jax.numpy as jnp
        import numpy as np
        N_NODES = 6250
        D_IN = 512
        D_OUT = 512
        N_EDGES = 100000
        src, dst = (edge_index[0], edge_index[1])
        agg = jax.ops.segment_sum(x[src], dst, num_segments=N_NODES)
        h = x + agg
        h = jax.nn.relu(h @ W1 + b1)
        h = h @ W2 + b2
        return jax.nn.relu(h)

    def _L0_mix_ref(x, w_qkv, w_proj, b_proj):
        import jax, jax.numpy as jnp
        import numpy as np
        NUM_HEADS = 8
        B, N, C = x.shape
        H = NUM_HEADS
        D = C // H
        qkv = (x @ w_qkv).reshape(B, N, 3, H, D)
        qkv = jnp.transpose(qkv, (2, 0, 3, 1, 4))
        q, k, v = (qkv[0], qkv[1], qkv[2])
        q = jax.nn.softmax(q, axis=-1)
        k = jax.nn.softmax(jax.nn.elu(k) + 1.0, axis=-2)
        context = jnp.einsum('bhnd,bhne->bhde', k, v)
        out = jnp.einsum('bhnd,bhde->bhne', q, context)
        out = jnp.transpose(out, (0, 2, 1, 3)).reshape(B, N, C)
        return out @ w_proj + b_proj

    def _L0_ffn_ref(x, Wr_sp, br_sp, Wr_fq, br_fq, Ws1, bs1, Ws2, bs2, W1_sp, b1_sp, W2_sp, b2_sp, W1_fq, b1_fq, W2_fq, b2_fq):
        import math
        import jax, jax.numpy as jnp
        import numpy as np
        B, T, D, FF, E = (32, 1024, 512, 256, 8)
        CAPACITY_FACTOR = 1.25
        CAP = int(math.ceil(CAPACITY_FACTOR * B * T / E))

        def _bank_residual(x2, Wr, br, W1, b1, W2, b2):
            N, d = x2.shape
            e = Wr.shape[1]
            logits = x2 @ Wr + br
            probs = jax.nn.softmax(logits, axis=-1)
            expert = jnp.argmax(probs, axis=-1)
            gate = jnp.take_along_axis(probs, expert[:, None], axis=-1)[:, 0]
            oneh = jax.nn.one_hot(expert, e, dtype=x2.dtype)
            pos = (jnp.cumsum(oneh, axis=0) * oneh).sum(-1).astype(jnp.int32) - 1
            keep = pos < CAP
            slot = expert.astype(jnp.int32) * CAP + jnp.minimum(pos, CAP - 1)
            xd = jnp.where(keep[:, None], x2, 0.0)
            buf = jnp.zeros((e * CAP, d), x2.dtype).at[slot].add(xd)
            buf = buf.reshape(e, CAP, d)
            h = jax.nn.gelu(jnp.einsum('ecd,edf->ecf', buf, W1) + b1[:, None, :], approximate=False)
            out = jnp.einsum('ecf,efd->ecd', h, W2) + b2[:, None, :]
            y = out.reshape(e * CAP, d)[slot]
            return y * (gate * keep.astype(x2.dtype))[:, None]
        b, t, d = x.shape
        x2 = x.reshape(b * t, d)
        shared = jax.nn.gelu(x2 @ Ws1 + bs1, approximate=False) @ Ws2 + bs2
        y = shared
        y = y + _bank_residual(x2, Wr_sp, br_sp, W1_sp, b1_sp, W2_sp, b2_sp)
        y = y + _bank_residual(x2, Wr_fq, br_fq, W1_fq, b1_fq, W2_fq, b2_fq)
        return y.reshape(b, t, d)
    edge_index = jnp.stack([src, dst])
    xn = _layernorm(x, axis=-1)
    x = x + _L0_gnn_ref(xn, edge_index, L0_gnn_W1, L0_gnn_b1, L0_gnn_W2, L0_gnn_b2) + _L0_mix_ref(xn[None], L0_mix_w_qkv, L0_mix_w_proj, L0_mix_b_proj)[0]
    x = x + _L0_ffn_ref(_layernorm(x, axis=-1)[None], L0_ffn_Wr_sp, L0_ffn_br_sp, L0_ffn_Wr_fq, L0_ffn_br_fq, L0_ffn_Ws1, L0_ffn_bs1, L0_ffn_Ws2, L0_ffn_bs2, L0_ffn_W1_sp, L0_ffn_b1_sp, L0_ffn_W2_sp, L0_ffn_b2_sp, L0_ffn_W1_fq, L0_ffn_b1_fq, L0_ffn_W2_fq, L0_ffn_b2_fq)[0]
    return x

_drawn_inputs = setup_inputs


def setup_inputs(seed=0):
    import zlib

    import numpy as np

    out = dict(_drawn_inputs(seed))
    spreads = {'L0_mix_b_proj': (0.0, 0.527),
     'L0_ffn_br_sp': (0.0, 0.642),
     'L0_ffn_br_fq': (0.0, 0.783),
     'L0_ffn_bs1': (0.0, 2.0),
     'L0_ffn_bs2': (0.0, 0.565),
     'L0_ffn_b1_sp': (0.0, 2.0),
     'L0_ffn_b2_sp': (0.0, 1.767),
     'L0_ffn_b1_fq': (0.0, 2.0),
     'L0_ffn_b2_fq': (0.0, 1.835)}
    factors = {'L0_gnn_b1': 49.947,
     'L0_gnn_b2': 17.512,
     'L0_mix_w_qkv': 4.438,
     'L0_mix_w_proj': 4.451,
     'L0_ffn_W1_sp': 3.829,
     'L0_ffn_W2_sp': 3.629,
     'L0_ffn_W1_fq': 3.95,
     'L0_ffn_W2_fq': 3.725,
     'L0_ffn_Ws1': 4.558,
     'L0_ffn_Ws2': 2.949}
    for name, (base, spread) in spreads.items():
        noise = np.random.default_rng([zlib.crc32(name.encode()), seed]).standard_normal(out[name].shape)
        drawn = base * np.exp(spread * noise) if base else spread * noise
        out[name] = jnp.asarray(drawn.astype(out[name].dtype))
    for name, factor in factors.items():
        out[name] = (out[name] * factor).astype(out[name].dtype)
    return out
```

```python
from contextlib import ExitStack

import concourse.bass as bass
from concourse import mybir

F32 = mybir.dt.float32
F16 = mybir.dt.float16
I32 = mybir.dt.int32
ALU = mybir.AluOpType
ACT = mybir.ActivationFunctionType
X = mybir.AxisListType.X

P = 128
N = 6250
D = 512
KC = D // P
TILES = -(-N // P)
ROWS = TILES * P
TAIL = N - (TILES - 1) * P
CHUNK = 7
CHUNKS = TILES // CHUNK
HEADS = 8
HD = D // HEADS
EDGES = 100000
WIN = 256
WINDOWS = -(-EDGES // WIN)
WROWS = WINDOWS + 1
WSLOTS = 4
WPARTS = WROWS // WSLOTS
PAD = WROWS * WIN - EDGES
NO_NODE = 1 << 20
NO_ROW = 1 << 16
PER = 9
PAIRS = TILES * PER
SETS = 4
PBANKS = 3
E = 8
BANKS = 2
EE = E * BANKS
TB = TILES * BANKS
FF = 256
FC = FF // P
CAP = -(-5 * 32 * 1024 // (4 * E))
SLOT_TILES = BANKS * (TILES + E - 1)
EXPERT_W = KC * FF + FC * D
EPS = 1e-5
NEVER = -1e30
UNROLL = 4
CREDIT_PAIR = 2
CREDIT_SEG = PER
CREDIT_BANK = PBANKS
CREDIT_F = CHUNK
CONSTS = 13
PLAN_TOUCH = 4
PLAN_KNOWN = 19
PLAN_STEPS = PLAN_KNOWN + SETS + 4
CTX_STEPS = 4
ROUTE_LESS = 2
ROUTE_HOT = 8
WMIX = 13

assert TILES == CHUNK * CHUNKS and WROWS == WSLOTS * WPARTS
assert WINDOWS + TILES - 1 <= PAIRS and PAIRS + PER <= SETS * P and PER % PBANKS == 0
assert SLOT_TILES <= P and SLOT_TILES % UNROLL == 0


class Steps:

    def __init__(self, engine, sem):
        self.engine, self.sem, self.count = engine, sem, 0

    def done(self, instruction):
        instruction.then_inc(self.sem, 1)
        self.count += 1

    def wait(self):
        self.engine.wait_ge(self.sem, self.count)

    def then(self, instruction):
        self.done(instruction)
        self.wait()


def wait_from(engine, sem, value):
    if not isinstance(value, int) or value > 0:
        engine.wait_ge(sem, value)


def gps_layer(nc, x, src, dst, w1, b1, w2, b2, w_qkv, w_proj, b_proj, wr_sp, br_sp, wr_fq, br_fq,
              ws1, bs1, ws2, bs2, w1_sp, b1_sp, w2_sp, b2_sp, w1_fq, b1_fq, w2_fq, b2_fq, out):
    with ExitStack() as ctx:
        def sb(name, shape, dt):
            return ctx.enter_context(nc.sbuf_tensor(name, shape, dt))

        def sem(name):
            return ctx.enter_context(nc.semaphore(name))

        xn_pair = nc.dram_tensor("xn_pair", (ROWS, 2 * D), F16).ap()
        qkv_rows = nc.dram_tensor("qkv_rows", (ROWS, 3 * D), F32).ap()
        base_rows = nc.dram_tensor("base_rows", (ROWS, D), F32).ap()
        src_win = nc.dram_tensor("src_win", (WROWS, WIN), I32).ap()
        dst_win = nc.dram_tensor("dst_win", (WROWS, WIN), I32).ap()
        slot_x = nc.dram_tensor("slot_x", (SLOT_TILES * P, D), F32).ap()
        slot_y = nc.dram_tensor("slot_y", (SLOT_TILES * P, D), F32).ap()

        AGG = TILES * D
        arena = sb("arena", [P, AGG + KC * 3 * D + KC * D], F32)
        work = sb("work", [P, 14848], F32)
        agg = arena[:, 0:AGG]

        def part(tensor, at, shape, dt=F32):
            n = 1
            for s in shape:
                n *= s
            words = n // 2 if dt == F16 else n
            assert at + words <= tensor.shape[1], (at, shape)
            ap = tensor[:, at:at + words]
            if dt != F32:
                ap = ap.bitcast(dt)
            if len(shape) == 2:
                ap = ap.rearrange("p (a b) -> p a b", a=shape[0])
            if len(shape) == 3:
                ap = ap.rearrange("p (a b c) -> p a b c", a=shape[0], b=shape[1])
            return ap

        def agg_tile(t):
            return agg[:, bass.ds(t * D, D)]

        wqkv_sb = part(arena, AGG, [KC, 3 * D])
        wproj_sb = part(arena, AGG + KC * 3 * D, [KC, D])
        mix_w = part(arena, AGG, [KC, D])
        w1_sb = part(arena, AGG + KC * D, [KC, D])
        w2_sb = part(arena, AGG + 2 * KC * D, [KC, D])

        ident = sb("ident", [P, P], F32)
        ones32 = sb("ones32", [P, P], F32)
        ones16 = sb("ones16", [P, P], F16)
        prefix16 = sb("prefix16", [P, P], F16)
        node16 = sb("node16", [P, P], F16)
        zero16 = sb("zero16", [P, D], F16)
        zero32 = sb("zero32", [P, D], F32)
        count = sb("count", [P, P], F32)
        pair_no = sb("pair_no", [P, SETS], F32)
        eps = sb("eps", [P, 1], F32)
        minus_half = sb("minus_half", [P, 1], F32)
        moments = sb("moments", [P, CHUNK, 2], F32)
        std = sb("std", [P, CHUNK], F32)
        rstd = sb("rstd", [P, CHUNK], F32)
        edge_node = sb("edge_node", [P, SETS * P, 2], F32)
        edge_src = sb("edge_src", [P, SETS * P, 2], I32)
        agg_at = sb("agg_at", [1, SETS * P], I32)
        src_now = sb("src_now", [P, 2 * PER], I32)
        head = sb("head", [P, 3, HEADS], F32)

        pairs_out = part(work, 0, [2 * CHUNK * 2 * D], F16)
        stats6 = part(work, 7168, [CHUNK, 6])
        pw = 7232
        ends = part(work, pw, [WSLOTS, WIN], I32)
        touch = part(work, pw + 1024, [2, WSLOTS, TILES])
        ab = part(work, pw + 1424, [2, TILES])
        pairs_of = part(work, pw + 1524, [TILES])
        pair_end = part(work, pw + 1574, [TILES])
        shift = part(work, pw + 1624, [TILES])
        cmp = part(work, pw + 1674, [SETS, TILES])
        node_no = part(work, pw + 1874, [SETS])
        win_no = part(work, pw + 1880, [SETS])
        win_idx = part(work, pw + 1886, [SETS], I32)
        agg_off = part(work, pw + 1892, [SETS])
        minus_first = part(work, pw + 1898, [SETS])
        pad_src = part(work, pw + 1904, [PAD], I32)
        pad_dst = part(work, pw + 2260, [PAD], I32)
        win_src = part(work, pw + 2624, [SETS, WIN], I32)
        win_dst = part(work, pw + 3648, [SETS, WIN], I32)
        local = part(work, pw + 4672, [SETS, WIN])
        off_tile = part(work, pw + 5696, [SETS, WIN])
        never = part(work, pw + 6720, [D])
        bounds = part(work, pw + 7232, [2, TILES])
        rows = part(work, 0, [2 * PER, 2 * D], F16)
        pick = part(work, 9216, [PER, 2, P], F16)
        pair_in = part(work, 10368, [2, D], F16)
        xn_tile = part(work, 10880, [D])
        xn_t = part(work, 11392, [KC, P])
        qkv_out = part(work, 11904, [3, D])
        k_max = part(work, 13440, [D])
        kv_in = [part(work, 1024 * k, [2, D]) for k in range(CHUNK)]
        k_top = part(work, 7168, [D])
        k_top_col = part(work, 7680, [KC])
        top_diag = part(work, 7688, [KC, P])
        ctx_t = part(work, 8200, [KC, P])
        k_sum = part(work, 8720, [KC])
        ws1_sb = part(work, 0, [KC, FF])
        ws2_sb = part(work, 1024, [FC, D])
        wr_sb = part(work, 2048, [KC, EE])
        b2_row = part(work, 2112, [D])
        bproj_row = part(work, 2624, [D])
        bs2_row = part(work, 3136, [D])
        br_row = part(work, 3648, [EE])
        b1_col = part(work, 3664, [KC])
        bs1_col = part(work, 3668, [FC])
        mx = 3680
        q_in = part(work, mx, [D])
        x_in = part(work, mx + 512, [D])
        x_b = part(work, mx + 1024, [D])
        h_t = part(work, mx + 1536, [KC, P])
        q_t = part(work, mx + 2048, [KC, P])
        h1_t = part(work, mx + 2560, [KC, P])
        gin = part(work, mx + 3072, [D])
        xa = part(work, mx + 3584, [D])
        x1 = part(work, mx + 4096, [D])
        xm_t = part(work, mx + 4608, [KC, P])
        x1_b = part(work, mx + 5120, [D])
        hs_t = part(work, mx + 5632, [FC, P])
        base_out = part(work, mx + 5888, [D])
        st6 = part(work, mx + 6400, [6])
        mv2 = part(work, mx + 6408, [2])
        rs2 = part(work, mx + 6412, [1])
        var2 = part(work, mx + 6414, [1])
        logits = part(work, 10112, [TILES * EE])
        h_now = part(work, 10896, [D])
        xm_now = part(work, 11408, [D])
        less = part(work, 0, [TB, E])
        expo = part(work, 784, [TB, E])
        key = part(work, 1568, [TB, E])
        hot = part(work, 2352, [TB, E])
        hot16 = part(work, 3136, [TILES * EE], F16)
        top = part(work, 3528, [TB])
        gate = part(work, 8564, [TB])
        before = part(work, 3724, [TILES * EE])
        tile_n = part(work, 4508, [TILES * EE])
        tile_inc = part(work, 5292, [TILES * EE])
        place = part(work, 6076, [TILES * EE])
        n_tiles = part(work, 6860, [EE])
        tile_end = part(work, 6876, [EE])
        tile_row = part(work, 6892, [EE])
        rank = part(work, 6908, [TB])
        slot_f = part(work, 7006, [TB])
        keep = part(work, 7104, [TB])
        expert_f = part(work, 7202, [SLOT_TILES])
        first_best = part(work, 7314, [E])
        tile_bound = part(work, 7322, [TILES])
        wide = part(work, 0, [SLOT_TILES, EE])
        slot_i = part(work, 8336, [TB], I32)
        weight_at = part(work, 8434, [P], I32)
        bias_at = part(work, 9456, [P], I32)
        gates = part(work, 8672, [TILES, EE])
        stage = [part(work, 512 * k, [D]) for k in range(CHUNK)]
        slot_now = part(work, 9584, [CHUNK * BANKS], I32)
        b1_all = part(work, 10240, [EE * FF])
        sx = [part(work, 512 * k, [D]) for k in range(UNROLL)]
        sx_t = [part(work, 2048 + 512 * k, [KC, P]) for k in range(2)]
        he = [part(work, 3072 + 256 * k, [FF]) for k in range(2)]
        he_t = [part(work, 3584 + 256 * k, [FC, P]) for k in range(2)]
        ye = [part(work, 4096 + 512 * k, [D]) for k in range(2)]
        y_in = [[part(arena, 1536 * k + 512 * b, [D]) for b in range(BANKS)] for k in range(CHUNK)]
        o_in = [part(arena, 1536 * k + 1024, [D]) for k in range(CHUNK)]
        fin = 1536 * CHUNK
        gates_t = [part(arena, fin + P * k, [P]) for k in range(CHUNK)]
        gates_now = [part(arena, fin + P * CHUNK + EE * k, [EE]) for k in range(CHUNK)]
        b2_all = part(arena, fin + (P + EE) * CHUNK, [D])

        bank = [ctx.enter_context(nc.psum_tensor(f"bank{k}", [P, D], F32)) for k in range(8)]

        consts = sem("consts")
        edges_copied = sem("edges_copied")
        pads_set, pads_written, ends_in = sem("pads_set"), sem("pads_written"), sem("ends_in")
        plan_own = sem("plan_own")
        touch_summed, at_summed = sem("touch_summed"), sem("at_summed")
        win_in, edge_turned, edge_ready = sem("win_in"), sem("edge_turned"), sem("edge_ready")
        tail_zeroed, x_landed, x_ready = sem("tail_zeroed"), sem("x_landed"), sem("x_ready")
        bn_own, std_done, rstd_done = sem("bn_own"), sem("std_done"), sem("rstd_done")
        xn_done, hi_done, lo_done = sem("xn_done"), sem("hi_done"), sem("lo_done")
        pair_stored, pair_free = sem("pair_stored"), sem("pair_free")
        wqkv_landed, zeros_stored, never_stored = sem("wqkv_landed"), sem("zeros_stored"), sem("never_stored")
        pair_landed, xn_ready = sem("pair_landed"), sem("xn_ready")
        xn_turned, xn_t_ready = sem("xn_turned"), sem("xn_t_ready")
        q_done, k_done, v_done = sem("q_done"), sem("k_done"), sem("v_done")
        q_less, k_less, q_exp, k_exp = sem("q_less"), sem("k_less"), sem("q_exp"), sem("k_exp")
        q_ready, k_ready, v_ready = sem("q_ready"), sem("k_ready"), sem("v_ready")
        qkv_stored, qkv_free = sem("qkv_stored"), sem("qkv_free")
        soft_own, k_max_done = sem("soft_own"), sem("k_max_done")
        src_copied, pick_ready = sem("src_copied"), sem("pick_ready")
        seg_done, seg_added = sem("seg_done"), sem("seg_added")
        row_in = [sem(f"row_in{k}") for k in range(2 * PER)]
        k_max_turned, top_own, top_spread, k_top_ready = (
            sem("k_max_turned"), sem("top_own"), sem("top_spread"), sem("k_top_ready"))
        kv_landed = [sem(f"kv_landed{k}") for k in range(CHUNK)]
        k_shifted, k_expd, kv_used = sem("k_shifted"), sem("k_expd"), sem("kv_used")
        ctx_own, mixw_done, mixw_ready = sem("ctx_own"), sem("mixw_done"), sem("mixw_ready")
        wmix_landed, q_landed, xr_landed = sem("wmix_landed"), sem("q_landed"), sem("xr_landed")
        h_ready, turned, h_t_ready, q_t_ready = sem("h_ready"), sem("turned"), sem("h_t_ready"), sem("q_t_ready")
        up_done, up_act, att_done, gin_done = sem("up_done"), sem("up_act"), sem("att_done"), sem("gin_done")
        xb_ready, gin_read, xa_done, x1_ready = sem("xb_ready"), sem("gin_read"), sem("xa_done"), sem("x1_ready")
        ln_own, var_ready, rs_ready, xm_ready = sem("ln_own"), sem("var_ready"), sem("rs_ready"), sem("xm_ready")
        x1_b_ready, xm_kept = sem("x1_b_ready"), sem("xm_kept")
        xm_turned, xm_t_ready, sh_up, sh_act = sem("xm_turned"), sem("xm_t_ready"), sem("sh_up"), sem("sh_act")
        lg_ready, sh_down, base_ready, base_stored = sem("lg_ready"), sem("sh_down"), sem("base_ready"), sem("base_stored")
        route_own, expo_done, hot_summed, counts_read = (
            sem("route_own"), sem("expo_done"), sem("hot_summed"), sem("counts_read"))
        routed, staged = sem("routed"), sem("staged")
        we_landed, b1_landed = sem("we_landed"), sem("b1_landed")
        sx_landed = [sem(f"sx_landed{k}") for k in range(UNROLL)]
        sx_turned, sx_t_ready, e_up, e_biased = sem("sx_turned"), sem("sx_t_ready"), sem("e_up"), sem("e_biased")
        e_act, e_turned, he_t_ready, e_down, e_out = (
            sem("e_act"), sem("e_turned"), sem("he_t_ready"), sem("e_down"), sem("e_out"))
        b2_landed, y_idx_ready, gates_ready = sem("b2_landed"), sem("y_idx_ready"), sem("gates_ready")
        g_turned, g_t_ready, g_done, f_own, f_ready = (
            sem("g_turned"), sem("g_t_ready"), sem("g_done"), sem("f_own"), sem("f_ready"))
        out_stored = [sem(f"out_stored{k}") for k in range(CHUNK)]
        pool_mark, act_mark, dve_mark, sp_mark = sem("pool_mark"), sem("act_mark"), sem("dve_mark"), sem("sp_mark")
        ye_stored = [base_stored, qkv_stored]
        YE_FROM = 16 * TILES
        SCATTER_FROM = 16 * TILES
        scattered = row_in[0:CHUNK]
        SCATTERED = SCATTER_FROM + 16 * CHUNKS * BANKS
        y_landed = [row_in[CHUNK:2 * CHUNK], scattered]
        Y_FROM = [16 * TILES, SCATTERED]
        o_landed = kv_landed
        O_FROM = 16 * CHUNKS

        block = ctx.enter_context(nc.Block())

        def rows_of(t, n=1):
            return bass.ds(t * P, n * P)

        def weight_tiles(w):
            return w.rearrange("(c p) n -> p c n", p=P)

        def spread(ap, n):
            return ap.unsqueeze(2).broadcast_to([ap.shape[0], ap.shape[1], n])

        def repeat(ap, n):
            return ap.unsqueeze(1).broadcast_to([ap.shape[0], n, ap.shape[1]])

        @block.sync
        def _(sp):
            def hold(sem, value):
                if not isinstance(value, int) or value > 0:
                    sp.wait_ge(sem, value)
                    sp.sem_inc(sp_mark, 1)

            agg_tiles = agg.rearrange("p (t d) -> p t d", t=TILES)
            with sp.Fori(0, CHUNKS - 1) as c:
                sp.dma_start(agg_tiles[:, bass.ds(c * CHUNK, CHUNK), :],
                             x[rows_of(c * CHUNK, CHUNK), :].rearrange("(t p) d -> p t d", p=P)
                             ).then_inc(x_landed, 16)
                hold(x_landed, c * 16 + 16)
                sp.sem_inc(x_ready, 1)
            full = TILES - CHUNK
            sp.dma_start(agg_tiles[:, full:TILES - 1, :],
                         x[full * P:(TILES - 1) * P, :].rearrange("(t p) d -> p t d", p=P)
                         ).then_inc(x_landed, 16)
            sp.wait_ge(tail_zeroed, 1)
            sp.dma_start(agg_tiles[0:TAIL, TILES - 1, :], x[(TILES - 1) * P:N, :]).then_inc(x_landed, 16)
            sp.wait_ge(x_landed, 16 * (CHUNKS + 1))
            sp.sem_inc(x_ready, 1)
            sp.dma_start(wqkv_sb, weight_tiles(w_qkv)).then_inc(wqkv_landed, 16)
            sp.dma_start(wproj_sb, weight_tiles(w_proj)).then_inc(wqkv_landed, 16)
            with sp.Fori(0, CHUNKS) as c:
                hold(lo_done, c + 1)
                sp.dma_start(xn_pair[rows_of(c * CHUNK, CHUNK), :].rearrange("(t p) d -> p t d", p=P),
                             pairs_out[:, bass.ds((c % 2) * (CHUNK * 2 * D), CHUNK * 2 * D)]
                             .rearrange("p (t d) -> p t d", t=CHUNK)).then_inc(pair_stored, 16)
                hold(pair_stored, c * 16 + 16)
                sp.sem_inc(pair_free, 1)
            sp.dma_start(slot_x[2 * TILES * P:, :].rearrange("(t p) d -> p t d", p=P),
                         repeat(zero32[:, :], SLOT_TILES - 2 * TILES)).then_inc(zeros_stored, 16)
            sp.wait_ge(seg_done, CREDIT_SEG)
            sp.dma_start(pair_in, xn_pair[0:P, :].rearrange("p (h d) -> p h d", h=2)).then_inc(pair_landed, 16)
            with sp.Fori(0, TILES) as i:
                hold(xn_ready, i + 1)
                sp.dma_start(pair_in, xn_pair[rows_of((i + 1) % TILES), :].rearrange("p (h d) -> p h d", h=2)
                             ).then_inc(pair_landed, 16)
                sp.dma_start(slot_x[rows_of(i * 2, 2), :].rearrange("(t p) d -> p t d", p=P),
                             repeat(zero32[:, :], 2)).then_inc(zeros_stored, 16)
                hold(q_ready, i + 1)
                hold(k_ready, i + 2)
                hold(v_ready, i + 2)
                sp.dma_start(qkv_rows[rows_of(i), :], qkv_out.rearrange("p a d -> p (a d)")
                             ).then_inc(qkv_stored, 16)
                hold(qkv_stored, i * 16 + 16)
                sp.sem_inc(qkv_free, 1)
            sp.dma_start(qkv_rows[N:ROWS, D:2 * D], never[0:ROWS - N, :]).then_inc(never_stored, 16)
            sp.wait_ge(never_stored, 16)
            sp.wait_ge(seg_done, CREDIT_SEG + PAIRS)

            def kv_load(t, k):
                sp.dma_start(kv_in[k], qkv_rows[rows_of(t), D:3 * D].rearrange("p (a d) -> p a d", a=2)
                             ).then_inc(kv_landed[k], 16)

            for k in range(CHUNK):
                kv_load(k, k)
            with sp.Fori(1, CHUNKS) as c:
                for k in range(CHUNK):
                    hold(kv_used, c * CHUNK + (k + 1 - CHUNK))
                    kv_load(c * CHUNK + k, k)
            sp.wait_ge(kv_used, TILES)

            def col(v, c):
                return v.rearrange("(c p) -> p c", c=c)

            def row(v):
                return v.unsqueeze(0).broadcast_to([P, v.shape[0]])

            with nc.allow_non_contiguous_dma(reason="bias columns, a few hundred words"):
                loads = [(w1_sb, weight_tiles(w1)), (w2_sb, weight_tiles(w2)), (ws1_sb, weight_tiles(ws1)),
                         (ws2_sb, weight_tiles(ws2)), (wr_sb[:, :, 0:E], weight_tiles(wr_sp)),
                         (wr_sb[:, :, E:EE], weight_tiles(wr_fq)), (b2_row, row(b2)), (bproj_row, row(b_proj)),
                         (bs2_row, row(bs2)), (br_row[:, 0:E], row(br_sp)), (br_row[:, E:EE], row(br_fq)),
                         (b1_col, col(b1, KC)), (bs1_col, col(bs1, FC))]
                assert len(loads) == WMIX
                for to, of in loads:
                    sp.dma_start(to, of).then_inc(wmix_landed, 16)

            def mix_load(t, last=False):
                hold(turned, t)
                sp.dma_start(q_in, qkv_rows[rows_of(t), 0:D]).then_inc(q_landed, 16)
                hold(xb_ready, t)
                if last:
                    sp.dma_start(x_in[0:TAIL, :], x[(TILES - 1) * P:N, :]).then_inc(xr_landed, 16)
                else:
                    sp.dma_start(x_in, x[rows_of(t), :]).then_inc(xr_landed, 16)

            def mix_store(t):
                hold(base_ready, t + 2)
                sp.dma_start(base_rows[rows_of(t), :], base_out).then_inc(base_stored, 16)

            mix_load(0)
            mix_load(1)
            with sp.Fori(2, TILES - 1) as t:
                mix_load(t)
                mix_store(t - 2)
            mix_load(TILES - 1, last=True)
            for t in range(TILES - 3, TILES):
                mix_store(t)
            sp.wait_ge(routed, 1)
            for b, v in enumerate((b1_sp, b1_fq)):
                sp.dma_start(b1_all[:, b * E * FF:(b + 1) * E * FF], row(v.rearrange("e f -> (e f)"))
                             ).then_inc(b1_landed, 16)
            sp.wait_ge(staged, TB)
            for b, (wa, wb) in enumerate(((w1_sp, w2_sp), (w1_fq, w2_fq))):
                for e in range(E):
                    at = (b * E + e) * EXPERT_W
                    sp.dma_start(part(arena, at, [KC, FF]), weight_tiles(wa[e])).then_inc(we_landed, 16)
                    sp.dma_start(part(arena, at + KC * FF, [FC, D]), weight_tiles(wb[e])).then_inc(we_landed, 16)
            for k in range(CHUNK):
                sp.wait_ge(scattered[k], SCATTERED)

            def slot_load(j, k):
                sp.dma_start(sx[k], slot_x[rows_of(j), :]).then_inc(sx_landed[k], 16)

            def slot_store(j, k):
                hold(e_out, j + 1)
                sp.dma_start(slot_y[rows_of(j), :], ye[k % 2]).then_inc(ye_stored[k % 2], 16)

            for k in range(UNROLL):
                slot_load(k, k)
            with sp.Fori(0, SLOT_TILES // UNROLL - 1) as g:
                for k in range(UNROLL):
                    j = g * UNROLL + k
                    hold(sx_turned, j + 1)
                    slot_load(j + UNROLL, k)
                    slot_store(j, k)
            for k in range(UNROLL):
                slot_store(SLOT_TILES - UNROLL + k, k)
            sp.wait_ge(e_down, SLOT_TILES)
            for b, v in enumerate((b2_sp, b2_fq)):
                sp.dma_start(b2_all[b * E:(b + 1) * E, :], v).then_inc(b2_landed, 16)

            def o_load(t, k):
                sp.dma_start(o_in[k], base_rows[rows_of(t), :]).then_inc(o_landed[k], 16)

            def o_store(t, k, last=False):
                hold(f_ready, t + (1 + CREDIT_F))
                if last:
                    sp.dma_start(out[(TILES - 1) * P:N, :], o_in[k][0:TAIL, :]).then_inc(out_stored[k], 16)
                else:
                    sp.dma_start(out[rows_of(t), :], o_in[k]).then_inc(out_stored[k], 16)

            LATE = 3
            for k in range(CHUNK):
                o_load(k, k)
            for k in range(CHUNK):
                o_store(k, k)
                if k >= LATE:
                    sp.wait_ge(out_stored[k - LATE], 16)
                    o_load(CHUNK + k - LATE, k - LATE)
            with sp.Fori(1, CHUNKS - 1) as c:
                for k in range(CHUNK):
                    t = c * CHUNK + k
                    o_store(t, k)
                    kk = (k - LATE) % CHUNK
                    hold(out_stored[kk], c * 16 + (16 if k >= LATE else 0))
                    o_load(t + (CHUNK - LATE), kk)
            for k in range(CHUNK):
                t = TILES - CHUNK + k
                o_store(t, k, last=k == CHUNK - 1)
                if k < LATE:
                    kk = k - LATE + CHUNK
                    sp.wait_ge(out_stored[kk], 16 * (CHUNKS - 1))
                    o_load(t + CHUNK - LATE, kk)
            for k in range(CHUNK):
                sp.wait_ge(out_stored[k], 16 * CHUNKS)
            sp.wait_ge(zeros_stored, 16 * (TILES + 1))

        @block.gpsimd
        def _(pool):
            made = Steps(pool, consts)
            made.done(pool.memset(ident[:, :], 0.0))
            made.done(pool.memset(ones16[:, :], 1.0))
            made.wait()
            made.done(pool.affine_select(out=ident[:, :], in_=ident[:, :], compare_op=ALU.not_equal, fill=1.0,
                                         base=0, pattern=[[-1, P]], channel_multiplier=1))
            made.done(pool.affine_select(out=prefix16[:, :], in_=ones16[:, :], compare_op=ALU.is_ge, fill=0.0,
                                         base=0, pattern=[[1, P]], channel_multiplier=-1))
            made.done(pool.memset(ones32[:, :], 1.0))
            made.done(pool.iota(count[:, :], [[1, P]], base=0, channel_multiplier=0,
                                allow_small_or_imprecise_dtypes=True))
            made.done(pool.iota(pair_no[:, :], [[P, SETS]], base=0, channel_multiplier=1,
                                allow_small_or_imprecise_dtypes=True))
            made.done(pool.iota(node16[:, :], [[1, P]], base=0, channel_multiplier=0,
                                allow_small_or_imprecise_dtypes=True))
            made.done(pool.memset(eps[:, :], EPS))
            made.done(pool.memset(minus_half[:, :], -0.5))
            made.done(pool.memset(zero16[:, :], 0.0))
            made.done(pool.memset(zero32[:, :], 0.0))
            made.done(pool.memset(never, NEVER))
            assert made.count == CONSTS
            last_node = pool.to_reg(N - 1)
            last_window = pool.to_reg(WROWS - 1)
            last_slot = pool.to_reg(SLOT_TILES * P - 1)

            pool.wait_ge(ends_in, 16)
            pool.wait_ge(plan_own, PLAN_KNOWN)
            for j in range(SETS):
                for to, of in ((win_src, src_win), (win_dst, dst_win)):
                    pool.indirect_dma_start(out=to[:, j, :], out_offset=None, in_=of[:, :],
                                            in_offset=bass.IndirectOffsetOnAxis(ap=win_idx[:, j:j + 1], axis=0),
                                            bounds_check=last_window, oob_is_err=False).then_inc(win_in, 16)
            with pool.Fori(0, CHUNKS) as c:
                pool.wait_ge(hi_done, c + 1)
                pool.sem_inc(pool_mark, 1)
                pair = pairs_out[:, bass.ds((c % 2) * (CHUNK * 2 * D), CHUNK * 2 * D)] \
                    .rearrange("p (t h d) -> p t h d", t=CHUNK, h=2)
                pool.tensor_tensor(pair[:, :, 1, :],
                                   agg[:, bass.ds(c * (CHUNK * D), CHUNK * D)].rearrange("p (t d) -> p t d", t=CHUNK),
                                   pair[:, :, 0, :], ALU.subtract).then_inc(lo_done, 1)
            pool.wait_ge(edge_ready, 4)
            pool.wait_ge(pair_stored, 16 * CHUNKS)
            with pool.Fori(0, TILES) as i:
                for third in range(PER // PBANKS):
                    g0 = third * PBANKS
                    pool.wait_ge(seg_done, i * PER + (g0 + PBANKS))
                    pool.sem_inc(pool_mark, 1)
                    pool.tensor_copy(src_now[:, 2 * g0:2 * (g0 + PBANKS)],
                                     edge_src[:, bass.ds(i * PER + g0, PBANKS), :].rearrange("p g h -> p (g h)")
                                     ).then_inc(src_copied, 1)
                    pool.wait_ge(src_copied, i * (PER // PBANKS) + (third + 1))
                    pool.sem_inc(pool_mark, 1)
                    for s in range(2 * g0, 2 * (g0 + PBANKS)):
                        pool.indirect_dma_start(out=rows[:, s, :], out_offset=None, in_=xn_pair[:, :],
                                                in_offset=bass.IndirectOffsetOnAxis(ap=src_now[:, s:s + 1], axis=0),
                                                bounds_check=last_node, oob_is_err=False).then_inc(row_in[s], 16)

            pool.wait_ge(wmix_landed, 16 * WMIX)
            with pool.Fori(0, TILES) as t:
                pool.wait_ge(xr_landed, t * 16 + 16)
                pool.wait_ge(x1_ready, t + 1)
                pool.sem_inc(pool_mark, 1)
                pool.tensor_tensor(x_b, x_in, bproj_row, ALU.add).then_inc(xb_ready, 1)
                pool.wait_ge(var_ready, t + 1)
                pool.sem_inc(pool_mark, 1)
                pool.tensor_tensor(rs2, var2, minus_half[:, :], ALU.pow).then_inc(rs_ready, 1)
                pool.wait_ge(base_ready, t + 1)
                pool.sem_inc(pool_mark, 1)
                pool.tensor_tensor(x1_b, x1, bs2_row, ALU.add).then_inc(x1_b_ready, 1)
                pool.wait_ge(xm_ready, t + 1)
                pool.sem_inc(pool_mark, 1)
                pool.tensor_copy(agg_tile(t), xm_now).then_inc(xm_kept, 1)

            pool.wait_ge(zeros_stored, 16 * (TILES + 1))
            for b in range(BANKS):
                with pool.Fori(0, CHUNKS) as c:
                    for k in range(CHUNK):
                        pool.wait_ge(staged, c * CHUNK + (b * TILES + k + 1))
                        pool.sem_inc(pool_mark, 1)
                        pool.indirect_dma_start(
                            out=slot_x[:, :], out_offset=bass.IndirectOffsetOnAxis(ap=slot_now[:, k:k + 1], axis=0),
                            in_=stage[k], in_offset=None, bounds_check=last_slot, oob_is_err=False
                        ).then_inc(scattered[k], 16)

            for s in ye_stored:
                pool.wait_ge(s, YE_FROM + 16 * SLOT_TILES // 2)
            with pool.Fori(0, CHUNKS) as c:
                for k in range(CHUNK):
                    pool.wait_ge(y_idx_ready, c * CHUNK + (k + 1))
                    pool.wait_ge(f_ready, c * CHUNK + (k + 1))
                    pool.sem_inc(pool_mark, 1)
                    for b in range(BANKS):
                        pool.indirect_dma_start(
                            out=y_in[k][b], out_offset=None, in_=slot_y[:, :],
                            in_offset=bass.IndirectOffsetOnAxis(ap=slot_now[:, 2 * k + b:2 * k + b + 1], axis=0),
                            bounds_check=last_slot, oob_is_err=False).then_inc(y_landed[b][k], 16)

        @block.scalar
        def _(act):
            def copy(to, of, **kw):
                return act.activation(to, of, ACT.Copy, **kw)

            def flat(w):
                return w.rearrange("a b -> (a b)")

            def sixteen(v):
                return v.rearrange("(a b) -> a b", a=16)

            act.dma_start(sixteen(flat(dst_win)[0:EDGES]), sixteen(dst)).then_inc(edges_copied, 16)
            act.dma_start(sixteen(flat(src_win)[0:EDGES]), sixteen(src)).then_inc(edges_copied, 16)
            act.wait_ge(pads_set, 2)
            act.dma_start(flat(src_win)[EDGES:].unsqueeze(0), pad_src[0:1, :]).then_inc(pads_written, 16)
            act.dma_start(flat(dst_win)[EDGES:].unsqueeze(0), pad_dst[0:1, :]).then_inc(pads_written, 16)
            act.wait_ge(edges_copied, 32)
            act.wait_ge(pads_written, 32)
            act.dma_start(ends[0:WPARTS, :, :], dst_win.rearrange("(p c) e -> p c e", c=WSLOTS)).then_inc(ends_in, 16)

            act.wait_ge(consts, CONSTS)
            with act.Fori(0, CHUNKS) as c:
                act.wait_ge(bn_own, c * (2 * CHUNK) + 2 * CHUNK)
                act.activation(std[:, :], moments[:, :, 1], ACT.Sqrt, bias=eps[:, 0:1]).then_inc(std_done, 1)
                act.wait_ge(xn_done, c * CHUNK + CHUNK)
                act.wait_ge(pair_free, c + 1)
                act.sem_inc(act_mark, 1)
                pair = pairs_out[:, bass.ds((c % 2) * (CHUNK * 2 * D), CHUNK * 2 * D)] \
                    .rearrange("p (t h d) -> p t h d", t=CHUNK, h=2)
                copy(pair[:, :, 0, :], agg[:, bass.ds(c * (CHUNK * D), CHUNK * D)]
                     .rearrange("p (t d) -> p t d", t=CHUNK)).then_inc(hi_done, 1)

            act.wait_ge(edge_turned, 4)
            for h in range(2):
                copy(edge_src[:, :, h], bank[4 + h][:, :]).then_inc(edge_ready, 1)

            with act.Fori(0, TILES) as i:
                act.wait_ge(xn_turned, i + 1)
                copy(xn_t.rearrange("p a b -> p (a b)"), bank[0][:, :]).then_inc(xn_t_ready, 1)
                act.wait_ge(q_less, i + 2)
                act.activation(qkv_out[:, 0, :], qkv_out[:, 0, :], ACT.Exp).then_inc(q_exp, 1)
                act.wait_ge(k_less, i + 1)
                act.activation(qkv_out[:, 1, :], qkv_out[:, 1, :], ACT.Exp).then_inc(k_exp, 1)
                act.wait_ge(v_done, i + 1)
                act.wait_ge(qkv_free, i + 1)
                copy(qkv_out[:, 2, :], bank[3][:, :]).then_inc(v_ready, 1)

            with act.Fori(0, CHUNKS) as c:
                for k in range(CHUNK):
                    act.wait_ge(k_shifted, c * CHUNK + (k + 1))
                    act.activation(kv_in[k][:, 0, :], kv_in[k][:, 0, :], ACT.Exp).then_inc(k_expd, 1)
            act.wait_ge(ctx_own, CTX_STEPS)
            act.wait_ge(mixw_done, KC)
            for hp in range(KC):
                copy(mix_w[:, hp, :], bank[4 + hp][:, :], scale=k_sum[:, hp:hp + 1]).then_inc(mixw_ready, 1)

            act.wait_ge(wmix_landed, 16 * WMIX)

            def hidden(t):
                wait_from(act, turned, t)
                act.sem_inc(act_mark, 1)
                copy(h_now, agg_tile(t)).then_inc(h_ready, 1)
                act.wait_ge(turned, t + 1)
                wait_from(act, up_done, t)
                copy(h_t.rearrange("p a b -> p (a b)"), bank[0][:, :]).then_inc(h_t_ready, 1)
                wait_from(act, att_done, t)
                copy(q_t.rearrange("p a b -> p (a b)"), bank[1][:, :]).then_inc(q_t_ready, 1)

            def relu(t):
                act.wait_ge(up_done, t + 1)
                wait_from(act, gin_done, t)
                for m in range(KC):
                    act.activation(h1_t[:, m, :], bank[2][:, m * P:(m + 1) * P], ACT.Relu,
                                   bias=b1_col[:, m:m + 1]).then_inc(up_act, 1)

            def turn_xm(t):
                act.wait_ge(xm_turned, t + 1)
                wait_from(act, sh_up, t)
                copy(xm_t.rearrange("p a b -> p (a b)"), bank[5][:, :]).then_inc(xm_t_ready, 1)

            def shared_gelu(t):
                act.wait_ge(lg_ready, t + 1)
                wait_from(act, sh_down, t)
                for m in range(FC):
                    act.activation(hs_t[:, m, :], bank[6][:, m * P:(m + 1) * P], ACT.Gelu,
                                   bias=bs1_col[:, m:m + 1]).then_inc(sh_act, 1)

            hidden(0)
            relu(0)

            def mixed(t):
                hidden(t)
                relu(t)
                turn_xm(t - 1)
                shared_gelu(t - 1)

            mixed(1)
            with act.Fori(2, TILES) as t:
                mixed(t)
            turn_xm(TILES - 1)
            shared_gelu(TILES - 1)

            act.wait_ge(route_own, ROUTE_LESS)
            act.activation(expo, less, ACT.Exp).then_inc(expo_done, 1)
            act.wait_ge(routed, 1)
            act.wait_ge(xm_kept, TILES)

            for b in range(BANKS):
                with act.Fori(0, CHUNKS) as c:
                    for k in range(CHUNK):
                        act.wait_ge(scattered[k], c * 16 + (SCATTER_FROM + 16 * CHUNKS * b))
                        act.sem_inc(act_mark, 1)
                        copy(stage[k], agg_tile(c * CHUNK + k))
                        copy(slot_now[:, k:k + 1], slot_i[:, bass.ds(c * (CHUNK * BANKS) + (k * BANKS + b), 1)]
                             ).then_inc(staged, 1)

            def turn_slot(j, k):
                act.wait_ge(sx_turned, j + 1)
                copy(sx_t[k % 2].rearrange("p a b -> p (a b)"), bank[k % 2][:, :]).then_inc(sx_t_ready, 1)

            def expert_gelu(j, k):
                act.wait_ge(e_biased, j + 1)
                act.activation(he[k % 2], he[k % 2], ACT.Gelu).then_inc(e_act, 1)

            turn_slot(0, 0)
            expert_gelu(0, 0)
            with act.Fori(0, SLOT_TILES // UNROLL - 1) as g:
                for k in range(UNROLL):
                    turn_slot(g * UNROLL + (k + 1), k + 1)
                    expert_gelu(g * UNROLL + (k + 1), k + 1)
            for k in range(UNROLL - 1):
                turn_slot(SLOT_TILES - UNROLL + k + 1, k + 1)
                expert_gelu(SLOT_TILES - UNROLL + k + 1, k + 1)

            act.wait_ge(e_down, SLOT_TILES)
            for k in range(CHUNK):
                act.wait_ge(scattered[k], SCATTERED)
            with act.Fori(0, CHUNKS) as c:
                for k in range(CHUNK):
                    for b in range(BANKS):
                        act.wait_ge(y_landed[b][k], c * 16 + Y_FROM[b])
                    act.sem_inc(act_mark, 1)
                    copy(slot_now[:, 2 * k:2 * k + 2],
                         slot_i[:, bass.ds(c * (CHUNK * BANKS) + k * BANKS, BANKS)]).then_inc(y_idx_ready, 1)
                    copy(gates_now[k], gates.rearrange("p t e -> p (t e)")[:, bass.ds(c * (CHUNK * EE) + k * EE, EE)]
                         ).then_inc(gates_ready, 1)
                    act.wait_ge(g_turned, c * CHUNK + (k + 1))
                    copy(gates_t[k][0:EE, :], bank[0][0:EE, 0:P]).then_inc(g_t_ready, 1)

        @block.tensor
        def _(pe):
            def turn(to, tile, n=KC):
                for c in range(n):
                    last = pe.transpose(to[:, c * P:(c + 1) * P], tile[:, c * P:(c + 1) * P], ident[:, :])
                return last

            def product(to, stationary, moving):
                for c, (s, m) in enumerate(zip(stationary, moving)):
                    last = pe.matmul(to, s, m, start=c == 0, stop=c == len(stationary) - 1)
                return last

            pe.wait_ge(consts, CONSTS)
            pe.wait_ge(plan_own, PLAN_TOUCH)
            pe.matmul(bank[0][:, 0:2 * WSLOTS * TILES], ones32[0:WPARTS, :],
                      touch[0:WPARTS].rearrange("p a w n -> p (a w n)"), start=True, stop=True).then_inc(touch_summed, 1)
            pe.wait_ge(plan_own, PLAN_KNOWN)
            for j in range(SETS):
                last = pe.matmul(bank[1][0:1, j * P:(j + 1) * P], agg_off[:, j:j + 1], ident[:, :],
                                 start=True, stop=True)
            last.then_inc(at_summed, 1)
            pe.wait_ge(plan_own, PLAN_STEPS)
            for n, of in enumerate((local, off_tile)):
                for h in range(2):
                    for j in range(SETS):
                        last = pe.transpose(bank[2 + 2 * n + h][:, j * P:(j + 1) * P],
                                            of[:, j, h * P:(h + 1) * P], ident[:, :])
                    last.then_inc(edge_turned, 1)

            pe.wait_ge(wqkv_landed, 32)
            pe.wait_ge(edge_ready, 4)
            with pe.Fori(0, TILES) as i:
                def segment(u):
                    for h in range(2):
                        pe.wait_ge(row_in[2 * u + h], i * 16 + 16)
                    pe.wait_ge(pick_ready, i * PER + (u + 1))
                    pe.wait_ge(seg_added, i * PER + (u + 1))
                    to = bank[4 + u % PBANKS][:, :]
                    for h in range(2):
                        for half in range(2):
                            last = pe.matmul(to, pick[:, u, h, :], rows[:, 2 * u + h, half * D:(half + 1) * D],
                                             start=h + half == 0, stop=h + half == 2)
                    last.then_inc(seg_done, 1)

                pe.wait_ge(xn_ready, i + 1)
                turn(bank[0], xn_tile).then_inc(xn_turned, 1)
                for u in range(4):
                    segment(u)
                pe.wait_ge(xn_t_ready, i + 1)
                for n, (free, done) in enumerate(((q_less, q_done), (k_ready, k_done), (v_ready, v_done))):
                    pe.wait_ge(free, i + 1)
                    product(bank[1 + n][:, :], [xn_t[:, c, :] for c in range(KC)],
                            [wqkv_sb[:, c, n * D:(n + 1) * D] for c in range(KC)]).then_inc(done, 1)
                for u in range(4, PER):
                    segment(u)

            pe.wait_ge(k_max_done, TILES + 1)
            turn(bank[0], k_max).then_inc(k_max_turned, 1)
            pe.wait_ge(top_own, 1 + KC)
            for c in range(KC):
                last = pe.matmul(bank[1][:, c * P:(c + 1) * P], ones32[:, :], top_diag[:, c, :], start=True, stop=True)
            last.then_inc(top_spread, 1)
            pe.wait_ge(v_ready, TILES + 1)
            for b in (2, 3):
                pe.matmul(bank[b][:, :], zero16[:, 0:P], zero16[:, :], start=True, stop=True)
            with pe.Fori(0, CHUNKS) as c:
                for k in range(CHUNK):
                    pe.wait_ge(k_expd, c * CHUNK + (k + 1))
                    for hp in range(KC):
                        cols = slice(hp * P, (hp + 1) * P)
                        ek, v = kv_in[k][:, 0, cols], kv_in[k][:, 1, cols]
                        pe.matmul(bank[2][:, cols], v, ek, start=False, stop=True, skip_group_check=True)
                        last = pe.matmul(bank[3][:, hp:hp + 1], ek, ones32[:, 0:1], start=False, stop=True,
                                         skip_group_check=True)
                    last.then_inc(kv_used, 1)
            pe.wait_ge(ctx_own, CTX_STEPS)
            pe.wait_ge(seg_added, CREDIT_BANK + PAIRS)
            for hp in range(KC):
                pe.matmul(bank[4 + hp][:, :], ctx_t[:, hp, :], wproj_sb[:, hp, :],
                          start=True, stop=True).then_inc(mixw_done, 1)

            pe.wait_ge(wmix_landed, 16 * WMIX)
            pe.wait_ge(mixw_ready, KC)

            def turn_in(t):
                pe.wait_ge(h_ready, t + 1)
                pe.wait_ge(q_landed, t * 16 + 16)
                turn(bank[0], h_now)
                turn(bank[1], q_in).then_inc(turned, 1)

            def gin_up(t):
                pe.wait_ge(h_t_ready, t + 1)
                for m in range(KC):
                    last = product(bank[2][:, m * P:(m + 1) * P], [w1_sb[:, c, m * P:(m + 1) * P] for c in range(KC)],
                                   [h_t[:, c, :] for c in range(KC)])
                last.then_inc(up_done, 1)

            def attention(t):
                pe.wait_ge(q_t_ready, t + 1)
                wait_from(pe, xa_done, t)
                product(bank[3][:, :], [q_t[:, c, :] for c in range(KC)],
                        [mix_w[:, c, :] for c in range(KC)]).then_inc(att_done, 1)

            def gin_down(t):
                pe.wait_ge(up_act, t * KC + KC)
                wait_from(pe, gin_read, t)
                product(bank[4][:, :], [h1_t[:, c, :] for c in range(KC)],
                        [w2_sb[:, c, :] for c in range(KC)]).then_inc(gin_done, 1)

            def turn_xm(t):
                pe.wait_ge(xm_ready, t + 1)
                turn(bank[5], xm_now).then_inc(xm_turned, 1)

            def shared_up(t):
                pe.wait_ge(xm_t_ready, t + 1)
                wait_from(pe, lg_ready, t)
                for m in range(FC):
                    product(bank[6][:, m * P:(m + 1) * P], [ws1_sb[:, c, m * P:(m + 1) * P] for c in range(KC)],
                            [xm_t[:, c, :] for c in range(KC)])
                product(bank[6][:, FF:FF + EE], [xm_t[:, c, :] for c in range(KC)],
                        [wr_sb[:, c, :] for c in range(KC)]).then_inc(sh_up, 1)

            def shared_down(t):
                pe.wait_ge(sh_act, t * FC + FC)
                pe.wait_ge(base_ready, t + 1)
                product(bank[7][:, :], [hs_t[:, m, :] for m in range(FC)],
                        [ws2_sb[:, m, :] for m in range(FC)]).then_inc(sh_down, 1)

            turn_in(0)
            gin_up(0)
            attention(0)
            gin_down(0)

            def mixed(t):
                turn_in(t)
                gin_up(t)
                turn_xm(t - 1)
                attention(t)
                shared_up(t - 1)
                gin_down(t)
                shared_down(t - 1)

            mixed(1)
            with pe.Fori(2, TILES) as t:
                mixed(t)
            turn_xm(TILES - 1)
            shared_up(TILES - 1)
            shared_down(TILES - 1)

            pe.wait_ge(route_own, ROUTE_HOT)
            half = TILES * EE // 2
            for n, by in enumerate((prefix16, ones16)):
                for h in range(2):
                    pe.matmul(bank[2 * n + h][:, 0:half], by[:, :], hot16[:, h * half:(h + 1) * half],
                              start=True, stop=True).then_inc(hot_summed, 1)

            pe.wait_ge(counts_read, 2)
            pe.wait_ge(we_landed, 16 * 2 * EE)
            pe.wait_ge(routed, 1)

            def turn_slot(j, k, g):
                pe.wait_ge(sx_landed[k % UNROLL], g * 16 + 16)
                turn(bank[k % 2], sx[k % UNROLL]).then_inc(sx_turned, 1)

            def weights(j):
                return pe.value_load(weight_at[0:1, bass.ds(j, 1)], min_val=0, max_val=(EE - 1) * EXPERT_W)

            def expert_up(j, k):
                at = weights(j)
                pe.wait_ge(sx_t_ready, j + 1)
                product(bank[2 + k % 2][:, 0:FF], [sx_t[k % 2][:, c, :] for c in range(KC)],
                        [arena[:, bass.ds(at + c * FF, FF)] for c in range(KC)]).then_inc(e_up, 1)

            def turn_hidden(j, k):
                pe.wait_ge(e_act, j + 1)
                turn(bank[4 + k % 2], he[k % 2], FC).then_inc(e_turned, 1)

            def expert_down(j, k):
                at = weights(j)
                pe.wait_ge(he_t_ready, j + 1)
                product(bank[6 + k % 2][:, :], [he_t[k % 2][:, m, :] for m in range(FC)],
                        [arena[:, bass.ds(at + (KC * FF + m * D), D)] for m in range(FC)]).then_inc(e_down, 1)

            turn_slot(0, 0, 0)
            expert_up(0, 0)
            with pe.Fori(0, SLOT_TILES // UNROLL - 1) as g:
                for k in range(UNROLL):
                    j = g * UNROLL + k
                    turn_slot(j + 1, k + 1, g + (k + 1) // UNROLL)
                    turn_hidden(j, k)
                    expert_up(j + 1, k + 1)
                    expert_down(j, k)
            for k in range(UNROLL):
                j = SLOT_TILES - UNROLL + k
                if k < UNROLL - 1:
                    turn_slot(j + 1, k + 1, SLOT_TILES // UNROLL - 1)
                turn_hidden(j, k)
                if k < UNROLL - 1:
                    expert_up(j + 1, k + 1)
                expert_down(j, k)

            pe.wait_ge(b2_landed, 32)
            pe.wait_ge(e_out, SLOT_TILES)
            with pe.Fori(0, CHUNKS) as c:
                for k in range(CHUNK):
                    pe.wait_ge(gates_ready, c * CHUNK + (k + 1))
                    pe.matmul(bank[0][0:EE, 0:P], gates_now[k], ident[:, :], start=True, stop=True).then_inc(g_turned, 1)
                    pe.wait_ge(g_t_ready, c * CHUNK + (k + 1))
                    pe.wait_ge(f_ready, c * CHUNK + (k + 1))
                    pe.matmul(bank[1 + k][:, :], gates_t[k][0:EE, :], b2_all[0:EE, :],
                              start=True, stop=True).then_inc(g_done, 1)

        @block.vector
        def _(dve):
            dve.memset(pad_src, 0).then_inc(pads_set, 1)
            dve.memset(pad_dst, NO_NODE).then_inc(pads_set, 1)
            dve.memset(agg[:, (TILES - 1) * D:], 0.0).then_inc(tail_zeroed, 1)
            dve.sem_inc(pair_free, CREDIT_PAIR)
            dve.sem_inc(seg_added, CREDIT_BANK)
            for s in (q_less, k_ready, v_ready, qkv_free, x1_ready, base_ready):
                dve.sem_inc(s, 1)
            dve.sem_inc(f_ready, CREDIT_F)

            plan = Steps(dve, plan_own)
            dve.wait_ge(consts, CONSTS)
            plan.done(dve.tensor_scalar(bounds[:, 0, :], count[:, 0:TILES], float(P), None, ALU.mult))
            plan.then(dve.tensor_scalar(bounds[:, 1, :], count[:, 0:TILES], float(P), float(P), ALU.mult, ALU.add))
            dve.wait_ge(ends_in, 16)
            for n, e in enumerate((WIN - 1, 0)):
                plan.done(dve.tensor_tensor(touch[0:WPARTS, n], spread(ends[0:WPARTS, :, e], TILES),
                                            repeat(bounds[0:WPARTS, n, :], WSLOTS), ALU.is_lt))
            assert plan.count == PLAN_TOUCH
            dve.wait_ge(touch_summed, 1)
            plan.then(dve.tensor_reduce(ab, bank[0][:, 0:2 * WSLOTS * TILES]
                                        .rearrange("p (a w n) -> p a n w", a=2, w=WSLOTS), X, ALU.add))
            plan.then(dve.tensor_tensor(pairs_of, ab[:, 1, :], ab[:, 0, :], ALU.subtract))
            plan.then(dve.tensor_scalar(pairs_of, pairs_of, 0.0, None, ALU.max))
            plan.then(dve.tensor_tensor_scan(pair_end, ones32[:, 0:TILES], pairs_of, 0.0, ALU.mult, ALU.add))
            plan.then(dve.tensor_tensor(shift, pairs_of, pair_end, ALU.subtract))
            plan.then(dve.tensor_tensor(shift, shift, ab[:, 0, :], ALU.add))
            plan.then(dve.tensor_tensor(cmp, repeat(pair_end, SETS), spread(pair_no[:, :], TILES), ALU.is_le))
            plan.then(dve.tensor_reduce(node_no, cmp, X, ALU.add))
            plan.then(dve.tensor_tensor(cmp, repeat(count[:, 0:TILES], SETS), spread(node_no, TILES), ALU.is_equal))
            plan.then(dve.tensor_tensor(cmp, cmp, repeat(shift, SETS), ALU.mult))
            plan.then(dve.tensor_reduce(win_no, cmp, X, ALU.add))
            plan.then(dve.tensor_tensor(win_no, win_no, pair_no[:, :], ALU.add))
            plan.done(dve.tensor_scalar(win_idx, win_no, float(WROWS - 1), None, ALU.min))
            plan.done(dve.tensor_scalar(minus_first, node_no, -float(P), None, ALU.mult))
            plan.then(dve.tensor_scalar(agg_off, node_no, float(TILES - 1), float(D), ALU.min, ALU.mult))
            assert plan.count == PLAN_KNOWN, plan.count
            dve.wait_ge(at_summed, 1)
            dve.tensor_copy(agg_at[0:1, :], bank[1][0:1, :]).then_inc(pads_set, 1)

            with dve.Fori(0, CHUNKS) as c:
                dve.wait_ge(x_ready, c + 1)
                dve.sem_inc(dve_mark, 1)
                for k in range(CHUNK):
                    dve.bn_stats(stats6[:, k, :], agg_tile(c * CHUNK + k)).then_inc(bn_own, 1)
                dve.wait_ge(bn_own, c * (2 * CHUNK) + CHUNK)
                dve.sem_inc(dve_mark, 1)
                for k in range(CHUNK):
                    dve.bn_aggr(moments[:, k, :], stats6[:, k, :]).then_inc(bn_own, 1)
                dve.wait_ge(std_done, c + 1)
                dve.reciprocal(rstd[:, :], std[:, :]).then_inc(rstd_done, 1)
                dve.wait_ge(rstd_done, c + 1)
                for k in range(CHUNK):
                    dve.tensor_scalar(agg_tile(c * CHUNK + k), agg_tile(c * CHUNK + k), moments[:, k, 0:1],
                                      rstd[:, k:k + 1], ALU.subtract, ALU.mult).then_inc(xn_done, 1)
                dve.wait_ge(xn_done, c * CHUNK + CHUNK)
                dve.sem_inc(dve_mark, 1)

            dve.wait_ge(win_in, 16 * 2 * SETS)
            for j in range(SETS):
                plan.done(dve.tensor_scalar(local[:, j, :], win_dst[:, j, :], minus_first[:, j:j + 1], None, ALU.add))
            plan.wait()
            half = (P - 1) / 2
            plan.then(dve.tensor_scalar(off_tile, local, half, None, ALU.subtract))
            plan.then(dve.tensor_tensor(off_tile, off_tile, off_tile, ALU.mult))
            plan.then(dve.tensor_scalar(off_tile, off_tile, (half + 0.25) ** 2, float(NO_ROW), ALU.is_gt, ALU.mult))
            plan.then(dve.tensor_tensor(off_tile, off_tile, win_src, ALU.add))
            assert plan.count == PLAN_STEPS, plan.count
            dve.wait_ge(edge_turned, 4)
            for h in range(2):
                dve.tensor_copy(edge_node[:, :, h], bank[2 + h][:, :]).then_inc(edge_ready, 1)
            dve.wait_ge(edge_ready, 4)
            dve.wait_ge(pair_stored, 16 * CHUNKS)
            dve.memset(rows.rearrange("p a b -> p (a b)"), 0.0).then_inc(soft_own, 1)
            dve.memset(k_max, 0.0).then_inc(k_max_done, 1)
            dve.wait_ge(soft_own, 1)
            dve.sem_inc(seg_done, CREDIT_SEG)

            def unpair():
                dve.tensor_tensor(xn_tile, pair_in[:, 0, :], pair_in[:, 1, :], ALU.add).then_inc(xn_ready, 1)

            def match(i, u):
                nodes = edge_node[:, bass.ds(i * PER + u, 1), :].rearrange("p a h -> p (a h)")
                dve.tensor_tensor(pick[:, u], repeat(node16[:, :], 2), spread(nodes, P), ALU.is_equal
                                  ).then_inc(pick_ready, 1)

            def add(i, u):
                at = dve.value_load(agg_at[0:1, bass.ds(i * PER + u, 1)], min_val=0, max_val=(TILES - 1) * D)
                dve.wait_ge(seg_done, i * PER + (CREDIT_SEG + u + 1))
                dve.wait_ge(seg_added, i * PER + (CREDIT_BANK + u))
                to = agg[:, bass.ds(at, D)]
                dve.tensor_tensor(to, bank[4 + u % PBANKS][:, :], to, ALU.add).then_inc(seg_added, 1)

            q3 = qkv_out[:, 0, :].rearrange("p (h d) -> p h d", h=HEADS)
            dve.wait_ge(pads_set, 3)
            dve.wait_ge(pair_landed, 16)
            unpair()
            for u in range(PER):
                match(0, u)
            with dve.Fori(0, TILES) as i:
                for u in range(4):
                    add(i, u)
                dve.wait_ge(q_done, i + 1)
                dve.wait_ge(qkv_free, i + 1)
                dve.tensor_reduce(head[:, 0, :], bank[1][:, :].rearrange("p (h d) -> p h d", h=HEADS), X, ALU.max
                                  ).then_inc(soft_own, 1)
                dve.wait_ge(soft_own, i * 3 + 2)
                dve.tensor_tensor(q3, bank[1][:, :].rearrange("p (h d) -> p h d", h=HEADS), spread(head[:, 0, :], HD),
                                  ALU.subtract).then_inc(q_less, 1)
                dve.wait_ge(k_done, i + 1)
                dve.tensor_scalar(qkv_out[:, 1, :], bank[2][:, :], 0.0, None, ALU.min).then_inc(k_less, 1)
                dve.wait_ge(q_exp, i + 1)
                dve.tensor_reduce(head[:, 1, :], q3, X, ALU.add).then_inc(soft_own, 1)
                dve.wait_ge(soft_own, i * 3 + 3)
                dve.reciprocal(head[:, 2, :], head[:, 1, :]).then_inc(soft_own, 1)
                dve.wait_ge(soft_own, i * 3 + 4)
                dve.tensor_tensor(q3, q3, spread(head[:, 2, :], HD), ALU.mult).then_inc(q_ready, 1)
                dve.wait_ge(k_exp, i + 1)
                dve.scalar_tensor_tensor(out=qkv_out[:, 1, :], in0=bank[2][:, :], scalar=0.0, in1=qkv_out[:, 1, :],
                                         op0=ALU.max, op1=ALU.add).then_inc(k_ready, 1)
                dve.wait_ge(k_ready, i + 2)
                dve.wait_ge(k_max_done, i + 1)
                dve.tensor_tensor(k_max, k_max, qkv_out[:, 1, :], ALU.max).then_inc(k_max_done, 1)
                dve.wait_ge(pair_landed, i * 16 + 32)
                dve.wait_ge(xn_turned, i + 1)
                unpair()
                for u in range(4):
                    match(i + 1, u)
                for u in range(4, PER):
                    add(i, u)
                    match(i + 1, u)

            top_steps = Steps(dve, top_own)
            dve.wait_ge(k_max_turned, 1)
            top_steps.then(dve.tensor_reduce(k_top_col, bank[0][:, :].rearrange("p (c j) -> p c j", c=KC), X, ALU.max))
            for c in range(KC):
                top_steps.done(dve.tensor_scalar(top_diag[:, c, :], ident[:, :], k_top_col[:, c:c + 1], None, ALU.mult))
            dve.wait_ge(top_spread, 1)
            dve.tensor_copy(k_top, bank[1][:, :]).then_inc(k_top_ready, 1)
            dve.wait_ge(k_top_ready, 1)
            with dve.Fori(0, CHUNKS) as c:
                for k in range(CHUNK):
                    dve.wait_ge(kv_landed[k], c * 16 + 16)
                    dve.tensor_tensor(kv_in[k][:, 0, :], kv_in[k][:, 0, :], k_top, ALU.subtract).then_inc(k_shifted, 1)
            dve.wait_ge(kv_used, TILES)
            context = Steps(dve, ctx_own)
            context.then(dve.memset(ctx_t.rearrange("p a b -> p (a b)"), 0.0))
            for h in range(2):
                side = slice(h * HD, (h + 1) * HD)
                context.done(dve.tensor_copy(ctx_t[side, :, side],
                                             bank[2][side, :].rearrange("p (a b) -> p a b", a=KC)[:, :, side]))
            context.done(dve.reciprocal(k_sum, bank[3][:, 0:KC]))
            assert context.count == CTX_STEPS

            dve.wait_ge(wmix_landed, 16 * WMIX)

            def residual(t):
                dve.wait_ge(gin_done, t + 1)
                dve.tensor_tensor(gin, bank[4][:, :], b2_row, ALU.add).then_inc(gin_read, 1)
                dve.wait_ge(xb_ready, t + 1)
                dve.tensor_tensor(xa, bank[3][:, :], x_b, ALU.add).then_inc(xa_done, 1)
                dve.wait_ge(gin_read, t + 1)
                dve.wait_ge(xa_done, t + 1)
                wait_from(dve, x1_b_ready, t)
                dve.scalar_tensor_tensor(out=x1, in0=gin, scalar=0.0, in1=xa, op0=ALU.max, op1=ALU.add
                                         ).then_inc(x1_ready, 1)
                dve.wait_ge(x1_ready, t + 2)
                dve.bn_stats(st6, x1).then_inc(ln_own, 1)
                dve.wait_ge(ln_own, t * 2 + 1)
                dve.sem_inc(dve_mark, 1)
                dve.bn_aggr(mv2, st6).then_inc(ln_own, 1)
                dve.wait_ge(ln_own, t * 2 + 2)
                dve.tensor_scalar(var2, mv2[:, 1:2], EPS, None, ALU.add).then_inc(var_ready, 1)
                dve.wait_ge(rs_ready, t + 1)
                wait_from(dve, xm_turned, t)
                wait_from(dve, xm_kept, t)
                dve.tensor_scalar(xm_now, x1, mv2[:, 0:1], rs2, ALU.subtract, ALU.mult).then_inc(xm_ready, 1)

            def router(t):
                dve.wait_ge(sh_up, t + 1)
                dve.tensor_tensor(logits[:, bass.ds(t * EE, EE)], bank[6][:, FF:FF + EE], br_row, ALU.add
                                  ).then_inc(lg_ready, 1)

            def base(t):
                dve.wait_ge(sh_down, t + 1)
                dve.wait_ge(x1_b_ready, t + 1)
                wait_from(dve, base_stored, t * 16)
                dve.tensor_tensor(base_out, bank[7][:, :], x1_b, ALU.add).then_inc(base_ready, 1)

            residual(0)

            def mixed(t):
                router(t - 1)
                residual(t)
                base(t - 1)

            mixed(1)
            with dve.Fori(2, TILES) as t:
                mixed(t)
            router(TILES - 1)
            base(TILES - 1)

            route = Steps(dve, route_own)
            dve.wait_ge(lg_ready, TILES)
            dve.wait_ge(base_stored, 16 * TILES)
            dve.wait_ge(xm_kept, TILES)

            def by_expert(ap):
                return ap.rearrange("p (a e) -> p a e", e=E)

            def flat(ap):
                return ap.rearrange("p a e -> p (a e)")

            route.then(dve.tensor_reduce(top, by_expert(logits), X, ALU.max))
            route.done(dve.tensor_tensor(less, by_expert(logits), spread(top, E), ALU.subtract))
            assert route.count == ROUTE_LESS
            route.then(dve.tensor_scalar(first_best, count[:, 0:E], -1.0, float(E), ALU.mult, ALU.add))
            route.then(dve.tensor_scalar(key, less, 0.0, None, ALU.is_equal))
            route.then(dve.tensor_tensor(key, key, repeat(first_best, TB), ALU.mult))
            route.then(dve.tensor_reduce(top, key, X, ALU.max))
            route.then(dve.tensor_tensor(hot, key, spread(top, E), ALU.is_equal))
            route.done(dve.tensor_copy(hot16, flat(hot)))
            assert route.count == ROUTE_HOT
            dve.wait_ge(expo_done, 1)
            route.then(dve.tensor_reduce(gate, expo, X, ALU.add))
            route.then(dve.reciprocal(gate, gate))
            dve.wait_ge(hot_summed, 4)
            half = TILES * EE // 2
            for h in range(2):
                cols = slice(h * half, (h + 1) * half)
                route.done(dve.tensor_copy(before[:, cols], bank[h][:, 0:half]))
                route.done(dve.tensor_copy(tile_n[:, cols], bank[2 + h][:, 0:half]))
            route.wait()
            dve.sem_inc(counts_read, 2)
            def of_expert(ap, be):
                return ap.rearrange("p (t e) -> p e t", e=EE)[:, be, :]

            for be in range(EE):
                route.done(dve.tensor_tensor_scan(of_expert(tile_inc, be), ones32[:, 0:TILES], of_expert(tile_n, be),
                                                  0.0, ALU.mult, ALU.add))
            route.wait()
            total = tile_inc[:, (TILES - 1) * EE:]
            route.then(dve.tensor_scalar(tile_bound, count[:, 0:TILES], float(P), None, ALU.mult))
            fits = place.rearrange("p (e t) -> p e t", e=EE)
            route.then(dve.tensor_tensor(fits, spread(total, TILES), repeat(tile_bound, EE), ALU.is_gt))
            route.then(dve.tensor_reduce(n_tiles, fits, X, ALU.add))
            route.then(dve.tensor_tensor_scan(tile_end, ones32[:, 0:EE], n_tiles, 0.0, ALU.mult, ALU.add))
            route.then(dve.tensor_tensor(tile_row, tile_end, n_tiles, ALU.subtract))
            route.then(dve.tensor_scalar(tile_row, tile_row, float(P), None, ALU.mult))
            route.then(dve.tensor_tensor(place, before, tile_inc, ALU.add))
            route.then(dve.tensor_tensor(place, place, tile_n, ALU.subtract))
            route.then(dve.tensor_tensor(key, hot, by_expert(place), ALU.mult))
            route.then(dve.tensor_reduce(rank, key, X, ALU.add))
            route.then(dve.tensor_scalar(keep, rank, float(CAP), None, ALU.is_le))
            route.then(dve.tensor_tensor(gate, gate, keep, ALU.mult))
            route.then(dve.tensor_tensor(place.rearrange("p (t e) -> p t e", e=EE),
                                         place.rearrange("p (t e) -> p t e", e=EE), repeat(tile_row, TILES), ALU.add))
            route.then(dve.tensor_tensor(key, hot, by_expert(place), ALU.mult))
            route.then(dve.tensor_reduce(slot_f, key, X, ALU.add))
            route.then(dve.tensor_scalar(slot_i, slot_f, 1.0, None, ALU.subtract))
            route.then(dve.tensor_tensor(by_expert(gates.rearrange("p t e -> p (t e)")), hot, spread(gate, E), ALU.mult))
            route.then(dve.tensor_tensor(wide, repeat(tile_end, SLOT_TILES), spread(count[:, 0:SLOT_TILES], EE), ALU.is_le))
            route.then(dve.tensor_reduce(expert_f, wide, X, ALU.add))
            route.then(dve.tensor_scalar(weight_at[:, 0:SLOT_TILES], expert_f, float(EE - 1), float(EXPERT_W), ALU.min, ALU.mult))
            route.then(dve.tensor_scalar(bias_at[:, 0:SLOT_TILES], expert_f, float(EE - 1), float(FF), ALU.min, ALU.mult))
            dve.sem_inc(routed, 1)

            dve.wait_ge(b1_landed, 16 * BANKS)

            def add_bias(j, k):
                at = dve.value_load(bias_at[0:1, bass.ds(j, 1)], min_val=0, max_val=(EE - 1) * FF)
                dve.wait_ge(e_up, j + 1)
                dve.tensor_tensor(he[k % 2], bank[2 + k % 2][:, 0:FF], b1_all[:, bass.ds(at, FF)], ALU.add
                                  ).then_inc(e_biased, 1)

            def turn_hidden(j, k):
                dve.wait_ge(e_turned, j + 1)
                dve.tensor_copy(he_t[k % 2].rearrange("p a b -> p (a b)"), bank[4 + k % 2][:, 0:FF]).then_inc(he_t_ready, 1)

            def result(j, k, stored):
                dve.wait_ge(e_down, j + 1)
                dve.wait_ge(ye_stored[k % 2], stored)
                dve.tensor_copy(ye[k % 2], bank[6 + k % 2][:, :]).then_inc(e_out, 1)

            for k in range(CHUNK):
                dve.wait_ge(scattered[k], SCATTERED)
            add_bias(0, 0)
            per = UNROLL // 2
            with dve.Fori(0, SLOT_TILES // UNROLL - 1) as g:
                for k in range(UNROLL):
                    j = g * UNROLL + k
                    turn_hidden(j, k)
                    add_bias(j + 1, k + 1)
                    result(j, k, g * (16 * per) + (YE_FROM + 16 * (k // 2)))
            for k in range(UNROLL):
                j = SLOT_TILES - UNROLL + k
                turn_hidden(j, k)
                if k < UNROLL - 1:
                    add_bias(j + 1, k + 1)
                result(j, k, YE_FROM + 16 * (j // 2))

            with dve.Fori(0, CHUNKS) as c:
                for k in range(CHUNK):
                    t = c * CHUNK + k
                    dve.wait_ge(g_done, t + 1)
                    dve.wait_ge(o_landed[k], c * 16 + (O_FROM + 16))
                    dve.tensor_tensor(o_in[k], bank[1 + k][:, :], o_in[k], ALU.add).then_inc(f_own, 1)
                    dve.wait_ge(y_landed[0][k], c * 16 + (Y_FROM[0] + 16))
                    dve.wait_ge(f_own, t * 2 + 1)
                    dve.scalar_tensor_tensor(out=o_in[k], in0=y_in[k][0], scalar=gate[:, bass.ds(t * BANKS, 1)],
                                             in1=o_in[k], op0=ALU.mult, op1=ALU.add).then_inc(f_own, 1)
                    dve.wait_ge(y_landed[1][k], c * 16 + (Y_FROM[1] + 16))
                    dve.wait_ge(f_own, t * 2 + 2)
                    dve.scalar_tensor_tensor(out=o_in[k], in0=y_in[k][1], scalar=gate[:, bass.ds(t * BANKS + 1, 1)],
                                             in1=o_in[k], op0=ALU.mult, op1=ALU.add).then_inc(f_ready, 1)


_INS = ["x", "src", "dst", "L0_gnn_W1", "L0_gnn_b1", "L0_gnn_W2", "L0_gnn_b2", "L0_mix_w_qkv", "L0_mix_w_proj",
        "L0_mix_b_proj", "L0_ffn_Wr_sp", "L0_ffn_br_sp", "L0_ffn_Wr_fq", "L0_ffn_br_fq", "L0_ffn_Ws1", "L0_ffn_bs1",
        "L0_ffn_Ws2", "L0_ffn_bs2", "L0_ffn_W1_sp", "L0_ffn_b1_sp", "L0_ffn_W2_sp", "L0_ffn_b2_sp", "L0_ffn_W1_fq",
        "L0_ffn_b1_fq", "L0_ffn_W2_fq", "L0_ffn_b2_fq"]


def kernel(**inputs):
    import numpy as _np
    import concourse.bacc as _bacc
    from concourse import mybir as _mybir
    from concourse.bass_utils import run_bass_kernel_spmd as _run

    nc = _bacc.Bacc("TRN2", target_bir_lowering=False, num_devices=1)
    arrays, args = {}, []
    for name in _INS:
        a = _np.ascontiguousarray(inputs[name])
        arrays[f"in_{name}_dram"] = a
        args.append(nc.dram_tensor(f"in_{name}_dram", a.shape, _mybir.dt.from_np(a.dtype), kind="ExternalInput").ap())
    args.append(nc.dram_tensor("out_0_dram", (N, D), _mybir.dt.float32, kind="ExternalOutput").ap())
    gps_layer(nc, *args)
    r = _run(nc, [arrays], core_ids=[0])
    return r.results[0]["out_0_dram"]
```

```python
from contextlib import ExitStack

import concourse.bass as bass
from concourse import mybir

F32 = mybir.dt.float32
F16 = mybir.dt.float16
I32 = mybir.dt.int32
ALU = mybir.AluOpType
ACT = mybir.ActivationFunctionType
X = mybir.AxisListType.X

P = 128
N = 6250
D = 512
KC = D // P
TILES = -(-N // P)
ROWS = TILES * P
TAIL = N - (TILES - 1) * P
CHUNK = 7
CHUNKS = TILES // CHUNK
HEADS = 8
HD = D // HEADS
EDGES = 100000
WIN = 256
WINDOWS = -(-EDGES // WIN)
WROWS = WINDOWS + 1
WSLOTS = 4
WPARTS = WROWS // WSLOTS
PAD = WROWS * WIN - EDGES
NO_NODE = 1 << 20
NO_ROW = 1 << 16
PER = 9
PAIRS = TILES * PER
SETS = 4
PBANKS = 3
E = 8
BANKS = 2
EE = E * BANKS
TB = TILES * BANKS
FF = 256
FC = FF // P
CAP = -(-5 * 32 * 1024 // (4 * E))
BANK_TILES = TILES + E - 1
SLOT_TILES = BANKS * BANK_TILES
EXPERT_W = KC * FF + FC * D
EPS = 1e-5
NEVER = -1e30
UNROLL = 4
STEPS = CHUNK + 1
LATE = 3
TURNS = CHUNKS
CREDIT_PAIR = 2
CREDIT_SEG = PER
CREDIT_BANK = PBANKS
CREDIT_F = CHUNK
CREDIT_SH = 1
CONSTS = 13
PLAN_TOUCH = 4
PLAN_KNOWN = 19
PLAN_STEPS = PLAN_KNOWN + SETS + 4
CTX_STEPS = 4
ROUTE_LESS = 2
ROUTE_HOT = 8
WGIN = 4
WMIX = 9
AHEAD = 3

assert (TILES - 1) % AHEAD == 0 and EXPERT_W % D == 0
assert TILES == CHUNK * CHUNKS and WROWS == WSLOTS * WPARTS
assert WINDOWS + TILES - 1 <= PAIRS and PAIRS + PER <= SETS * P and PER % PBANKS == 0
assert SLOT_TILES <= P and BANK_TILES % UNROLL == 0 and BANK_TILES == TURNS * STEPS


class Steps:

    def __init__(self, engine, sem):
        self.engine, self.sem, self.count = engine, sem, 0

    def done(self, instruction):
        instruction.then_inc(self.sem, 1)
        self.count += 1

    def wait(self):
        self.engine.wait_ge(self.sem, self.count)

    def then(self, instruction):
        self.done(instruction)
        self.wait()


def wait_from(engine, sem, value):
    if not isinstance(value, int) or value > 0:
        engine.wait_ge(sem, value)


def gps_layer(nc, x, src, dst, w1, b1, w2, b2, w_qkv, w_proj, b_proj, wr_sp, br_sp, wr_fq, br_fq,
              ws1, bs1, ws2, bs2, w1_sp, b1_sp, w2_sp, b2_sp, w1_fq, b1_fq, w2_fq, b2_fq, out):
    with ExitStack() as ctx:
        def sb(name, shape, dt):
            return ctx.enter_context(nc.sbuf_tensor(name, shape, dt))

        def sem(name):
            return ctx.enter_context(nc.semaphore(name))

        xn_pair = nc.dram_tensor("xn_pair", (ROWS, 2 * D), F16).ap()
        qkv_rows = nc.dram_tensor("qkv_rows", (ROWS, 3 * D), F32).ap()
        base_rows = nc.dram_tensor("base_rows", (ROWS, D), F32).ap()
        src_win = nc.dram_tensor("src_win", (WROWS, WIN), I32).ap()
        dst_win = nc.dram_tensor("dst_win", (WROWS, WIN), I32).ap()
        slot_x = nc.dram_tensor("slot_x", (SLOT_TILES * P, D), F32).ap()
        slot_y = nc.dram_tensor("slot_y", (SLOT_TILES * P, D), F32).ap()

        AGG = TILES * D
        arena = sb("arena", [P, AGG + KC * 3 * D + KC * D], F32)
        work = sb("work", [P, 14848], F32)
        agg = arena[:, 0:AGG]

        def part(tensor, at, shape, dt=F32):
            n = 1
            for s in shape:
                n *= s
            words = n // 2 if dt == F16 else n
            assert at + words <= tensor.shape[1], (at, shape)
            ap = tensor[:, at:at + words]
            if dt != F32:
                ap = ap.bitcast(dt)
            if len(shape) == 2:
                ap = ap.rearrange("p (a b) -> p a b", a=shape[0])
            if len(shape) == 3:
                ap = ap.rearrange("p (a b c) -> p a b c", a=shape[0], b=shape[1])
            return ap

        def agg_tile(t):
            return agg[:, bass.ds(t * D, D)]

        wqkv_sb = part(arena, AGG, [KC, 3 * D])
        wproj_sb = part(arena, AGG + KC * 3 * D, [KC, D])
        mix_w = part(arena, AGG, [KC, D])
        w1_sb = part(arena, AGG + KC * D, [KC, D])
        w2_sb = part(arena, AGG + 2 * KC * D, [KC, D])

        ident = sb("ident", [P, P], F32)
        ones32 = sb("ones32", [P, P], F32)
        ones16 = sb("ones16", [P, P], F16)
        prefix16 = sb("prefix16", [P, P], F16)
        node16 = sb("node16", [P, P], F16)
        zero16 = sb("zero16", [P, D], F16)
        zero32 = sb("zero32", [P, D], F32)
        count = sb("count", [P, P], F32)
        pair_no = sb("pair_no", [P, SETS], F32)
        eps = sb("eps", [P, 1], F32)
        minus_half = sb("minus_half", [P, 1], F32)
        moments = sb("moments", [P, CHUNK, 2], F32)
        std = sb("std", [P, CHUNK], F32)
        rstd = sb("rstd", [P, CHUNK], F32)
        edge_node = sb("edge_node", [P, SETS * P, 2], F32)
        edge_src = sb("edge_src", [P, SETS * P, 2], I32)
        agg_at = sb("agg_at", [1, SETS * P], I32)
        src_now = sb("src_now", [P, 2 * PER], I32)
        head = sb("head", [P, 3, HEADS], F32)

        pairs_out = part(work, 0, [2 * CHUNK * 2 * D], F16)
        stats6 = part(work, 7168, [CHUNK, 6])
        pw = 7232
        ends = part(work, pw, [WSLOTS, WIN], I32)
        touch = part(work, pw + 1024, [2, WSLOTS, TILES])
        ab = part(work, pw + 1424, [2, TILES])
        pairs_of = part(work, pw + 1524, [TILES])
        pair_end = part(work, pw + 1574, [TILES])
        shift = part(work, pw + 1624, [TILES])
        cmp = part(work, pw + 1674, [SETS, TILES])
        node_no = part(work, pw + 1874, [SETS])
        win_no = part(work, pw + 1880, [SETS])
        win_idx = part(work, pw + 1886, [SETS], I32)
        agg_off = part(work, pw + 1892, [SETS])
        minus_first = part(work, pw + 1898, [SETS])
        pad_src = part(work, pw + 1904, [PAD], I32)
        pad_dst = part(work, pw + 2260, [PAD], I32)
        win_src = part(work, pw + 2624, [SETS, WIN], I32)
        win_dst = part(work, pw + 3648, [SETS, WIN], I32)
        local = part(work, pw + 4672, [SETS, WIN])
        off_tile = part(work, pw + 5696, [SETS, WIN])
        never = part(work, pw + 6720, [D])
        bounds = part(work, pw + 7232, [2, TILES])
        rows = part(work, 0, [2 * PER, 2 * D], F16)
        pick = part(work, 9216, [PER, 2, P], F16)
        pair_in = part(work, 10368, [2, D], F16)
        xn_tile = part(work, 10880, [D])
        xn_t = part(work, 11392, [KC, P])
        qkv_out = part(work, 11904, [3, D])
        k_max = part(work, 13440, [D])
        kv_in = [part(work, 1024 * k, [2, D]) for k in range(AHEAD)]
        k_top = part(work, 3072, [D])
        top_diag = part(work, 3584, [KC, P])
        ctx_t = part(work, 4096, [KC, P])
        k_top_col = part(work, 4608, [KC])
        k_sum = part(work, 4612, [KC])
        b1_col = part(work, 4616, [KC])
        b2_row = part(work, 4640, [D])
        h_now = part(work, 5664, [D])
        h_t = part(work, 6176, [KC, P])
        h1_t = part(work, 6688, [KC, P])
        br_row = part(work, 4624, [EE])
        bproj_row = part(work, 5152, [D])
        q_t = part(work, 6176, [KC, P])
        xm_now = part(work, 6688, [D])
        wr_sb = part(work, 7200, [KC, EE])
        st6 = part(work, 7264, [6])
        var2 = part(work, 7272, [1])
        mv2 = part(work, 7274, [2])
        q_in = part(work, 7428, [D])
        x_in = part(work, 7940, [D])
        x_b = part(work, 8452, [D])
        xa = part(work, 8964, [D])
        logits = part(work, 10112, [TILES * EE])
        ws1_sb = part(work, 10896, [KC, FF])
        ws2_sb = part(work, 11920, [FC, D])
        mean_all = part(work, 12944, [TILES])
        rs_all = part(work, 13042, [TILES])
        bs1_col = part(work, 13092, [FC])
        hs_t = part(work, 13094, [FC, P])
        xm_t = part(work, 13350, [KC, P])
        less = part(work, 0, [TB, E])
        expo = part(work, 784, [TB, E])
        key = part(work, 1568, [TB, E])
        hot = part(work, 2352, [TB, E])
        hot16 = part(work, 3136, [TILES * EE], F16)
        top = part(work, 3528, [TB])
        gate = part(work, 8564, [TB])
        before = part(work, 3724, [TILES * EE])
        tile_n = part(work, 4508, [TILES * EE])
        tile_inc = part(work, 5292, [TILES * EE])
        place = part(work, 6076, [TILES * EE])
        n_tiles = part(work, 6860, [EE])
        tile_end = part(work, 6876, [EE])
        tile_row = part(work, 6892, [EE])
        rank = part(work, 6908, [TB])
        slot_f = part(work, 7006, [TB])
        keep = part(work, 7104, [TB])
        expert_f = part(work, 7202, [SLOT_TILES])
        first_best = part(work, 7314, [E])
        tile_bound = part(work, 7322, [TILES])
        wide = part(work, 0, [SLOT_TILES, EE])
        slot_i = part(work, 8336, [TB], I32)
        weight_at = part(work, 8434, [P], I32)
        bias_at = part(work, 9456, [P], I32)
        gates = part(work, 8672, [TILES, EE])
        stage = [part(work, 512 * k, [D]) for k in range(CHUNK)]
        slot_now = part(work, 9584, [CHUNK * BANKS], I32)
        b1_all = part(work, 3584, [EE * FF])
        sx = [part(work, 512 * k, [D]) for k in range(UNROLL)]
        sx_t = [part(work, 2048 + 512 * k, [KC, P]) for k in range(2)]
        he = [part(work, 3072 + 256 * k, [FF]) for k in range(2)]
        he_t = [part(work, 11920 + 256 * k, [FC, P]) for k in range(2)]
        ye = [part(work, 10896 + 512 * k, [D]) for k in range(2)]
        y_in = [part(arena, 2 * D * k, [D]) for k in range(CHUNK)]
        o_in = [part(arena, 2 * D * k + D, [D]) for k in range(CHUNK)]
        fin = 2 * D * CHUNK
        gates_t = [part(arena, fin + P * k, [P]) for k in range(CHUNK)]
        gates_now = [part(arena, fin + P * CHUNK + (EE + 1) * k, [EE + 1]) for k in range(CHUNK)]
        b2_all = part(arena, fin + (P + EE + 1) * CHUNK, [D])
        assert fin + (P + EE + 1) * CHUNK + D <= E * EXPERT_W

        bank = [ctx.enter_context(nc.psum_tensor(f"bank{k}", [P, D], F32)) for k in range(8)]

        consts = sem("consts")
        edges_copied = sem("edges_copied")
        pads_set, pads_written, ends_in = sem("pads_set"), sem("pads_written"), sem("ends_in")
        plan_own = sem("plan_own")
        touch_summed, at_summed = sem("touch_summed"), sem("at_summed")
        win_in, edge_turned, edge_ready = sem("win_in"), sem("edge_turned"), sem("edge_ready")
        tail_zeroed, x_landed, x_ready = sem("tail_zeroed"), sem("x_landed"), sem("x_ready")
        bn_own, std_done, rstd_done = sem("bn_own"), sem("std_done"), sem("rstd_done")
        xn_done, hi_done, lo_done = sem("xn_done"), sem("hi_done"), sem("lo_done")
        pair_stored, pair_free = sem("pair_stored"), sem("pair_free")
        wqkv_landed, zeros_stored, never_stored = sem("wqkv_landed"), sem("zeros_stored"), sem("never_stored")
        pair_landed, xn_ready = sem("pair_landed"), sem("xn_ready")
        xn_turned, xn_t_ready = sem("xn_turned"), sem("xn_t_ready")
        q_done, k_done, v_done = sem("q_done"), sem("k_done"), sem("v_done")
        q_less, k_less, q_exp, k_exp = sem("q_less"), sem("k_less"), sem("q_exp"), sem("k_exp")
        q_ready, k_ready, v_ready = sem("q_ready"), sem("k_ready"), sem("v_ready")
        qkv_stored, qkv_free = sem("qkv_stored"), sem("qkv_free")
        soft_own, k_max_done = sem("soft_own"), sem("k_max_done")
        src_copied, pick_ready = sem("src_copied"), sem("pick_ready")
        seg_done, seg_added = sem("seg_done"), sem("seg_added")
        row_in = [sem(f"row_in{k}") for k in range(2 * PER)]
        k_max_turned, top_own, top_spread, k_top_ready = (
            sem("k_max_turned"), sem("top_own"), sem("top_spread"), sem("k_top_ready"))
        kv_landed = [sem(f"kv_landed{k}") for k in range(AHEAD)]
        o_landed = [sem(f"o_landed{k}") for k in range(CHUNK)]
        k_shifted, k_expd, kv_used = sem("k_shifted"), sem("k_expd"), sem("kv_used")
        ctx_own, mixw_done, mixw_ready = sem("ctx_own"), sem("mixw_done"), sem("mixw_ready")
        wgin_landed, wmix_landed, q_landed, xr_landed = (
            sem("wgin_landed"), sem("wmix_landed"), sem("q_landed"), sem("xr_landed"))
        h_ready, h_turned, h_t_ready = sem("h_ready"), sem("h_turned"), sem("h_t_ready")
        up_done, up_act, gin_done, gin_kept = sem("up_done"), sem("up_act"), sem("gin_done"), sem("gin_kept")
        q_turned, q_t_ready, att_done = sem("q_turned"), sem("q_t_ready"), sem("att_done")
        xb_ready, xa_done, x1_ready = sem("xb_ready"), sem("xa_done"), sem("x1_ready")
        ln_own, var_ready, rs_ready, xm_ready = sem("ln_own"), sem("var_ready"), sem("rs_ready"), sem("xm_ready")
        xm_turned, xm_t_ready, lg_done, lg_ready = sem("xm_turned"), sem("xm_t_ready"), sem("lg_done"), sem("lg_ready")
        sh_up, sh_act, sh_down = sem("sh_up"), sem("sh_act"), sem("sh_down")
        base_ready, base_stored, ones_set = sem("base_ready"), sem("base_stored"), sem("ones_set")
        route_own, expo_done, hot_summed, counts_read = (
            sem("route_own"), sem("expo_done"), sem("hot_summed"), sem("counts_read"))
        routed, staged = sem("routed"), sem("staged")
        we_landed, b1_landed = sem("we_landed"), sem("b1_landed")
        sx_landed = [sem(f"sx_landed{k}") for k in range(UNROLL)]
        sx_turned, sx_t_ready, e_up, e_biased = sem("sx_turned"), sem("sx_t_ready"), sem("e_up"), sem("e_biased")
        e_act, e_turned, he_t_ready, e_down, e_out = (
            sem("e_act"), sem("e_turned"), sem("he_t_ready"), sem("e_down"), sem("e_out"))
        b2_landed, y_idx_ready, gates_ready = sem("b2_landed"), sem("y_idx_ready"), sem("gates_ready")
        g_turned, g_t_ready, g_done, f_own, f_ready = (
            sem("g_turned"), sem("g_t_ready"), sem("g_done"), sem("f_own"), sem("f_ready"))
        out_stored = [sem(f"out_stored{k}") for k in range(CHUNK)]
        pool_mark, act_mark, dve_mark, sp_mark = sem("pool_mark"), sem("act_mark"), sem("dve_mark"), sem("sp_mark")
        ye_stored = [base_stored, qkv_stored]
        YE_FROM = 16 * TILES
        SCATTER_FROM = 16 * TILES
        scattered = row_in[0:CHUNK]
        SCATTERED = SCATTER_FROM + 16 * CHUNKS * BANKS
        y_landed = [row_in[CHUNK:2 * CHUNK], scattered]
        Y_FROM = [16 * TILES, SCATTERED]
        O_FROM = [0, 16 * CHUNKS]
        OUT_FROM = 16 * CHUNKS

        block = ctx.enter_context(nc.Block())

        def rows_of(t, n=1):
            return bass.ds(t * P, n * P)

        def weight_tiles(w):
            return w.rearrange("(c p) n -> p c n", p=P)

        def spread(ap, n):
            return ap.unsqueeze(2).broadcast_to([ap.shape[0], ap.shape[1], n])

        def repeat(ap, n):
            return ap.unsqueeze(1).broadcast_to([ap.shape[0], n, ap.shape[1]])

        @block.sync
        def _(sp):
            def hold(sem, value):
                if not isinstance(value, int) or value > 0:
                    sp.wait_ge(sem, value)
                    sp.sem_inc(sp_mark, 1)

            agg_tiles = agg.rearrange("p (t d) -> p t d", t=TILES)
            with sp.Fori(0, CHUNKS - 1) as c:
                sp.dma_start(agg_tiles[:, bass.ds(c * CHUNK, CHUNK), :],
                             x[rows_of(c * CHUNK, CHUNK), :].rearrange("(t p) d -> p t d", p=P)
                             ).then_inc(x_landed, 16)
                hold(x_landed, c * 16 + 16)
                sp.sem_inc(x_ready, 1)
            full = TILES - CHUNK
            sp.dma_start(agg_tiles[:, full:TILES - 1, :],
                         x[full * P:(TILES - 1) * P, :].rearrange("(t p) d -> p t d", p=P)
                         ).then_inc(x_landed, 16)
            sp.wait_ge(tail_zeroed, 1)
            sp.dma_start(agg_tiles[0:TAIL, TILES - 1, :], x[(TILES - 1) * P:N, :]).then_inc(x_landed, 16)
            sp.wait_ge(x_landed, 16 * (CHUNKS + 1))
            sp.sem_inc(x_ready, 1)
            sp.dma_start(wqkv_sb, weight_tiles(w_qkv)).then_inc(wqkv_landed, 16)
            sp.dma_start(wproj_sb, weight_tiles(w_proj)).then_inc(wqkv_landed, 16)
            with sp.Fori(0, CHUNKS) as c:
                hold(lo_done, c + 1)
                sp.dma_start(xn_pair[rows_of(c * CHUNK, CHUNK), :].rearrange("(t p) d -> p t d", p=P),
                             pairs_out[:, bass.ds((c % 2) * (CHUNK * 2 * D), CHUNK * 2 * D)]
                             .rearrange("p (t d) -> p t d", t=CHUNK)).then_inc(pair_stored, 16)
                hold(pair_stored, c * 16 + 16)
                sp.sem_inc(pair_free, 1)
            sp.dma_start(slot_x[2 * TILES * P:, :].rearrange("(t p) d -> p t d", p=P),
                         repeat(zero32[:, :], SLOT_TILES - 2 * TILES)).then_inc(zeros_stored, 16)
            sp.wait_ge(seg_done, CREDIT_SEG)
            sp.dma_start(pair_in, xn_pair[0:P, :].rearrange("p (h d) -> p h d", h=2)).then_inc(pair_landed, 16)
            with sp.Fori(0, TILES) as i:
                hold(xn_ready, i + 1)
                sp.dma_start(pair_in, xn_pair[rows_of((i + 1) % TILES), :].rearrange("p (h d) -> p h d", h=2)
                             ).then_inc(pair_landed, 16)
                sp.dma_start(slot_x[rows_of(i * 2, 2), :].rearrange("(t p) d -> p t d", p=P),
                             repeat(zero32[:, :], 2)).then_inc(zeros_stored, 16)
                hold(q_ready, i + 1)
                hold(k_ready, i + 2)
                hold(v_ready, i + 2)
                sp.dma_start(qkv_rows[rows_of(i), :], qkv_out.rearrange("p a d -> p (a d)")
                             ).then_inc(qkv_stored, 16)
                hold(qkv_stored, i * 16 + 16)
                sp.sem_inc(qkv_free, 1)
            sp.dma_start(qkv_rows[N:ROWS, D:2 * D], never[0:ROWS - N, :]).then_inc(never_stored, 16)
            sp.wait_ge(never_stored, 16)
            sp.wait_ge(v_done, TILES)
            sp.dma_start(w1_sb, weight_tiles(w1)).then_inc(wgin_landed, 16)
            sp.wait_ge(seg_done, CREDIT_SEG + PAIRS)

            def kv_load(t, b):
                sp.dma_start(kv_in[b], qkv_rows[rows_of(t), D:3 * D].rearrange("p (a d) -> p a d", a=2)
                             ).then_inc(kv_landed[b], 16)

            def col(v, c):
                return v.rearrange("(c p) -> p c", c=c)

            def row(v):
                return v.unsqueeze(0).broadcast_to([P, v.shape[0]])

            for t in range(AHEAD):
                kv_load(t, t)
            with nc.allow_non_contiguous_dma(reason="bias columns, a few hundred words"):
                sp.dma_start(w2_sb, weight_tiles(w2)).then_inc(wgin_landed, 16)
                sp.dma_start(b1_col, col(b1, KC)).then_inc(wgin_landed, 16)
                sp.dma_start(b2_row, row(b2)).then_inc(wgin_landed, 16)
                sp.wait_ge(k_max_turned, 1)
                loads = [(wr_sb[:, :, 0:E], weight_tiles(wr_sp)), (wr_sb[:, :, E:EE], weight_tiles(wr_fq)),
                         (bproj_row, row(b_proj)), (br_row[:, 0:E], row(br_sp)), (br_row[:, E:EE], row(br_fq)),
                         (ws1_sb, weight_tiles(ws1)), (ws2_sb, weight_tiles(ws2)), (bs1_col, col(bs1, FC)),
                         (q_in, qkv_rows[0:P, 0:D])]
                assert len(loads) == WMIX
                for to, of in loads:
                    sp.dma_start(to, of).then_inc(wmix_landed, 16)
            with sp.Fori(0, (TILES - 1) // AHEAD - 1) as g:
                for k in range(AHEAD):
                    hold(kv_used, g * AHEAD + (k + 1))
                    kv_load(g * AHEAD + (AHEAD + k), k)
            sp.wait_ge(kv_used, TILES - AHEAD)
            kv_load(TILES - 1, 0)

            def mix_load(t, last=False):
                if not isinstance(t, int) or t > 0:
                    hold(q_turned, t)
                    sp.dma_start(q_in, qkv_rows[rows_of(t), 0:D]).then_inc(q_landed, 16)
                hold(xb_ready, t)
                if last:
                    sp.dma_start(x_in[0:TAIL, :], x[(TILES - 1) * P:N, :]).then_inc(xr_landed, 16)
                else:
                    sp.dma_start(x_in, x[rows_of(t), :]).then_inc(xr_landed, 16)

            mix_load(0)
            with sp.Fori(1, TILES - 1) as t:
                mix_load(t)
            mix_load(TILES - 1, last=True)

            sp.wait_ge(routed, 1)
            for b, v in enumerate((b1_sp, b1_fq)):
                sp.dma_start(b1_all[:, b * E * FF:(b + 1) * E * FF], row(v.rearrange("e f -> (e f)"))
                             ).then_inc(b1_landed, 16)

            def base_store(t):
                hold(base_ready, t + 2)
                sp.dma_start(base_rows[rows_of(t), :], agg_tile(t)).then_inc(base_stored, 16)

            def weights_load(b, e):
                wa, wb = ((w1_sp, w2_sp), (w1_fq, w2_fq))[b]
                at = e * EXPERT_W + b * (E * EXPERT_W)
                sp.dma_start(arena[:, bass.ds(at, KC * FF)].rearrange("p (c n) -> p c n", c=KC),
                             wa[bass.ds(e, 1)].rearrange("a (c p) n -> p (a c) n", p=P)).then_inc(we_landed, 16)
                sp.dma_start(arena[:, bass.ds(at + KC * FF, FC * D)].rearrange("p (c n) -> p c n", c=FC),
                             wb[bass.ds(e, 1)].rearrange("a (c p) n -> p (a c) n", p=P)).then_inc(we_landed, 16)

            over = EXPERT_W // D
            with sp.Fori(0, E) as e:
                for k in range(over):
                    base_store(e * over + k)
                hold(base_stored, e * (16 * over) + 16 * over)
                weights_load(0, e)
            with sp.Fori(E * over, TILES) as t:
                base_store(t)
            sp.wait_ge(base_stored, 16 * TILES)
            for k in range(CHUNK):
                sp.wait_ge(scattered[k], SCATTERED)

            def slot_load(j, k):
                sp.dma_start(sx[k], slot_x[rows_of(j), :]).then_inc(sx_landed[k], 16)

            def slot_store(j, k):
                hold(e_out, j + 1)
                sp.dma_start(slot_y[rows_of(j), :], ye[k % 2]).then_inc(ye_stored[k % 2], 16)

            def o_load(t, k):
                sp.dma_start(o_in[k], base_rows[rows_of(t), :]).then_inc(o_landed[k], 16)

            for k in range(UNROLL):
                slot_load(k, k)

            def turn_of_bank0(g):
                for k in range(UNROLL):
                    j = g * UNROLL + k
                    hold(sx_turned, j + 1)
                    slot_load(j + UNROLL, k)
                    slot_store(j, k)

            with sp.Fori(0, E) as e:
                weights_load(1, e)
                turn_of_bank0(e)
            with sp.Fori(E, BANK_TILES // UNROLL) as g:
                turn_of_bank0(g)
            sp.wait_ge(e_down, BANK_TILES)
            for b, v in enumerate((b2_sp, b2_fq)):
                sp.dma_start(b2_all[b * E:(b + 1) * E, :], v).then_inc(b2_landed, 16)
            sp.dma_start(b2_all[EE:EE + 1, :], bs2.unsqueeze(0)).then_inc(b2_landed, 16)
            for k in range(CHUNK - LATE + 1):
                o_load(k, k)

            def turn_of_bank1(h, first=False, last=False):
                for k in range(STEPS):
                    j = h * STEPS + (BANK_TILES + k)
                    if not last or k < STEPS - UNROLL:
                        hold(sx_turned, j + 1)
                        slot_load(j + UNROLL, k % UNROLL)
                    slot_store(j, k)
                    if k:
                        hold(f_ready, h * CHUNK + (k + CREDIT_F))
                        sp.dma_start(base_rows[rows_of(h * CHUNK + (k - 1)), :], o_in[k - 1]
                                     ).then_inc(out_stored[k - 1], 16)
                    if k < LATE - 1:
                        u = CHUNK - LATE + 1 + k
                        if not first:
                            hold(out_stored[u], h * 16)
                        o_load(h * CHUNK + u, u)
                    elif k >= LATE and not last:
                        hold(out_stored[k - LATE], h * 16 + 16)
                        o_load(h * CHUNK + (CHUNK + k - LATE), k - LATE)

            turn_of_bank1(0, first=True)
            with sp.Fori(1, TURNS - 1) as h:
                turn_of_bank1(h)
            turn_of_bank1(TURNS - 1, last=True)

            def o_store(t, k, last=False):
                hold(f_ready, t + (TILES + 1 + CREDIT_F))
                if last:
                    sp.dma_start(out[(TILES - 1) * P:N, :], o_in[k][0:TAIL, :]).then_inc(out_stored[k], 16)
                else:
                    sp.dma_start(out[rows_of(t), :], o_in[k]).then_inc(out_stored[k], 16)

            for k in range(CHUNK):
                sp.wait_ge(out_stored[k], OUT_FROM)
                o_load(k, k)
            for k in range(CHUNK):
                o_store(k, k)
                if k >= LATE:
                    sp.wait_ge(out_stored[k - LATE], OUT_FROM + 16)
                    o_load(CHUNK + k - LATE, k - LATE)
            with sp.Fori(1, CHUNKS - 1) as c:
                for k in range(CHUNK):
                    t = c * CHUNK + k
                    o_store(t, k)
                    kk = (k - LATE) % CHUNK
                    hold(out_stored[kk], c * 16 + (OUT_FROM + (16 if k >= LATE else 0)))
                    o_load(t + (CHUNK - LATE), kk)
            for k in range(CHUNK):
                t = TILES - CHUNK + k
                o_store(t, k, last=k == CHUNK - 1)
                if k < LATE:
                    kk = k - LATE + CHUNK
                    sp.wait_ge(out_stored[kk], OUT_FROM + 16 * (CHUNKS - 1))
                    o_load(t + CHUNK - LATE, kk)
            for k in range(CHUNK):
                sp.wait_ge(out_stored[k], OUT_FROM + 16 * CHUNKS)
            for s in ye_stored:
                sp.wait_ge(s, YE_FROM + 8 * SLOT_TILES)
            sp.wait_ge(zeros_stored, 16 * (TILES + 1))

        @block.gpsimd
        def _(pool):
            made = Steps(pool, consts)
            made.done(pool.memset(ident[:, :], 0.0))
            made.done(pool.memset(ones16[:, :], 1.0))
            made.wait()
            made.done(pool.affine_select(out=ident[:, :], in_=ident[:, :], compare_op=ALU.not_equal, fill=1.0,
                                         base=0, pattern=[[-1, P]], channel_multiplier=1))
            made.done(pool.affine_select(out=prefix16[:, :], in_=ones16[:, :], compare_op=ALU.is_ge, fill=0.0,
                                         base=0, pattern=[[1, P]], channel_multiplier=-1))
            made.done(pool.memset(ones32[:, :], 1.0))
            made.done(pool.iota(count[:, :], [[1, P]], base=0, channel_multiplier=0,
                                allow_small_or_imprecise_dtypes=True))
            made.done(pool.iota(pair_no[:, :], [[P, SETS]], base=0, channel_multiplier=1,
                                allow_small_or_imprecise_dtypes=True))
            made.done(pool.iota(node16[:, :], [[1, P]], base=0, channel_multiplier=0,
                                allow_small_or_imprecise_dtypes=True))
            made.done(pool.memset(eps[:, :], EPS))
            made.done(pool.memset(minus_half[:, :], -0.5))
            made.done(pool.memset(zero16[:, :], 0.0))
            made.done(pool.memset(zero32[:, :], 0.0))
            made.done(pool.memset(never, NEVER))
            assert made.count == CONSTS
            last_node = pool.to_reg(N - 1)
            last_window = pool.to_reg(WROWS - 1)
            last_slot = pool.to_reg(SLOT_TILES * P - 1)
            pool_last = [pool.to_reg(BANK_TILES * P - 1), last_slot]

            pool.wait_ge(ends_in, 16)
            pool.wait_ge(plan_own, PLAN_KNOWN)
            for j in range(SETS):
                for to, of in ((win_src, src_win), (win_dst, dst_win)):
                    pool.indirect_dma_start(out=to[:, j, :], out_offset=None, in_=of[:, :],
                                            in_offset=bass.IndirectOffsetOnAxis(ap=win_idx[:, j:j + 1], axis=0),
                                            bounds_check=last_window, oob_is_err=False).then_inc(win_in, 16)
            with pool.Fori(0, CHUNKS) as c:
                pool.wait_ge(hi_done, c + 1)
                pool.sem_inc(pool_mark, 1)
                pair = pairs_out[:, bass.ds((c % 2) * (CHUNK * 2 * D), CHUNK * 2 * D)] \
                    .rearrange("p (t h d) -> p t h d", t=CHUNK, h=2)
                pool.tensor_tensor(pair[:, :, 1, :],
                                   agg[:, bass.ds(c * (CHUNK * D), CHUNK * D)].rearrange("p (t d) -> p t d", t=CHUNK),
                                   pair[:, :, 0, :], ALU.subtract).then_inc(lo_done, 1)
            pool.wait_ge(edge_ready, 4)
            pool.wait_ge(pair_stored, 16 * CHUNKS)
            with pool.Fori(0, TILES) as i:
                for third in range(PER // PBANKS):
                    g0 = third * PBANKS
                    pool.wait_ge(src_copied, i * (PER // PBANKS) + (third + 1))
                    pool.sem_inc(pool_mark, 1)
                    for s in range(2 * g0, 2 * (g0 + PBANKS)):
                        pool.indirect_dma_start(out=rows[:, s, :], out_offset=None, in_=xn_pair[:, :],
                                                in_offset=bass.IndirectOffsetOnAxis(ap=src_now[:, s:s + 1], axis=0),
                                                bounds_check=last_node, oob_is_err=False).then_inc(row_in[s], 16)

            pool.wait_ge(wmix_landed, 16 * WMIX)

            def x_and_bias(t):
                pool.wait_ge(xr_landed, t * 16 + 16)
                wait_from(pool, xa_done, t)
                pool.sem_inc(pool_mark, 1)
                pool.tensor_tensor(x_b, x_in, bproj_row, ALU.add).then_inc(xb_ready, 1)
                pool.wait_ge(var_ready, t + 1)
                pool.sem_inc(pool_mark, 1)
                pool.tensor_tensor(rs_all[:, bass.ds(t, 1)], var2, minus_half[:, :], ALU.pow).then_inc(rs_ready, 1)

            x_and_bias(0)
            with pool.Fori(1, TILES) as t:
                x_and_bias(t)

            pool.wait_ge(zeros_stored, 16 * (TILES + 1))
            with pool.Fori(0, CHUNKS) as c:
                for k in range(CHUNK):
                    pool.wait_ge(staged, c * (2 * CHUNK) + (2 * k + 2))
                    pool.sem_inc(pool_mark, 1)
                    for b in range(BANKS):
                        pool.indirect_dma_start(
                            out=slot_x[:, :],
                            out_offset=bass.IndirectOffsetOnAxis(ap=slot_now[:, 2 * k + b:2 * k + b + 1], axis=0),
                            in_=stage[k], in_offset=None, bounds_check=last_slot, oob_is_err=False
                        ).then_inc(scattered[k], 16)

            for b in range(BANKS):
                rows_made = (b + 1) * BANK_TILES * P
                for s in ye_stored:
                    pool.wait_ge(s, YE_FROM + 8 * BANK_TILES * (b + 1))
                with pool.Fori(0, CHUNKS) as c:
                    for k in range(CHUNK):
                        n = c * CHUNK + (b * TILES + k + 1)
                        pool.wait_ge(y_idx_ready, n)
                        pool.wait_ge(f_ready, n)
                        pool.sem_inc(pool_mark, 1)
                        pool.indirect_dma_start(out=y_in[k], out_offset=None, in_=slot_y[0:rows_made, :],
                                                in_offset=bass.IndirectOffsetOnAxis(ap=slot_now[:, k:k + 1], axis=0),
                                                bounds_check=pool_last[b], oob_is_err=False
                                                ).then_inc(y_landed[b][k], 16)

        @block.scalar
        def _(act):
            def copy(to, of, **kw):
                return act.activation(to, of, ACT.Copy, **kw)

            def flat(w):
                return w.rearrange("a b -> (a b)")

            def sixteen(v):
                return v.rearrange("(a b) -> a b", a=16)

            act.dma_start(sixteen(flat(dst_win)[0:EDGES]), sixteen(dst)).then_inc(edges_copied, 16)
            act.dma_start(sixteen(flat(src_win)[0:EDGES]), sixteen(src)).then_inc(edges_copied, 16)
            act.wait_ge(pads_set, 2)
            act.dma_start(flat(src_win)[EDGES:].unsqueeze(0), pad_src[0:1, :]).then_inc(pads_written, 16)
            act.dma_start(flat(dst_win)[EDGES:].unsqueeze(0), pad_dst[0:1, :]).then_inc(pads_written, 16)
            act.wait_ge(edges_copied, 32)
            act.wait_ge(pads_written, 32)
            act.dma_start(ends[0:WPARTS, :, :], dst_win.rearrange("(p c) e -> p c e", c=WSLOTS)).then_inc(ends_in, 16)

            act.wait_ge(consts, CONSTS)
            with act.Fori(0, CHUNKS) as c:
                act.wait_ge(bn_own, c * (2 * CHUNK) + 2 * CHUNK)
                act.activation(std[:, :], moments[:, :, 1], ACT.Sqrt, bias=eps[:, 0:1]).then_inc(std_done, 1)
                act.wait_ge(xn_done, c * CHUNK + CHUNK)
                act.wait_ge(pair_free, c + 1)
                act.sem_inc(act_mark, 1)
                pair = pairs_out[:, bass.ds((c % 2) * (CHUNK * 2 * D), CHUNK * 2 * D)] \
                    .rearrange("p (t h d) -> p t h d", t=CHUNK, h=2)
                copy(pair[:, :, 0, :], agg[:, bass.ds(c * (CHUNK * D), CHUNK * D)]
                     .rearrange("p (t d) -> p t d", t=CHUNK)).then_inc(hi_done, 1)

            act.wait_ge(edge_turned, 4)
            for h in range(2):
                copy(edge_src[:, :, h], bank[4 + h][:, :]).then_inc(edge_ready, 1)

            def indices(i, third, summed):
                g0 = third * PBANKS
                act.wait_ge(seg_done, summed)
                act.sem_inc(act_mark, 1)
                copy(src_now[:, 2 * g0:2 * (g0 + PBANKS)],
                     edge_src[:, bass.ds(i * PER + g0, PBANKS), :].rearrange("p g h -> p (g h)")
                     ).then_inc(src_copied, 1)

            act.wait_ge(edge_ready, 4)
            indices(0, 0, CREDIT_SEG)
            indices(0, 1, CREDIT_SEG)
            with act.Fori(0, TILES) as i:
                indices(i, 2, i * PER + CREDIT_SEG)
                act.wait_ge(xn_turned, i + 1)
                copy(xn_t.rearrange("p a b -> p (a b)"), bank[0][:, :]).then_inc(xn_t_ready, 1)
                indices(i + 1, 0, i * PER + (CREDIT_SEG + PBANKS))
                act.wait_ge(q_less, i + 2)
                act.activation(qkv_out[:, 0, :], qkv_out[:, 0, :], ACT.Exp).then_inc(q_exp, 1)
                act.wait_ge(k_less, i + 1)
                act.activation(qkv_out[:, 1, :], qkv_out[:, 1, :], ACT.Exp).then_inc(k_exp, 1)
                act.wait_ge(v_done, i + 1)
                act.wait_ge(qkv_free, i + 1)
                copy(qkv_out[:, 2, :], bank[3][:, :]).then_inc(v_ready, 1)
                indices(i + 1, 1, i * PER + (CREDIT_SEG + 2 * PBANKS))

            act.wait_ge(seg_added, CREDIT_BANK + PAIRS)
            act.wait_ge(wgin_landed, 16 * WGIN)

            def hidden(t):
                wait_from(act, h_turned, t)
                act.sem_inc(act_mark, 1)
                copy(h_now, agg_tile(t)).then_inc(h_ready, 1)

            def relu(t):
                act.wait_ge(up_done, t + 1)
                act.wait_ge(gin_done, t + 1)
                for m in range(KC):
                    act.activation(h1_t[:, m, :], bank[1][:, m * P:(m + 1) * P], ACT.Relu,
                                   bias=b1_col[:, m:m + 1]).then_inc(up_act, 1)

            def turned_hidden(t):
                act.wait_ge(h_turned, t + 1)
                wait_from(act, up_done, t)
                copy(h_t.rearrange("p a b -> p (a b)"), bank[0][:, :]).then_inc(h_t_ready, 1)

            def k_exponent(t, b):
                act.wait_ge(k_shifted, t + 1)
                act.activation(kv_in[b][:, 0, :], kv_in[b][:, 0, :], ACT.Exp).then_inc(k_expd, 1)

            hidden(0)
            turned_hidden(0)
            k_exponent(0, 0)
            with act.Fori(0, (TILES - 1) // AHEAD) as g:
                for k in range(AHEAD):
                    t = g * AHEAD + (k + 1)
                    hidden(t)
                    relu(g * AHEAD + k)
                    turned_hidden(t)
                    k_exponent(t, (k + 1) % AHEAD)
            relu(TILES - 1)
            act.wait_ge(ctx_own, CTX_STEPS)
            act.wait_ge(mixw_done, KC)
            for hp in range(KC):
                copy(mix_w[:, hp, :], bank[4 + hp][:, :], scale=k_sum[:, hp:hp + 1]).then_inc(mixw_ready, 1)

            def turned_q(t):
                act.wait_ge(q_turned, t + 1)
                wait_from(act, att_done, t)
                copy(q_t.rearrange("p a b -> p (a b)"), bank[0][:, :]).then_inc(q_t_ready, 1)

            def turned_xm(t):
                act.wait_ge(xm_turned, t + 1)
                wait_from(act, lg_done, t)
                copy(xm_t.rearrange("p a b -> p (a b)"), bank[5][:, :]).then_inc(xm_t_ready, 1)

            def mixed(t):
                turned_q(t)
                turned_xm(t - 2)

            turned_q(0)
            turned_q(1)
            mixed(2)
            with act.Fori(3, TILES) as t:
                mixed(t)
            turned_xm(TILES - 2)
            turned_xm(TILES - 1)

            act.wait_ge(route_own, ROUTE_LESS)
            act.activation(expo, less, ACT.Exp).then_inc(expo_done, 1)

            act.wait_ge(wmix_landed, 16 * WMIX)
            act.wait_ge(lg_done, TILES)

            def shared_gelu(t):
                act.wait_ge(sh_up, t + (CREDIT_SH + 1))
                act.wait_ge(sh_down, t + CREDIT_SH)
                for m in range(FC):
                    act.activation(hs_t[:, m, :], bank[6][:, m * P:(m + 1) * P], ACT.Gelu,
                                   bias=bs1_col[:, m:m + 1]).then_inc(sh_act, 1)

            with act.Fori(0, CHUNKS) as c:
                for k in range(CHUNK):
                    if k:
                        shared_gelu(c * CHUNK + (k - 1))
                    act.wait_ge(xm_turned, c * CHUNK + (TILES + k + 1))
                    act.wait_ge(sh_up, c * CHUNK + (k + CREDIT_SH))
                    copy(xm_t.rearrange("p a b -> p (a b)"), bank[5][:, :]).then_inc(xm_t_ready, 1)
                shared_gelu(c * CHUNK + (CHUNK - 1))

            def turn_slot(j, k):
                act.wait_ge(sx_turned, j + 1)
                copy(sx_t[k % 2].rearrange("p a b -> p (a b)"), bank[k % 2][:, :]).then_inc(sx_t_ready, 1)

            def expert_gelu(j, k):
                act.wait_ge(e_biased, j + 1)
                act.activation(he[k % 2], he[k % 2], ACT.Gelu).then_inc(e_act, 1)

            with act.Fori(0, BANK_TILES // UNROLL) as g:
                for k in range(UNROLL):
                    turn_slot(g * UNROLL + k, k)
                    expert_gelu(g * UNROLL + k, k)
            for k in range(CHUNK):
                act.wait_ge(scattered[k], SCATTERED)
            with act.Fori(0, TURNS) as h:
                for k in range(STEPS):
                    turn_slot(h * STEPS + (BANK_TILES + k), k)
                    expert_gelu(h * STEPS + (BANK_TILES + k), k)
                    if k < CHUNK:
                        act.wait_ge(y_landed[0][k], h * 16 + Y_FROM[0])
                        act.sem_inc(act_mark, 1)
                        copy(slot_now[:, k:k + 1], slot_i[:, bass.ds(h * (CHUNK * BANKS) + k * BANKS, 1)]
                             ).then_inc(y_idx_ready, 1)

            for k in range(CHUNK):
                act.wait_ge(y_landed[0][k], Y_FROM[0] + 16 * CHUNKS)
                copy(gates_now[k][:, EE:EE + 1], ones32[:, 0:1]).then_inc(ones_set, 1)
            def turned_gates(c, k):
                act.wait_ge(g_turned, c * CHUNK + (k + 1))
                copy(gates_t[k][0:EE + 1, :], bank[0][0:EE + 1, 0:P]).then_inc(g_t_ready, 1)

            act.wait_ge(sx_turned, SLOT_TILES)
            with act.Fori(0, CHUNKS) as c:
                for k in range(CHUNK):
                    act.wait_ge(y_landed[1][k], c * 16 + Y_FROM[1])
                    act.sem_inc(act_mark, 1)
                    copy(slot_now[:, k:k + 1], slot_i[:, bass.ds(c * (CHUNK * BANKS) + (k * BANKS + 1), 1)]
                         ).then_inc(y_idx_ready, 1)
                    copy(gates_now[k][:, 0:EE], gates.rearrange("p t e -> p (t e)")[:, bass.ds(c * (CHUNK * EE) + k * EE, EE)]
                         ).then_inc(gates_ready, 1)
                    if k:
                        turned_gates(c, k - 1)
                turned_gates(c, CHUNK - 1)

        @block.tensor
        def _(pe):
            def turn(to, tile, n=KC):
                for c in range(n):
                    last = pe.transpose(to[:, c * P:(c + 1) * P], tile[:, c * P:(c + 1) * P], ident[:, :])
                return last

            def product(to, stationary, moving):
                for c, (s, m) in enumerate(zip(stationary, moving)):
                    last = pe.matmul(to, s, m, start=c == 0, stop=c == len(stationary) - 1)
                return last

            pe.wait_ge(consts, CONSTS)
            pe.wait_ge(plan_own, PLAN_TOUCH)
            pe.matmul(bank[0][:, 0:2 * WSLOTS * TILES], ones32[0:WPARTS, :],
                      touch[0:WPARTS].rearrange("p a w n -> p (a w n)"), start=True, stop=True).then_inc(touch_summed, 1)
            pe.wait_ge(plan_own, PLAN_KNOWN)
            for j in range(SETS):
                last = pe.matmul(bank[1][0:1, j * P:(j + 1) * P], agg_off[:, j:j + 1], ident[:, :],
                                 start=True, stop=True)
            last.then_inc(at_summed, 1)
            pe.wait_ge(plan_own, PLAN_STEPS)
            for n, of in enumerate((local, off_tile)):
                for h in range(2):
                    for j in range(SETS):
                        last = pe.transpose(bank[2 + 2 * n + h][:, j * P:(j + 1) * P],
                                            of[:, j, h * P:(h + 1) * P], ident[:, :])
                    last.then_inc(edge_turned, 1)

            pe.wait_ge(wqkv_landed, 32)
            pe.wait_ge(edge_ready, 4)
            with pe.Fori(0, TILES) as i:
                def segment(u):
                    for h in range(2):
                        pe.wait_ge(row_in[2 * u + h], i * 16 + 16)
                    pe.wait_ge(pick_ready, i * PER + (u + 1))
                    pe.wait_ge(seg_added, i * PER + (u + 1))
                    to = bank[4 + u % PBANKS][:, :]
                    for h in range(2):
                        for half in range(2):
                            last = pe.matmul(to, pick[:, u, h, :], rows[:, 2 * u + h, half * D:(half + 1) * D],
                                             start=h + half == 0, stop=h + half == 2)
                    last.then_inc(seg_done, 1)

                pe.wait_ge(xn_ready, i + 1)
                turn(bank[0], xn_tile).then_inc(xn_turned, 1)
                for u in range(4):
                    segment(u)
                pe.wait_ge(xn_t_ready, i + 1)
                for n, (free, done) in enumerate(((q_less, q_done), (k_ready, k_done), (v_ready, v_done))):
                    pe.wait_ge(free, i + 1)
                    product(bank[1 + n][:, :], [xn_t[:, c, :] for c in range(KC)],
                            [wqkv_sb[:, c, n * D:(n + 1) * D] for c in range(KC)]).then_inc(done, 1)
                for u in range(4, PER):
                    segment(u)

            pe.wait_ge(k_max_done, TILES + 1)
            turn(bank[0], k_max).then_inc(k_max_turned, 1)
            pe.wait_ge(top_own, 1 + KC)
            for c in range(KC):
                last = pe.matmul(bank[1][:, c * P:(c + 1) * P], ones32[:, :], top_diag[:, c, :], start=True, stop=True)
            last.then_inc(top_spread, 1)
            pe.wait_ge(v_ready, TILES + 1)
            for b in (2, 3):
                pe.matmul(bank[b][:, :], zero16[:, 0:P], zero16[:, :], start=True, stop=True)
            def context(t, b):
                pe.wait_ge(k_expd, t + 1)
                for hp in range(KC):
                    cols = slice(hp * P, (hp + 1) * P)
                    ek, v = kv_in[b][:, 0, cols], kv_in[b][:, 1, cols]
                    pe.matmul(bank[2][:, cols], v, ek, start=False, stop=True, skip_group_check=True)
                    last = pe.matmul(bank[3][:, hp:hp + 1], ek, ones32[:, 0:1], start=False, stop=True,
                                     skip_group_check=True)
                last.then_inc(kv_used, 1)

            def turn_h(t):
                pe.wait_ge(h_ready, t + 1)
                wait_from(pe, h_t_ready, t)
                turn(bank[0], h_now).then_inc(h_turned, 1)

            def gin_up(t):
                pe.wait_ge(h_t_ready, t + 1)
                wait_from(pe, up_act, t * KC)
                for m in range(KC):
                    last = product(bank[1][:, m * P:(m + 1) * P], [w1_sb[:, c, m * P:(m + 1) * P] for c in range(KC)],
                                   [h_t[:, c, :] for c in range(KC)])
                last.then_inc(up_done, 1)

            def gin_down(t):
                pe.wait_ge(up_act, t * KC + KC)
                pe.wait_ge(gin_kept, t + 1)
                product(bank[4][:, :], [h1_t[:, c, :] for c in range(KC)],
                        [w2_sb[:, c, :] for c in range(KC)]).then_inc(gin_done, 1)

            pe.wait_ge(wgin_landed, 16 * WGIN)
            pe.wait_ge(k_top_ready, 1)
            turn_h(0)
            gin_up(0)
            context(0, 0)
            with pe.Fori(0, (TILES - 1) // AHEAD) as g:
                for k in range(AHEAD):
                    t = g * AHEAD + (k + 1)
                    turn_h(t)
                    gin_down(g * AHEAD + k)
                    gin_up(t)
                    context(t, (k + 1) % AHEAD)
            gin_down(TILES - 1)
            pe.wait_ge(ctx_own, CTX_STEPS)
            pe.wait_ge(gin_kept, TILES + 1)
            for hp in range(KC):
                pe.matmul(bank[4 + hp][:, :], ctx_t[:, hp, :], wproj_sb[:, hp, :],
                          start=True, stop=True).then_inc(mixw_done, 1)

            pe.wait_ge(wmix_landed, 16 * WMIX)
            pe.wait_ge(mixw_ready, KC)

            def turn_q(t):
                wait_from(pe, q_landed, t * 16)
                wait_from(pe, q_t_ready, t)
                turn(bank[0], q_in).then_inc(q_turned, 1)

            def attention(t):
                pe.wait_ge(q_t_ready, t + 1)
                wait_from(pe, xa_done, t)
                product(bank[3][:, :], [q_t[:, c, :] for c in range(KC)],
                        [mix_w[:, c, :] for c in range(KC)]).then_inc(att_done, 1)

            def turn_xm(t):
                pe.wait_ge(xm_ready, t + 1)
                wait_from(pe, xm_t_ready, t)
                turn(bank[5], xm_now).then_inc(xm_turned, 1)

            def router(t):
                pe.wait_ge(xm_t_ready, t + 1)
                wait_from(pe, lg_ready, t)
                product(bank[6][:, 0:EE], [xm_t[:, c, :] for c in range(KC)],
                        [wr_sb[:, c, :] for c in range(KC)]).then_inc(lg_done, 1)

            def mixed(t):
                turn_q(t)
                turn_xm(t - 2)
                attention(t)
                router(t - 2)

            for t in range(2):
                turn_q(t)
                attention(t)
            mixed(2)
            with pe.Fori(3, TILES) as t:
                mixed(t)
            for t in (TILES - 2, TILES - 1):
                turn_xm(t)
                router(t)

            pe.wait_ge(route_own, ROUTE_HOT)
            half = TILES * EE // 2
            for n, by in enumerate((prefix16, ones16)):
                for h in range(2):
                    pe.matmul(bank[2 * n + h][:, 0:half], by[:, :], hot16[:, h * half:(h + 1) * half],
                              start=True, stop=True).then_inc(hot_summed, 1)

            pe.wait_ge(counts_read, 2)

            def shared_down(t):
                pe.wait_ge(sh_act, t * FC + (CREDIT_SH + 1) * FC)
                pe.wait_ge(base_ready, t + CREDIT_SH)
                product(bank[7][:, :], [hs_t[:, m, :] for m in range(FC)],
                        [ws2_sb[:, m, :] for m in range(FC)]).then_inc(sh_down, 1)

            with pe.Fori(0, CHUNKS) as c:
                for k in range(CHUNK):
                    t = c * CHUNK + k
                    pe.wait_ge(staged, c * (2 * CHUNK) + (2 * k + 2))
                    pe.wait_ge(xm_t_ready, t + TILES)
                    turn(bank[5], stage[k]).then_inc(xm_turned, 1)
                    if k:
                        shared_down(c * CHUNK + (k - 1))
                    pe.wait_ge(xm_t_ready, t + (TILES + 1))
                    pe.wait_ge(sh_act, t * FC + CREDIT_SH * FC)
                    for m in range(FC):
                        last = product(bank[6][:, m * P:(m + 1) * P],
                                       [ws1_sb[:, n, m * P:(m + 1) * P] for n in range(KC)],
                                       [xm_t[:, n, :] for n in range(KC)])
                    last.then_inc(sh_up, 1)
                shared_down(c * CHUNK + (CHUNK - 1))

            pe.wait_ge(we_landed, 16 * 2 * E)
            pe.wait_ge(routed, 1)

            def turn_slot(j, k, landed):
                pe.wait_ge(sx_landed[k % UNROLL], landed)
                turn(bank[k % 2], sx[k % UNROLL]).then_inc(sx_turned, 1)

            def weights(j):
                return pe.value_load(weight_at[0:1, bass.ds(j, 1)], min_val=0, max_val=(EE - 1) * EXPERT_W)

            def expert_up(j, k):
                at = weights(j)
                pe.wait_ge(sx_t_ready, j + 1)
                product(bank[2 + k % 2][:, 0:FF], [sx_t[k % 2][:, c, :] for c in range(KC)],
                        [arena[:, bass.ds(at + c * FF, FF)] for c in range(KC)]).then_inc(e_up, 1)

            def turn_hidden(j, k):
                pe.wait_ge(e_act, j + 1)
                turn(bank[4 + k % 2], he[k % 2], FC).then_inc(e_turned, 1)

            def expert_down(j, k):
                at = weights(j)
                pe.wait_ge(he_t_ready, j + 1)
                product(bank[6 + k % 2][:, :], [he_t[k % 2][:, m, :] for m in range(FC)],
                        [arena[:, bass.ds(at + (KC * FF + m * D), D)] for m in range(FC)]).then_inc(e_down, 1)

            def filled(j, k, landed):
                turn_slot(j, k, landed)
                turn_hidden(j - 1, k + 1)
                expert_up(j, k)
                expert_down(j - 1, k + 1)

            turn_slot(0, 0, 16)
            expert_up(0, 0)
            for k in range(1, UNROLL):
                filled(k, k, 16)
            with pe.Fori(1, BANK_TILES // UNROLL) as g:
                for k in range(UNROLL):
                    filled(g * UNROLL + k, k, g * 16 + 16)
            pe.wait_ge(we_landed, 16 * 2 * EE)
            with pe.Fori(0, TURNS) as h:
                for k in range(STEPS):
                    filled(h * STEPS + (BANK_TILES + k), k,
                           h * (16 * STEPS // UNROLL) + 16 * (BANK_TILES // UNROLL + k // UNROLL + 1))
            turn_hidden(SLOT_TILES - 1, 1)
            expert_down(SLOT_TILES - 1, 1)

            pe.wait_ge(b2_landed, 48)
            pe.wait_ge(ones_set, CHUNK)
            pe.wait_ge(e_out, SLOT_TILES)
            def gated_bias(c, k):
                pe.wait_ge(g_t_ready, c * CHUNK + (k + 1))
                pe.wait_ge(f_ready, c * CHUNK + (TILES + k + 1))
                pe.matmul(bank[1 + k][:, :], gates_t[k][0:EE + 1, :], b2_all[0:EE + 1, :],
                          start=True, stop=True).then_inc(g_done, 1)

            with pe.Fori(0, CHUNKS) as c:
                for k in range(CHUNK):
                    pe.wait_ge(gates_ready, c * CHUNK + (k + 1))
                    if k:
                        pe.wait_ge(g_t_ready, c * CHUNK + k)
                    pe.matmul(bank[0][0:EE + 1, 0:P], gates_now[k], ident[:, :], start=True, stop=True).then_inc(g_turned, 1)
                    if k:
                        gated_bias(c, k - 1)
                gated_bias(c, CHUNK - 1)

        @block.vector
        def _(dve):
            dve.memset(pad_src, 0).then_inc(pads_set, 1)
            dve.memset(pad_dst, NO_NODE).then_inc(pads_set, 1)
            dve.memset(agg[:, (TILES - 1) * D:], 0.0).then_inc(tail_zeroed, 1)
            dve.sem_inc(pair_free, CREDIT_PAIR)
            dve.sem_inc(seg_added, CREDIT_BANK)
            for s in (q_less, k_ready, v_ready, qkv_free, gin_done, gin_kept):
                dve.sem_inc(s, 1)
            for s, n in ((sh_up, 1), (sh_down, 1), (base_ready, 1), (sh_act, FC)):
                dve.sem_inc(s, n * CREDIT_SH)
            dve.sem_inc(f_ready, CREDIT_F)

            plan = Steps(dve, plan_own)
            dve.wait_ge(consts, CONSTS)
            plan.done(dve.tensor_scalar(bounds[:, 0, :], count[:, 0:TILES], float(P), None, ALU.mult))
            plan.then(dve.tensor_scalar(bounds[:, 1, :], count[:, 0:TILES], float(P), float(P), ALU.mult, ALU.add))
            dve.wait_ge(ends_in, 16)
            for n, e in enumerate((WIN - 1, 0)):
                plan.done(dve.tensor_tensor(touch[0:WPARTS, n], spread(ends[0:WPARTS, :, e], TILES),
                                            repeat(bounds[0:WPARTS, n, :], WSLOTS), ALU.is_lt))
            assert plan.count == PLAN_TOUCH
            dve.wait_ge(touch_summed, 1)
            plan.then(dve.tensor_reduce(ab, bank[0][:, 0:2 * WSLOTS * TILES]
                                        .rearrange("p (a w n) -> p a n w", a=2, w=WSLOTS), X, ALU.add))
            plan.then(dve.tensor_tensor(pairs_of, ab[:, 1, :], ab[:, 0, :], ALU.subtract))
            plan.then(dve.tensor_scalar(pairs_of, pairs_of, 0.0, None, ALU.max))
            plan.then(dve.tensor_tensor_scan(pair_end, ones32[:, 0:TILES], pairs_of, 0.0, ALU.mult, ALU.add))
            plan.then(dve.tensor_tensor(shift, pairs_of, pair_end, ALU.subtract))
            plan.then(dve.tensor_tensor(shift, shift, ab[:, 0, :], ALU.add))
            plan.then(dve.tensor_tensor(cmp, repeat(pair_end, SETS), spread(pair_no[:, :], TILES), ALU.is_le))
            plan.then(dve.tensor_reduce(node_no, cmp, X, ALU.add))
            plan.then(dve.tensor_tensor(cmp, repeat(count[:, 0:TILES], SETS), spread(node_no, TILES), ALU.is_equal))
            plan.then(dve.tensor_tensor(cmp, cmp, repeat(shift, SETS), ALU.mult))
            plan.then(dve.tensor_reduce(win_no, cmp, X, ALU.add))
            plan.then(dve.tensor_tensor(win_no, win_no, pair_no[:, :], ALU.add))
            plan.done(dve.tensor_scalar(win_idx, win_no, float(WROWS - 1), None, ALU.min))
            plan.done(dve.tensor_scalar(minus_first, node_no, -float(P), None, ALU.mult))
            plan.then(dve.tensor_scalar(agg_off, node_no, float(TILES - 1), float(D), ALU.min, ALU.mult))
            assert plan.count == PLAN_KNOWN, plan.count
            dve.wait_ge(at_summed, 1)
            dve.tensor_copy(agg_at[0:1, :], bank[1][0:1, :]).then_inc(pads_set, 1)

            with dve.Fori(0, CHUNKS) as c:
                dve.wait_ge(x_ready, c + 1)
                dve.sem_inc(dve_mark, 1)
                for k in range(CHUNK):
                    dve.bn_stats(stats6[:, k, :], agg_tile(c * CHUNK + k)).then_inc(bn_own, 1)
                dve.wait_ge(bn_own, c * (2 * CHUNK) + CHUNK)
                dve.sem_inc(dve_mark, 1)
                for k in range(CHUNK):
                    dve.bn_aggr(moments[:, k, :], stats6[:, k, :]).then_inc(bn_own, 1)
                dve.wait_ge(std_done, c + 1)
                dve.reciprocal(rstd[:, :], std[:, :]).then_inc(rstd_done, 1)
                dve.wait_ge(rstd_done, c + 1)
                for k in range(CHUNK):
                    dve.tensor_scalar(agg_tile(c * CHUNK + k), agg_tile(c * CHUNK + k), moments[:, k, 0:1],
                                      rstd[:, k:k + 1], ALU.subtract, ALU.mult).then_inc(xn_done, 1)
                dve.wait_ge(xn_done, c * CHUNK + CHUNK)
                dve.sem_inc(dve_mark, 1)

            dve.wait_ge(win_in, 16 * 2 * SETS)
            for j in range(SETS):
                plan.done(dve.tensor_scalar(local[:, j, :], win_dst[:, j, :], minus_first[:, j:j + 1], None, ALU.add))
            plan.wait()
            half = (P - 1) / 2
            plan.then(dve.tensor_scalar(off_tile, local, half, None, ALU.subtract))
            plan.then(dve.tensor_tensor(off_tile, off_tile, off_tile, ALU.mult))
            plan.then(dve.tensor_scalar(off_tile, off_tile, (half + 0.25) ** 2, float(NO_ROW), ALU.is_gt, ALU.mult))
            plan.then(dve.tensor_tensor(off_tile, off_tile, win_src, ALU.add))
            assert plan.count == PLAN_STEPS, plan.count
            dve.wait_ge(edge_turned, 4)
            for h in range(2):
                dve.tensor_copy(edge_node[:, :, h], bank[2 + h][:, :]).then_inc(edge_ready, 1)
            dve.wait_ge(edge_ready, 4)
            dve.wait_ge(pair_stored, 16 * CHUNKS)
            dve.memset(rows.rearrange("p a b -> p (a b)"), 0.0).then_inc(soft_own, 1)
            dve.memset(k_max, 0.0).then_inc(k_max_done, 1)
            dve.wait_ge(soft_own, 1)
            dve.sem_inc(seg_done, CREDIT_SEG)

            def unpair():
                dve.tensor_tensor(xn_tile, pair_in[:, 0, :], pair_in[:, 1, :], ALU.add).then_inc(xn_ready, 1)

            def match(i, u):
                nodes = edge_node[:, bass.ds(i * PER + u, 1), :].rearrange("p a h -> p (a h)")
                dve.tensor_tensor(pick[:, u], repeat(node16[:, :], 2), spread(nodes, P), ALU.is_equal
                                  ).then_inc(pick_ready, 1)

            def add(i, u):
                at = dve.value_load(agg_at[0:1, bass.ds(i * PER + u, 1)], min_val=0, max_val=(TILES - 1) * D)
                dve.wait_ge(seg_done, i * PER + (CREDIT_SEG + u + 1))
                dve.wait_ge(seg_added, i * PER + (CREDIT_BANK + u))
                to = agg[:, bass.ds(at, D)]
                dve.tensor_tensor(to, bank[4 + u % PBANKS][:, :], to, ALU.add).then_inc(seg_added, 1)

            q3 = qkv_out[:, 0, :].rearrange("p (h d) -> p h d", h=HEADS)
            dve.wait_ge(pads_set, 3)
            dve.wait_ge(pair_landed, 16)
            unpair()
            for u in range(PER):
                match(0, u)
            with dve.Fori(0, TILES) as i:
                for u in range(4):
                    add(i, u)
                dve.wait_ge(q_done, i + 1)
                dve.wait_ge(qkv_free, i + 1)
                dve.tensor_reduce(head[:, 0, :], bank[1][:, :].rearrange("p (h d) -> p h d", h=HEADS), X, ALU.max
                                  ).then_inc(soft_own, 1)
                dve.wait_ge(soft_own, i * 3 + 2)
                dve.tensor_tensor(q3, bank[1][:, :].rearrange("p (h d) -> p h d", h=HEADS), spread(head[:, 0, :], HD),
                                  ALU.subtract).then_inc(q_less, 1)
                dve.wait_ge(k_done, i + 1)
                dve.tensor_scalar(qkv_out[:, 1, :], bank[2][:, :], 0.0, None, ALU.min).then_inc(k_less, 1)
                dve.wait_ge(q_exp, i + 1)
                dve.tensor_reduce(head[:, 1, :], q3, X, ALU.add).then_inc(soft_own, 1)
                dve.wait_ge(soft_own, i * 3 + 3)
                dve.reciprocal(head[:, 2, :], head[:, 1, :]).then_inc(soft_own, 1)
                dve.wait_ge(soft_own, i * 3 + 4)
                dve.tensor_tensor(q3, q3, spread(head[:, 2, :], HD), ALU.mult).then_inc(q_ready, 1)
                dve.wait_ge(k_exp, i + 1)
                dve.scalar_tensor_tensor(out=qkv_out[:, 1, :], in0=bank[2][:, :], scalar=0.0, in1=qkv_out[:, 1, :],
                                         op0=ALU.max, op1=ALU.add).then_inc(k_ready, 1)
                dve.wait_ge(k_ready, i + 2)
                dve.wait_ge(k_max_done, i + 1)
                dve.tensor_tensor(k_max, k_max, qkv_out[:, 1, :], ALU.max).then_inc(k_max_done, 1)
                dve.wait_ge(pair_landed, i * 16 + 32)
                dve.wait_ge(xn_turned, i + 1)
                unpair()
                for u in range(4):
                    match(i + 1, u)
                for u in range(4, PER):
                    add(i, u)
                    match(i + 1, u)

            top_steps = Steps(dve, top_own)
            dve.wait_ge(k_max_turned, 1)
            top_steps.then(dve.tensor_reduce(k_top_col, bank[0][:, :].rearrange("p (c j) -> p c j", c=KC), X, ALU.max))
            for c in range(KC):
                top_steps.done(dve.tensor_scalar(top_diag[:, c, :], ident[:, :], k_top_col[:, c:c + 1], None, ALU.mult))
            dve.wait_ge(top_spread, 1)
            dve.tensor_copy(k_top, bank[1][:, :]).then_inc(k_top_ready, 1)
            dve.wait_ge(k_top_ready, 1)
            dve.wait_ge(wgin_landed, 16 * WGIN)

            def shift_k(b, turn):
                dve.wait_ge(kv_landed[b], turn * 16 + 16)
                dve.tensor_tensor(kv_in[b][:, 0, :], kv_in[b][:, 0, :], k_top, ALU.subtract).then_inc(k_shifted, 1)

            def keep_gin(t):
                dve.wait_ge(gin_done, t + 2)
                dve.tensor_tensor(agg_tile(t), bank[4][:, :], b2_row, ALU.add).then_inc(gin_kept, 1)

            shift_k(0, 0)
            with dve.Fori(0, (TILES - 1) // AHEAD) as g:
                for k in range(AHEAD):
                    shift_k((k + 1) % AHEAD, g + (k + 1) // AHEAD)
                    keep_gin(g * AHEAD + k)
            keep_gin(TILES - 1)
            dve.wait_ge(kv_used, TILES)
            context = Steps(dve, ctx_own)
            context.then(dve.memset(ctx_t.rearrange("p a b -> p (a b)"), 0.0))
            for h in range(2):
                side = slice(h * HD, (h + 1) * HD)
                context.done(dve.tensor_copy(ctx_t[side, :, side],
                                             bank[2][side, :].rearrange("p (a b) -> p a b", a=KC)[:, :, side]))
            context.done(dve.reciprocal(k_sum, bank[3][:, 0:KC]))
            assert context.count == CTX_STEPS

            dve.wait_ge(wmix_landed, 16 * WMIX)
            dve.wait_ge(gin_kept, TILES + 1)

            def residual(t):
                dve.wait_ge(att_done, t + 1)
                dve.wait_ge(xb_ready, t + 1)
                dve.tensor_tensor(xa, bank[3][:, :], x_b, ALU.add).then_inc(xa_done, 1)
                dve.wait_ge(xa_done, t + 1)
                dve.scalar_tensor_tensor(out=agg_tile(t), in0=agg_tile(t), scalar=0.0, in1=xa, op0=ALU.max, op1=ALU.add
                                         ).then_inc(x1_ready, 1)
                dve.wait_ge(x1_ready, t + 1)
                dve.sem_inc(dve_mark, 1)
                dve.bn_stats(st6, agg_tile(t)).then_inc(ln_own, 1)
                dve.wait_ge(ln_own, t * 3 + 1)
                dve.sem_inc(dve_mark, 1)
                dve.bn_aggr(mv2, st6).then_inc(ln_own, 1)
                dve.wait_ge(ln_own, t * 3 + 2)
                dve.tensor_scalar(var2, mv2[:, 1:2], EPS, None, ALU.add).then_inc(var_ready, 1)
                dve.tensor_copy(mean_all[:, bass.ds(t, 1)], mv2[:, 0:1]).then_inc(ln_own, 1)
                dve.wait_ge(rs_ready, t + 1)
                wait_from(dve, xm_turned, t)
                dve.tensor_scalar(xm_now, agg_tile(t), mv2[:, 0:1], rs_all[:, bass.ds(t, 1)], ALU.subtract, ALU.mult
                                  ).then_inc(xm_ready, 1)

            def keep_logits(t):
                dve.wait_ge(lg_done, t + 1)
                dve.tensor_tensor(logits[:, bass.ds(t * EE, EE)], bank[6][:, 0:EE], br_row, ALU.add
                                  ).then_inc(lg_ready, 1)

            residual(0)
            residual(1)
            with dve.Fori(2, TILES) as t:
                residual(t)
                keep_logits(t - 2)
            keep_logits(TILES - 2)
            keep_logits(TILES - 1)

            route = Steps(dve, route_own)
            dve.wait_ge(lg_ready, TILES)

            def by_expert(ap):
                return ap.rearrange("p (a e) -> p a e", e=E)

            def flat(ap):
                return ap.rearrange("p a e -> p (a e)")

            route.then(dve.tensor_reduce(top, by_expert(logits), X, ALU.max))
            route.done(dve.tensor_tensor(less, by_expert(logits), spread(top, E), ALU.subtract))
            assert route.count == ROUTE_LESS
            route.then(dve.tensor_scalar(first_best, count[:, 0:E], -1.0, float(E), ALU.mult, ALU.add))
            route.then(dve.tensor_scalar(key, less, 0.0, None, ALU.is_equal))
            route.then(dve.tensor_tensor(key, key, repeat(first_best, TB), ALU.mult))
            route.then(dve.tensor_reduce(top, key, X, ALU.max))
            route.then(dve.tensor_tensor(hot, key, spread(top, E), ALU.is_equal))
            route.done(dve.tensor_copy(hot16, flat(hot)))
            assert route.count == ROUTE_HOT
            dve.wait_ge(expo_done, 1)
            route.then(dve.tensor_reduce(gate, expo, X, ALU.add))
            route.then(dve.reciprocal(gate, gate))
            dve.wait_ge(hot_summed, 4)
            half = TILES * EE // 2
            for h in range(2):
                cols = slice(h * half, (h + 1) * half)
                route.done(dve.tensor_copy(before[:, cols], bank[h][:, 0:half]))
                route.done(dve.tensor_copy(tile_n[:, cols], bank[2 + h][:, 0:half]))
            route.wait()
            dve.sem_inc(counts_read, 2)
            def of_expert(ap, be):
                return ap.rearrange("p (t e) -> p e t", e=EE)[:, be, :]

            for be in range(EE):
                route.done(dve.tensor_tensor_scan(of_expert(tile_inc, be), ones32[:, 0:TILES], of_expert(tile_n, be),
                                                  0.0, ALU.mult, ALU.add))
            route.wait()
            total = tile_inc[:, (TILES - 1) * EE:]
            route.then(dve.tensor_scalar(tile_bound, count[:, 0:TILES], float(P), None, ALU.mult))
            fits = place.rearrange("p (e t) -> p e t", e=EE)
            route.then(dve.tensor_tensor(fits, spread(total, TILES), repeat(tile_bound, EE), ALU.is_gt))
            route.then(dve.tensor_reduce(n_tiles, fits, X, ALU.add))
            for b in range(BANKS):
                of = slice(b * E, (b + 1) * E)
                route.done(dve.tensor_tensor_scan(tile_end[:, of], ones32[:, 0:E], n_tiles[:, of], float(b * BANK_TILES),
                                                  ALU.mult, ALU.add))
            route.wait()
            route.then(dve.tensor_tensor(tile_row, tile_end, n_tiles, ALU.subtract))
            route.then(dve.tensor_scalar(tile_row, tile_row, float(P), None, ALU.mult))
            route.then(dve.tensor_tensor(place, before, tile_inc, ALU.add))
            route.then(dve.tensor_tensor(place, place, tile_n, ALU.subtract))
            route.then(dve.tensor_tensor(key, hot, by_expert(place), ALU.mult))
            route.then(dve.tensor_reduce(rank, key, X, ALU.add))
            route.then(dve.tensor_scalar(keep, rank, float(CAP), None, ALU.is_le))
            route.then(dve.tensor_tensor(gate, gate, keep, ALU.mult))
            route.then(dve.tensor_tensor(place.rearrange("p (t e) -> p t e", e=EE),
                                         place.rearrange("p (t e) -> p t e", e=EE), repeat(tile_row, TILES), ALU.add))
            route.then(dve.tensor_tensor(key, hot, by_expert(place), ALU.mult))
            route.then(dve.tensor_reduce(slot_f, key, X, ALU.add))
            route.then(dve.tensor_scalar(slot_i, slot_f, 1.0, None, ALU.subtract))
            route.then(dve.tensor_tensor(by_expert(gates.rearrange("p t e -> p (t e)")), hot, spread(gate, E), ALU.mult))
            route.then(dve.tensor_tensor(wide, repeat(tile_end, SLOT_TILES), spread(count[:, 0:SLOT_TILES], EE), ALU.is_le))
            route.then(dve.tensor_reduce(expert_f, wide, X, ALU.add))
            for b in range(BANKS):
                of = slice(b * BANK_TILES, (b + 1) * BANK_TILES)
                last = float((b + 1) * E - 1)
                route.done(dve.tensor_scalar(weight_at[:, of], expert_f[:, of], last, float(EXPERT_W), ALU.min, ALU.mult))
                route.done(dve.tensor_scalar(bias_at[:, of], expert_f[:, of], last, float(FF), ALU.min, ALU.mult))
            route.wait()
            dve.sem_inc(routed, 1)

            def stage_xm(c, k):
                t = c * CHUNK + k
                dve.wait_ge(scattered[k], c * 32 + SCATTER_FROM)
                dve.tensor_scalar(stage[k], agg_tile(t), mean_all[:, bass.ds(t, 1)], rs_all[:, bass.ds(t, 1)], ALU.subtract, ALU.mult
                                  ).then_inc(staged, 1)
                dve.tensor_copy(slot_now[:, 2 * k:2 * k + 2], slot_i[:, bass.ds(c * (CHUNK * BANKS) + k * BANKS, BANKS)]
                                ).then_inc(staged, 1)

            def keep_base(t):
                dve.wait_ge(sh_down, t + (CREDIT_SH + 1))
                dve.tensor_tensor(agg_tile(t), bank[7][:, :], agg_tile(t), ALU.add).then_inc(base_ready, 1)

            with dve.Fori(0, CHUNKS) as c:
                stage_xm(c, 0)
                for k in range(1, CHUNK):
                    stage_xm(c, k)
                    keep_base(c * CHUNK + (k - 1))
                keep_base(c * CHUNK + (CHUNK - 1))

            dve.wait_ge(b1_landed, 16 * BANKS)

            def add_bias(j, k):
                at = dve.value_load(bias_at[0:1, bass.ds(j, 1)], min_val=0, max_val=(EE - 1) * FF)
                dve.wait_ge(e_up, j + 1)
                dve.tensor_tensor(he[k % 2], bank[2 + k % 2][:, 0:FF], b1_all[:, bass.ds(at, FF)], ALU.add
                                  ).then_inc(e_biased, 1)

            def turn_hidden(j, k):
                dve.wait_ge(e_turned, j + 1)
                dve.tensor_copy(he_t[k % 2].rearrange("p a b -> p (a b)"), bank[4 + k % 2][:, 0:FF]).then_inc(he_t_ready, 1)

            def result(j, k, stored):
                dve.wait_ge(e_down, j + 1)
                dve.wait_ge(ye_stored[k % 2], stored)
                dve.tensor_copy(ye[k % 2], bank[6 + k % 2][:, :]).then_inc(e_out, 1)

            def filled(j, k, stored):
                turn_hidden(j - 1, k + 1)
                add_bias(j, k)
                result(j - 1, k + 1, stored)

            for k in range(CHUNK):
                dve.wait_ge(scattered[k], SCATTERED)
            add_bias(0, 0)
            for k in range(1, UNROLL):
                filled(k, k, YE_FROM + 16 * ((k - 1) // 2))
            with dve.Fori(1, BANK_TILES // UNROLL) as g:
                for k in range(UNROLL):
                    filled(g * UNROLL + k, k, g * (8 * UNROLL) + (YE_FROM + 16 * ((k - 1) // 2)))
            with dve.Fori(0, TURNS) as h:
                for k in range(STEPS):
                    filled(h * STEPS + (BANK_TILES + k), k,
                           h * (8 * STEPS) + (YE_FROM + 8 * BANK_TILES + 16 * ((k - 1) // 2)))
                    if k:
                        u = k - 1
                        dve.wait_ge(o_landed[u], h * 16 + (O_FROM[0] + 16))
                        dve.wait_ge(y_landed[0][u], h * 16 + (Y_FROM[0] + 16))
                        dve.scalar_tensor_tensor(out=o_in[u], in0=y_in[u],
                                                 scalar=gate[:, bass.ds(h * (CHUNK * BANKS) + u * BANKS, 1)],
                                                 in1=o_in[u], op0=ALU.mult, op1=ALU.add).then_inc(f_ready, 1)
            turn_hidden(SLOT_TILES - 1, 1)
            result(SLOT_TILES - 1, 1, YE_FROM + 16 * (SLOT_TILES // 2 - 1))

            with dve.Fori(0, CHUNKS) as c:
                for k in range(CHUNK):
                    t = c * CHUNK + k
                    dve.wait_ge(g_done, t + 1)
                    dve.wait_ge(o_landed[k], c * 16 + (O_FROM[1] + 16))
                    dve.tensor_tensor(o_in[k], bank[1 + k][:, :], o_in[k], ALU.add).then_inc(f_own, 1)
                    dve.wait_ge(y_landed[1][k], c * 16 + (Y_FROM[1] + 16))
                    dve.wait_ge(f_own, t + 1)
                    dve.scalar_tensor_tensor(out=o_in[k], in0=y_in[k], scalar=gate[:, bass.ds(t * BANKS + 1, 1)],
                                             in1=o_in[k], op0=ALU.mult, op1=ALU.add).then_inc(f_ready, 1)


_INS = ["x", "src", "dst", "L0_gnn_W1", "L0_gnn_b1", "L0_gnn_W2", "L0_gnn_b2", "L0_mix_w_qkv", "L0_mix_w_proj",
        "L0_mix_b_proj", "L0_ffn_Wr_sp", "L0_ffn_br_sp", "L0_ffn_Wr_fq", "L0_ffn_br_fq", "L0_ffn_Ws1", "L0_ffn_bs1",
        "L0_ffn_Ws2", "L0_ffn_bs2", "L0_ffn_W1_sp", "L0_ffn_b1_sp", "L0_ffn_W2_sp", "L0_ffn_b2_sp", "L0_ffn_W1_fq",
        "L0_ffn_b1_fq", "L0_ffn_W2_fq", "L0_ffn_b2_fq"]


def kernel(**inputs):
    import numpy as _np
    import concourse.bacc as _bacc
    from concourse import mybir as _mybir
    from concourse.bass_utils import run_bass_kernel_spmd as _run

    nc = _bacc.Bacc("TRN2", target_bir_lowering=False, num_devices=1)
    arrays, args = {}, []
    for name in _INS:
        a = _np.ascontiguousarray(inputs[name])
        arrays[f"in_{name}_dram"] = a
        args.append(nc.dram_tensor(f"in_{name}_dram", a.shape, _mybir.dt.from_np(a.dtype), kind="ExternalInput").ap())
    args.append(nc.dram_tensor("out_0_dram", (N, D), _mybir.dt.float32, kind="ExternalOutput").ap())
    gps_layer(nc, *args)
    r = _run(nc, [arrays], core_ids=[0])
    return r.results[0]["out_0_dram"]
```

```python
from contextlib import ExitStack

import concourse.bass as bass
from concourse import mybir

F32 = mybir.dt.float32
F16 = mybir.dt.float16
I32 = mybir.dt.int32
ALU = mybir.AluOpType
ACT = mybir.ActivationFunctionType
X = mybir.AxisListType.X

P = 128
N = 6250
D = 512
KC = D // P
TILES = -(-N // P)
ROWS = TILES * P
TAIL = N - (TILES - 1) * P
CHUNK = 7
CHUNKS = TILES // CHUNK
HEADS = 8
HD = D // HEADS
EDGES = 100000
WIN = 256
WINDOWS = -(-EDGES // WIN)
WROWS = WINDOWS + 1
WSLOTS = 4
WPARTS = WROWS // WSLOTS
PAD = WROWS * WIN - EDGES
NO_NODE = 1 << 20
NO_ROW = 1 << 16
PER = 9
PAIRS = TILES * PER
SETS = 4
PBANKS = 3
E = 8
BANKS = 2
EE = E * BANKS
TB = TILES * BANKS
FF = 256
FC = FF // P
CAP = -(-5 * 32 * 1024 // (4 * E))
BANK_TILES = TILES + E - 1
SLOT_TILES = BANKS * BANK_TILES
EXPERT_W = KC * FF + FC * D
EPS = 1e-5
NEVER = -1e30
UNROLL = 4
BANK_TURNS = BANK_TILES // UNROLL
ROW = D + 1 + BANKS
CREDIT_PAIR = 2
CREDIT_SEG = PER
CREDIT_BANK = PBANKS
CREDIT_O = 2
STAGES = 6
STAGE_FIRST = STAGES + 1
STAGE_TURNS = (TILES - STAGE_FIRST) // STAGES
CONSTS = 15
PLAN_TOUCH = 4
PLAN_KNOWN = 19
PLAN_STEPS = PLAN_KNOWN + SETS + 4
CTX_STEPS = 4
ROUTE_LESS = 2
ROUTE_HOT = 8
WGIN = 3
WMIX = 10
AHEAD = 3

assert (TILES - 1) % AHEAD == 0 and EXPERT_W % D == 0
assert TILES == CHUNK * CHUNKS and WROWS == WSLOTS * WPARTS
assert WINDOWS + TILES - 1 <= PAIRS and PAIRS + PER <= SETS * P and PER % PBANKS == 0
assert SLOT_TILES <= P and BANK_TILES % UNROLL == 0


class Steps:

    def __init__(self, engine, sem):
        self.engine, self.sem, self.count = engine, sem, 0

    def done(self, instruction):
        instruction.then_inc(self.sem, 1)
        self.count += 1

    def wait(self):
        self.engine.wait_ge(self.sem, self.count)

    def then(self, instruction):
        self.done(instruction)
        self.wait()


def wait_from(engine, sem, value):
    if not isinstance(value, int) or value > 0:
        engine.wait_ge(sem, value)


def gps_layer(nc, x, src, dst, w1, b1, w2, b2, w_qkv, w_proj, b_proj, wr_sp, br_sp, wr_fq, br_fq,
              ws1, bs1, ws2, bs2, w1_sp, b1_sp, w2_sp, b2_sp, w1_fq, b1_fq, w2_fq, b2_fq, out):
    with ExitStack() as ctx:
        def sb(name, shape, dt):
            return ctx.enter_context(nc.sbuf_tensor(name, shape, dt))

        def sem(name):
            return ctx.enter_context(nc.semaphore(name))

        xn_pair = nc.dram_tensor("xn_pair", (ROWS, 2 * D), F16).ap()
        qkv_rows = nc.dram_tensor("qkv_rows", (ROWS, 3 * D), F32).ap()
        base_rows = nc.dram_tensor("base_rows", (ROWS, D), F32).ap()
        src_win = nc.dram_tensor("src_win", (WROWS, WIN), I32).ap()
        dst_win = nc.dram_tensor("dst_win", (WROWS, WIN), I32).ap()
        slot_x = nc.dram_tensor("slot_x", (SLOT_TILES * P, ROW), F32).ap()
        half_rows = nc.dram_tensor("half_rows", (ROWS, D), F32).ap()

        AGG = TILES * D
        arena = sb("arena", [P, AGG + KC * 3 * D + KC * D], F32)
        work = sb("work", [P, 14848], F32)
        agg = arena[:, 0:AGG]

        def part(tensor, at, shape, dt=F32):
            n = 1
            for s in shape:
                n *= s
            words = n // 2 if dt == F16 else n
            assert at + words <= tensor.shape[1], (at, shape)
            ap = tensor[:, at:at + words]
            if dt != F32:
                ap = ap.bitcast(dt)
            if len(shape) == 2:
                ap = ap.rearrange("p (a b) -> p a b", a=shape[0])
            if len(shape) == 3:
                ap = ap.rearrange("p (a b c) -> p a b c", a=shape[0], b=shape[1])
            return ap

        def agg_tile(t):
            return agg[:, bass.ds(t * D, D)]

        wqkv_sb = part(arena, AGG, [KC, 3 * D])
        wproj_sb = part(arena, AGG + KC * 3 * D, [KC, D])
        mix_w = part(arena, AGG, [KC, D])
        w1_sb = part(arena, AGG + KC * D, [KC, D])
        w2_sb = part(arena, AGG + 2 * KC * D, [KC, D])

        ident = sb("ident", [P, P], F32)
        ones32 = sb("ones32", [P, P], F32)
        ones16 = sb("ones16", [P, P], F16)
        prefix16 = sb("prefix16", [P, P], F16)
        node16 = sb("node16", [P, P], F16)
        zero16 = sb("zero16", [P, D], F16)
        no_token = sb("no_token", [P, ROW], F32)
        count = sb("count", [P, P], F32)
        pair_no = sb("pair_no", [P, SETS], F32)
        eps = sb("eps", [P, 1], F32)
        minus_half = sb("minus_half", [P, 1], F32)
        moments = sb("moments", [P, CHUNK, 2], F32)
        std = sb("std", [P, CHUNK], F32)
        rstd = sb("rstd", [P, CHUNK], F32)
        edge_node = sb("edge_node", [P, SETS * P, 2], F32)
        edge_src = sb("edge_src", [P, SETS * P, 2], I32)
        agg_at = sb("agg_at", [1, SETS * P], I32)
        src_now = sb("src_now", [P, 2 * PER], I32)
        head = sb("head", [P, 3, HEADS], F32)

        pairs_out = part(work, 0, [2 * CHUNK * 2 * D], F16)
        stats6 = part(work, 7168, [CHUNK, 6])
        pw = 7232
        ends = part(work, pw, [WSLOTS, WIN], I32)
        touch = part(work, pw + 1024, [2, WSLOTS, TILES])
        ab = part(work, pw + 1424, [2, TILES])
        pairs_of = part(work, pw + 1524, [TILES])
        pair_end = part(work, pw + 1574, [TILES])
        shift = part(work, pw + 1624, [TILES])
        cmp = part(work, pw + 1674, [SETS, TILES])
        node_no = part(work, pw + 1874, [SETS])
        win_no = part(work, pw + 1880, [SETS])
        win_idx = part(work, pw + 1886, [SETS], I32)
        agg_off = part(work, pw + 1892, [SETS])
        minus_first = part(work, pw + 1898, [SETS])
        pad_src = part(work, pw + 1904, [PAD], I32)
        pad_dst = part(work, pw + 2260, [PAD], I32)
        win_src = part(work, pw + 2624, [SETS, WIN], I32)
        win_dst = part(work, pw + 3648, [SETS, WIN], I32)
        local = part(work, pw + 4672, [SETS, WIN])
        off_tile = part(work, pw + 5696, [SETS, WIN])
        never = part(work, pw + 6720, [D])
        bounds = part(work, pw + 7232, [2, TILES])
        rows = part(work, 0, [2 * PER, 2 * D], F16)
        pick = part(work, 9216, [PER, 2, P], F16)
        pair_in = part(work, 10368, [2, D], F16)
        xn_tile = part(work, 10880, [D])
        xn_t = part(work, 11392, [KC, P])
        qkv_out = part(work, 11904, [3, D])
        k_max = part(work, 13440, [D])
        kv_in = [part(work, 1024 * k, [2, D]) for k in range(AHEAD)]
        k_top = part(work, 3072, [D])
        top_diag = part(work, 3584, [KC, P])
        ctx_t = part(work, 4096, [KC, P])
        k_top_col = part(work, 4608, [KC])
        k_sum = part(work, 4612, [KC])
        b1_col = part(work, 4616, [KC])
        b2_row = part(work, 4640, [D])
        h_now = part(work, 5664, [D])
        h_t = part(work, 6176, [KC, P])
        h1_t = part(work, 6688, [KC, P])
        br_row = part(work, 4624, [EE])
        bproj_row = part(work, 5152, [D])
        q_t = part(work, 6176, [KC, P])
        xm_now = part(work, 6688, [D])
        wr_sb = part(work, 7200, [KC, EE])
        st6 = part(work, 7264, [6])
        var2 = part(work, 7272, [1])
        mv2 = part(work, 7274, [2])
        q_in = part(work, 7428, [D])
        x_in = part(work, 7940, [D])
        x_b = part(work, 8452, [D])
        xa = part(work, 8964, [D])
        logits = part(work, 10112, [TILES * EE])
        ws1_sb = part(work, 10896, [KC, FF])
        ws2_sb = part(work, 11920, [FC, D])
        mean_all = part(work, 12944, [TILES])
        rs_all = part(work, 13042, [TILES])
        bs1_col = part(work, 13092, [FC])
        hs_t = [part(work, 13094, [FC, P]), part(work, 14374, [FC, P])]
        xm_t = part(work, 13350, [KC, P])
        bs2_row = part(work, 13862, [D])
        less = part(work, 0, [TB, E])
        expo = part(work, 784, [TB, E])
        key = part(work, 1568, [TB, E])
        hot = part(work, 2352, [TB, E])
        hot16 = part(work, 3136, [TILES * EE], F16)
        top = part(work, 3528, [TB])
        gate = part(work, 8564, [TB])
        before = part(work, 3724, [TILES * EE])
        tile_n = part(work, 4508, [TILES * EE])
        tile_inc = part(work, 5292, [TILES * EE])
        place = part(work, 6076, [TILES * EE])
        n_tiles = part(work, 6860, [EE])
        tile_end = part(work, 6876, [EE])
        tile_row = part(work, 6892, [EE])
        rank = part(work, 6908, [TB])
        slot_f = part(work, 7006, [TB])
        keep = part(work, 7104, [TB])
        expert_f = part(work, 7202, [SLOT_TILES])
        first_best = part(work, 7314, [E])
        tile_bound = part(work, 7322, [TILES])
        wide = part(work, 5080, [SLOT_TILES, EE])
        slot_i = part(work, 8336, [TB], I32)
        weight_at = part(work, 8434, [P], I32)
        bias_at = part(work, 9456, [P], I32)
        bias2_at = part(work, 8672, [P], I32)
        info = part(work, 8800, [TILES, 1 + BANKS])
        token_now = [part(work, 8948 + k, [1], I32) for k in range(UNROLL)]
        gate_now = [part(work, 8952 + k, [1]) for k in range(UNROLL)]
        stage = [part(work, ROW * k, [ROW]) for k in range(STAGES)]
        slot_now = part(work, 9584, [STAGES * BANKS], I32)
        b1_all = part(work, 3608, [EE * FF])
        assert ROW * STAGES <= 3608 and STAGE_FIRST + STAGE_TURNS * STAGES == TILES and STAGES % 2 == 0
        sx = [part(work, ROW * k, [ROW]) for k in range(UNROLL)]
        sx_t = [part(work, 2064 + 512 * k, [KC, P]) for k in range(2)]
        he = [part(work, 3088 + 256 * k, [FF]) for k in range(2)]
        he_t = [part(work, 7704 + 256 * k, [FC, P]) for k in range(2)]
        ye = [part(work, 9600 + 512 * k, [D]) for k in range(2)]
        o_in = [edge_node[:, :, :].rearrange("p a b -> p (a b)")[:, k * D:(k + 1) * D] for k in range(2)]
        b2_all = [part(work, 10752, [E * D]), part(arena, 0, [E * D])]

        bank = [ctx.enter_context(nc.psum_tensor(f"bank{k}", [P, D], F32)) for k in range(8)]

        consts = sem("consts")
        edges_copied = sem("edges_copied")
        pads_set, pads_written, ends_in = sem("pads_set"), sem("pads_written"), sem("ends_in")
        plan_own = sem("plan_own")
        touch_summed, at_summed = sem("touch_summed"), sem("at_summed")
        win_in, edge_turned, edge_ready = sem("win_in"), sem("edge_turned"), sem("edge_ready")
        tail_zeroed, x_ready = sem("tail_zeroed"), sem("x_ready")
        x_landed = [sem(f"x_landed{c}") for c in range(CHUNKS)]
        bn_own, std_done, rstd_done = sem("bn_own"), sem("std_done"), sem("rstd_done")
        xn_done, hi_done, lo_done = sem("xn_done"), sem("hi_done"), sem("lo_done")
        pair_stored, pair_free = sem("pair_stored"), sem("pair_free")
        wqkv_landed, zeros_stored, never_stored = sem("wqkv_landed"), sem("zeros_stored"), sem("never_stored")
        pair_landed, xn_ready = sem("pair_landed"), sem("xn_ready")
        xn_turned, xn_t_ready = sem("xn_turned"), sem("xn_t_ready")
        q_done, k_done, v_done = sem("q_done"), sem("k_done"), sem("v_done")
        q_less, k_less, q_exp, k_exp = sem("q_less"), sem("k_less"), sem("q_exp"), sem("k_exp")
        q_ready, k_ready, v_ready = sem("q_ready"), sem("k_ready"), sem("v_ready")
        qkv_stored, qkv_free = sem("qkv_stored"), sem("qkv_free")
        soft_own, k_max_done = sem("soft_own"), sem("k_max_done")
        src_copied, pick_ready = sem("src_copied"), sem("pick_ready")
        seg_done, seg_added = sem("seg_done"), sem("seg_added")
        row_in = [sem(f"row_in{k}") for k in range(2 * PER)]
        k_max_turned, top_own, top_spread, k_top_ready = (
            sem("k_max_turned"), sem("top_own"), sem("top_spread"), sem("k_top_ready"))
        kv_landed = [sem(f"kv_landed{k}") for k in range(AHEAD)]
        k_shifted, k_expd, kv_used = sem("k_shifted"), sem("k_expd"), sem("kv_used")
        ctx_own, mixw_done, mixw_ready = sem("ctx_own"), sem("mixw_done"), sem("mixw_ready")
        wgin_landed, wmix_landed, q_landed, xr_landed = (
            sem("wgin_landed"), sem("wmix_landed"), sem("q_landed"), sem("xr_landed"))
        h_ready, h_turned, h_t_ready = sem("h_ready"), sem("h_turned"), sem("h_t_ready")
        up_done, up_act, gin_done, gin_kept = sem("up_done"), sem("up_act"), sem("gin_done"), sem("gin_kept")
        q_turned, q_t_ready, att_done = sem("q_turned"), sem("q_t_ready"), sem("att_done")
        xb_ready, xa_done, x1_ready = sem("xb_ready"), sem("xa_done"), sem("x1_ready")
        ln_own, var_ready, rs_ready, xm_ready = sem("ln_own"), sem("var_ready"), sem("rs_ready"), sem("xm_ready")
        xm_turned, xm_t_ready, lg_done, lg_ready = sem("xm_turned"), sem("xm_t_ready"), sem("lg_done"), sem("lg_ready")
        sh_up, sh_act, sh_down = sem("sh_up"), sem("sh_act"), sem("sh_down")
        base_ready, base_stored = sem("base_ready"), sem("base_stored")
        route_own, expo_done, hot_summed, counts_read = (
            sem("route_own"), sem("expo_done"), sem("hot_summed"), sem("counts_read"))
        routed, staged = sem("routed"), sem("staged")
        we_landed, b1_landed = sem("we_landed"), sem("b1_landed")
        sx_landed = [sem(f"sx_landed{k}") for k in range(UNROLL)]
        sx_turned, sx_t_ready, e_up, e_biased = sem("sx_turned"), sem("sx_t_ready"), sem("e_up"), sem("e_biased")
        e_act, e_turned, he_t_ready, e_down, e_out = (
            sem("e_act"), sem("e_turned"), sem("he_t_ready"), sem("e_down"), sem("e_out"))
        b2_landed, token_ready, shared_added = sem("b2_landed"), sem("token_ready"), sem("shared_added")
        w1_landed = sem("w1_landed")
        e_own, o_set = sem("e_own"), sem("o_set")
        pool_mark, act_mark, dve_mark, sp_mark = sem("pool_mark"), sem("act_mark"), sem("dve_mark"), sem("sp_mark")
        SCATTER_FROM = 16 * TILES
        scattered = row_in[0:STAGES]
        SCATTERED = [SCATTER_FROM + 16 * BANKS * len(range(k, TILES, STAGES)) for k in range(STAGES)]
        o_landed, y_scattered = row_in[CHUNK:CHUNK + 2], row_in[CHUNK + 2:CHUNK + 4]
        Y_FROM = 16 * TILES

        SHARED_UP = (6, 4)

        block = ctx.enter_context(nc.Block())

        def each_stage(engine, step):
            for t in range(STAGE_FIRST):
                step(t, t % STAGES, t // STAGES)
            with engine.Fori(0, STAGE_TURNS) as g:
                for k in range(STAGES):
                    t = STAGE_FIRST + k
                    step(g * STAGES + t, t % STAGES, g + t // STAGES)

        def rows_of(t, n=1):
            return bass.ds(t * P, n * P)

        def weight_tiles(w):
            return w.rearrange("(c p) n -> p c n", p=P)

        def spread(ap, n):
            return ap.unsqueeze(2).broadcast_to([ap.shape[0], ap.shape[1], n])

        def repeat(ap, n):
            return ap.unsqueeze(1).broadcast_to([ap.shape[0], n, ap.shape[1]])

        @block.sync
        def _(sp):
            def hold(sem, value):
                if not isinstance(value, int) or value > 0:
                    sp.wait_ge(sem, value)
                    sp.sem_inc(sp_mark, 1)

            def line(w):
                return w.rearrange("a b -> (a b)")

            def sixteen(v):
                return v.rearrange("(a b) -> a b", a=16)

            sp.dma_start(sixteen(line(dst_win)[0:EDGES]), sixteen(dst)).then_inc(edges_copied, 16)
            sp.dma_start(sixteen(line(src_win)[0:EDGES]), sixteen(src)).then_inc(edges_copied, 16)
            sp.wait_ge(pads_set, 2)
            sp.dma_start(line(src_win)[EDGES:].unsqueeze(0), pad_src[0:1, :]).then_inc(pads_written, 16)
            sp.dma_start(line(dst_win)[EDGES:].unsqueeze(0), pad_dst[0:1, :]).then_inc(pads_written, 16)

            agg_tiles = agg.rearrange("p (t d) -> p t d", t=TILES)

            def x_load(c):
                t0, t1 = c * CHUNK, min((c + 1) * CHUNK, TILES - 1)
                sp.dma_start(agg_tiles[:, t0:t1, :],
                             x[t0 * P:t1 * P, :].rearrange("(t p) d -> p t d", p=P)).then_inc(x_landed[c], 16)

            EARLY = 3
            for c in range(EARLY):
                x_load(c)
            sp.wait_ge(edges_copied, 32)
            sp.wait_ge(pads_written, 32)
            sp.dma_start(ends[0:WPARTS, :, :], dst_win.rearrange("(p c) e -> p c e", c=WSLOTS)).then_inc(ends_in, 16)
            for c in range(EARLY, CHUNKS):
                x_load(c)
            sp.wait_ge(tail_zeroed, 1)
            sp.dma_start(agg_tiles[0:TAIL, TILES - 1, :], x[(TILES - 1) * P:N, :]).then_inc(x_landed[CHUNKS - 1], 16)

            def x_here(c):
                sp.wait_ge(x_landed[c], 16 if c < CHUNKS - 1 else 32)
                sp.sem_inc(x_ready, 1)

            def pairs_store(c):
                sp.wait_ge(lo_done, c + 1)
                sp.dma_start(xn_pair[rows_of(c * CHUNK, CHUNK), :].rearrange("(t p) d -> p t d", p=P),
                             pairs_out[:, (c % 2) * (CHUNK * 2 * D):(c % 2 + 1) * (CHUNK * 2 * D)]
                             .rearrange("p (t d) -> p t d", t=CHUNK)).then_inc(pair_stored, 16)

            def pairs_here(c):
                sp.wait_ge(pair_stored, 16 * c + 16)
                sp.sem_inc(pair_free, 1)

            for c in range(EARLY + 1):
                x_here(c)
            for c in range(CHUNKS):
                if c:
                    pairs_here(c - 1)
                pairs_store(c)
                if c + EARLY + 1 < CHUNKS:
                    x_here(c + EARLY + 1)
                elif c + EARLY + 1 == CHUNKS:
                    sp.dma_start(wqkv_sb, weight_tiles(w_qkv)).then_inc(wqkv_landed, 16)
                    sp.dma_start(wproj_sb, weight_tiles(w_proj)).then_inc(wqkv_landed, 16)
            pairs_here(CHUNKS - 1)
            sp.wait_ge(edge_ready, 4)
            sp.dma_start(pair_in, xn_pair[0:P, :].rearrange("p (h d) -> p h d", h=2)).then_inc(pair_landed, 16)

            def gather_io(i):
                hold(xn_ready, i + 1)
                sp.dma_start(pair_in, xn_pair[rows_of((i + 1) % TILES), :].rearrange("p (h d) -> p h d", h=2)
                             ).then_inc(pair_landed, 16)
                sp.dma_start(slot_x[rows_of(i * 2, 2), :].rearrange("(t p) d -> p t d", p=P),
                             repeat(no_token[:, :], 2)).then_inc(zeros_stored, 16)
                hold(q_ready, i + 1)
                hold(k_ready, i + 2)
                hold(v_ready, i + 2)
                sp.dma_start(qkv_rows[rows_of(i), :], qkv_out.rearrange("p a d -> p (a d)")
                             ).then_inc(qkv_stored, 16)

            with sp.Fori(0, TILES - 1) as i:
                gather_io(i)
                hold(qkv_stored, i * 16 + 16)
                sp.sem_inc(qkv_free, 1)
            gather_io(TILES - 1)
            sp.wait_ge(v_done, TILES)
            sp.dma_start(w1_sb, weight_tiles(w1)).then_inc(w1_landed, 16)
            sp.wait_ge(seg_done, CREDIT_SEG + PAIRS)

            def kv_load(t, b):
                sp.dma_start(kv_in[b], qkv_rows[rows_of(t), D:3 * D].rearrange("p (a d) -> p a d", a=2)
                             ).then_inc(kv_landed[b], 16)

            def col(v, c):
                return v.rearrange("(c p) -> p c", c=c)

            def row(v):
                return v.unsqueeze(0).broadcast_to([P, v.shape[0]])

            for t in range(AHEAD):
                kv_load(t, t)
            sp.wait_ge(qkv_stored, 16 * TILES)
            sp.dma_start(qkv_rows[N:ROWS, D:2 * D], never[0:ROWS - N, :]).then_inc(never_stored, 16)
            with nc.allow_non_contiguous_dma(reason="bias columns, a few hundred words"):
                sp.dma_start(w2_sb, weight_tiles(w2)).then_inc(wgin_landed, 16)
                sp.dma_start(b1_col, col(b1, KC)).then_inc(wgin_landed, 16)
                sp.dma_start(b2_row, row(b2)).then_inc(wgin_landed, 16)
                sp.wait_ge(never_stored, 16)
                sp.wait_ge(k_max_turned, 1)
                loads = [(wr_sb[:, :, 0:E], weight_tiles(wr_sp)), (wr_sb[:, :, E:EE], weight_tiles(wr_fq)),
                         (bproj_row, row(b_proj)), (br_row[:, 0:E], row(br_sp)), (br_row[:, E:EE], row(br_fq)),
                         (ws1_sb, weight_tiles(ws1)), (ws2_sb, weight_tiles(ws2)), (bs1_col, col(bs1, FC)),
                         (bs2_row, row(bs2)),
                         (q_in, qkv_rows[0:P, 0:D])]
                assert len(loads) == WMIX
                for to, of in loads:
                    sp.dma_start(to, of).then_inc(wmix_landed, 16)
            with sp.Fori(0, (TILES - 1) // AHEAD - 1) as g:
                for k in range(AHEAD):
                    hold(kv_used, g * AHEAD + (k + 1))
                    kv_load(g * AHEAD + (AHEAD + k), k)
            sp.wait_ge(kv_used, TILES - AHEAD)
            kv_load(TILES - 1, 0)

            def mix_load(t, last=False):
                if not isinstance(t, int) or t > 0:
                    hold(q_turned, t)
                    sp.dma_start(q_in, qkv_rows[rows_of(t), 0:D]).then_inc(q_landed, 16)
                hold(xb_ready, t)
                if last:
                    sp.dma_start(x_in[0:TAIL, :], x[(TILES - 1) * P:N, :]).then_inc(xr_landed, 16)
                else:
                    sp.dma_start(x_in, x[rows_of(t), :]).then_inc(xr_landed, 16)

            mix_load(0)
            with sp.Fori(1, SLOT_TILES - 2 * TILES + 1) as t:
                mix_load(t)
                sp.dma_start(slot_x[rows_of(t + (2 * TILES - 1)), :], no_token[:, :]).then_inc(zeros_stored, 16)
            with sp.Fori(SLOT_TILES - 2 * TILES + 1, TILES - 1) as t:
                mix_load(t)
            mix_load(TILES - 1, last=True)

            sp.wait_ge(routed, 1)
            for b, v in enumerate((b1_sp, b1_fq)):
                sp.dma_start(b1_all[:, b * E * FF:(b + 1) * E * FF], row(v.rearrange("e f -> (e f)"))
                             ).then_inc(b1_landed, 16)

            def base_store(t):
                hold(base_ready, t + 1)
                sp.dma_start(base_rows[rows_of(t), :], agg_tile(t)).then_inc(base_stored, 16)

            def weights_load(b, e):
                wa, wb = ((w1_sp, w2_sp), (w1_fq, w2_fq))[b]
                at = e * EXPERT_W + b * (E * EXPERT_W)
                sp.dma_start(arena[:, bass.ds(at, KC * FF)].rearrange("p (c n) -> p c n", c=KC),
                             wa[bass.ds(e, 1)].rearrange("a (c p) n -> p (a c) n", p=P)).then_inc(we_landed, 16)
                sp.dma_start(arena[:, bass.ds(at + KC * FF, FC * D)].rearrange("p (c n) -> p c n", c=FC),
                             wb[bass.ds(e, 1)].rearrange("a (c p) n -> p (a c) n", p=P)).then_inc(we_landed, 16)

            over = EXPERT_W // D
            with sp.Fori(0, E) as e:
                for k in range(over):
                    base_store(e * over + k)
                hold(base_stored, e * (16 * over) + 16 * over)
                weights_load(0, e)
            with sp.Fori(E * over, TILES) as t:
                base_store(t)
            sp.wait_ge(base_stored, 16 * TILES)
            for k in range(STAGES):
                sp.wait_ge(scattered[k], SCATTERED[k])

            def slot_load(j, k):
                sp.dma_start(sx[k], slot_x[rows_of(j), :]).then_inc(sx_landed[k], 16)

            def turn_of_slots(g):
                for k in range(UNROLL):
                    j = g * UNROLL + k
                    hold(token_ready, j * 2 + 2)
                    slot_load(j + UNROLL, k)

            for k in range(UNROLL):
                slot_load(k, k)
            sp.dma_start(b2_all[0], row(b2_sp.rearrange("e d -> (e d)"))).then_inc(b2_landed, 16)
            with sp.Fori(0, E) as e:
                weights_load(1, e)
                turn_of_slots(e)
            with sp.Fori(E, BANK_TURNS) as g:
                turn_of_slots(g)
            sp.wait_ge(e_down, BANK_TILES)
            sp.dma_start(b2_all[1], row(b2_fq.rearrange("e d -> (e d)"))).then_inc(b2_landed, 16)
            with sp.Fori(BANK_TURNS, BANKS * BANK_TURNS - 1) as g:
                turn_of_slots(g)
            for s in y_scattered:
                sp.wait_ge(s, Y_FROM + 8 * SLOT_TILES)

        @block.gpsimd
        def _(pool):
            made = Steps(pool, consts)
            made.done(pool.memset(ident[:, :], 0.0))
            made.done(pool.memset(ones16[:, :], 1.0))
            made.wait()
            made.done(pool.affine_select(out=ident[:, :], in_=ident[:, :], compare_op=ALU.not_equal, fill=1.0,
                                         base=0, pattern=[[-1, P]], channel_multiplier=1))
            made.done(pool.affine_select(out=prefix16[:, :], in_=ones16[:, :], compare_op=ALU.is_ge, fill=0.0,
                                         base=0, pattern=[[1, P]], channel_multiplier=-1))
            made.done(pool.memset(ones32[:, :], 1.0))
            made.done(pool.iota(count[:, :], [[1, P]], base=0, channel_multiplier=0,
                                allow_small_or_imprecise_dtypes=True))
            made.done(pool.iota(pair_no[:, :], [[P, SETS]], base=0, channel_multiplier=1,
                                allow_small_or_imprecise_dtypes=True))
            made.done(pool.iota(node16[:, :], [[1, P]], base=0, channel_multiplier=0,
                                allow_small_or_imprecise_dtypes=True))
            made.done(pool.memset(eps[:, :], EPS))
            made.done(pool.memset(minus_half[:, :], -0.5))
            made.done(pool.memset(zero16[:, :], 0.0))
            made.done(pool.memset(no_token[:, 0:D], 0.0))
            made.done(pool.memset(no_token[:, D:D + 1], float(NO_ROW)))
            made.done(pool.memset(no_token[:, D + 1:ROW], 0.0))
            made.done(pool.memset(never, NEVER))
            assert made.count == CONSTS
            last_node = pool.to_reg(N - 1)
            last_window = pool.to_reg(WROWS - 1)
            last_slot = pool.to_reg(SLOT_TILES * P - 1)
            last_row = pool.to_reg(ROWS - 1)

            def low(c):
                pool.wait_ge(hi_done, c + 1)
                pool.sem_inc(pool_mark, 1)
                pair = pairs_out[:, bass.ds((c % 2) * (CHUNK * 2 * D), CHUNK * 2 * D)] \
                    .rearrange("p (t h d) -> p t h d", t=CHUNK, h=2)
                pool.tensor_tensor(pair[:, :, 1, :],
                                   agg[:, bass.ds(c * (CHUNK * D), CHUNK * D)].rearrange("p (t d) -> p t d", t=CHUNK),
                                   pair[:, :, 0, :], ALU.subtract).then_inc(lo_done, 1)

            with pool.Fori(0, CHUNKS // 2) as c:
                low(c)
            pool.wait_ge(ends_in, 16)
            pool.wait_ge(plan_own, PLAN_KNOWN)
            for j in range(SETS):
                for to, of in ((win_src, src_win), (win_dst, dst_win)):
                    pool.indirect_dma_start(out=to[:, j, :], out_offset=None, in_=of[:, :],
                                            in_offset=bass.IndirectOffsetOnAxis(ap=win_idx[:, j:j + 1], axis=0),
                                            bounds_check=last_window, oob_is_err=False).then_inc(win_in, 16)
            with pool.Fori(CHUNKS // 2, CHUNKS) as c:
                low(c)
            pool.wait_ge(edge_ready, 4)
            pool.wait_ge(pair_stored, 16 * CHUNKS)
            with pool.Fori(0, TILES) as i:
                for third in range(PER // PBANKS):
                    g0 = third * PBANKS
                    pool.wait_ge(src_copied, i * (PER // PBANKS) + (third + 1))
                    pool.sem_inc(pool_mark, 1)
                    for s in range(2 * g0, 2 * (g0 + PBANKS)):
                        pool.indirect_dma_start(out=rows[:, s, :], out_offset=None, in_=xn_pair[:, :],
                                                in_offset=bass.IndirectOffsetOnAxis(ap=src_now[:, s:s + 1], axis=0),
                                                bounds_check=last_node, oob_is_err=False).then_inc(row_in[s], 16)

            pool.wait_ge(wmix_landed, 16 * WMIX)

            def x_and_bias(t):
                pool.wait_ge(xr_landed, t * 16 + 16)
                wait_from(pool, xa_done, t)
                pool.sem_inc(pool_mark, 1)
                pool.tensor_tensor(x_b, x_in, bproj_row, ALU.add).then_inc(xb_ready, 1)
                pool.wait_ge(var_ready, t + 1)
                pool.sem_inc(pool_mark, 1)
                pool.tensor_tensor(rs_all[:, bass.ds(t, 1)], var2, minus_half[:, :], ALU.pow).then_inc(rs_ready, 1)

            x_and_bias(0)
            with pool.Fori(1, TILES) as t:
                x_and_bias(t)

            pool.wait_ge(zeros_stored, 16 * (SLOT_TILES - TILES))
            def add_bias(t):
                pool.wait_ge(shared_added, t + 1)
                pool.sem_inc(pool_mark, 1)
                pool.tensor_tensor(agg_tile(t), agg_tile(t), bs2_row, ALU.add).then_inc(base_ready, 1)

            def scatter(t, k, _):
                pool.wait_ge(staged, t * 3 + 3)
                pool.sem_inc(pool_mark, 1)
                for b in range(BANKS):
                    pool.indirect_dma_start(
                        out=slot_x[:, :],
                        out_offset=bass.IndirectOffsetOnAxis(ap=slot_now[:, 2 * k + b:2 * k + b + 1], axis=0),
                        in_=stage[k], in_offset=None, bounds_check=last_slot, oob_is_err=False
                    ).then_inc(scattered[k], 16)
                if not isinstance(t, int) or t >= 3:
                    add_bias(t - 3)

            each_stage(pool, scatter)
            for t in range(TILES - 3, TILES):
                add_bias(t)

            for s, n in zip(scattered, SCATTERED):
                pool.wait_ge(s, n)
            pool.wait_ge(base_stored, 16 * TILES)
            pool.wait_ge(o_set, 1)

            def tokens_in(g, k, of):
                pool.wait_ge(token_ready, g * (2 * UNROLL) + (2 * k + 2))
                pool.wait_ge(e_out, g * UNROLL + (k + 1))
                pool.sem_inc(pool_mark, 1)
                pool.indirect_dma_start(out=o_in[k % 2], out_offset=None, in_=of[:, :],
                                        in_offset=bass.IndirectOffsetOnAxis(ap=token_now[k], axis=0),
                                        bounds_check=last_row, oob_is_err=False).then_inc(o_landed[k % 2], 16)

            def tokens_out(g, k, to, last):
                pool.wait_ge(e_out, g * UNROLL + (k + CREDIT_O + 1))
                pool.sem_inc(pool_mark, 1)
                pool.indirect_dma_start(out=to[:, :], out_offset=bass.IndirectOffsetOnAxis(ap=token_now[k], axis=0),
                                        in_=ye[k % 2], in_offset=None,
                                        bounds_check=last, oob_is_err=False).then_inc(y_scattered[k % 2], 16)

            for b, (of, to, last) in enumerate(((base_rows, half_rows, last_row), (half_rows, out, last_node))):
                g0 = b * BANK_TURNS
                if b:
                    for s in y_scattered:
                        pool.wait_ge(s, Y_FROM + 8 * BANK_TILES)
                tokens_in(g0, 0, of)
                for k in range(1, UNROLL):
                    tokens_in(g0, k, of)
                    tokens_out(g0, k - 1, to, last)
                with pool.Fori(g0 + 1, g0 + BANK_TURNS) as g:
                    tokens_in(g, 0, of)
                    tokens_out(g - 1, UNROLL - 1, to, last)
                    for k in range(1, UNROLL):
                        tokens_in(g, k, of)
                        tokens_out(g, k - 1, to, last)
                tokens_out(g0 + BANK_TURNS - 1, UNROLL - 1, to, last)

        @block.scalar
        def _(act):
            def copy(to, of, **kw):
                return act.activation(to, of, ACT.Copy, **kw)

            act.wait_ge(consts, CONSTS)
            with act.Fori(0, CHUNKS) as c:
                act.wait_ge(bn_own, c * (2 * CHUNK) + 2 * CHUNK)
                act.activation(std[:, :], moments[:, :, 1], ACT.Sqrt, bias=eps[:, 0:1]).then_inc(std_done, 1)
                act.wait_ge(xn_done, c * CHUNK + CHUNK)
                act.wait_ge(pair_free, c + 1)
                act.sem_inc(act_mark, 1)
                pair = pairs_out[:, bass.ds((c % 2) * (CHUNK * 2 * D), CHUNK * 2 * D)] \
                    .rearrange("p (t h d) -> p t h d", t=CHUNK, h=2)
                copy(pair[:, :, 0, :], agg[:, bass.ds(c * (CHUNK * D), CHUNK * D)]
                     .rearrange("p (t d) -> p t d", t=CHUNK)).then_inc(hi_done, 1)

            act.wait_ge(edge_turned, 4)
            for h in range(2):
                copy(edge_src[:, :, h], bank[4 + h][:, :]).then_inc(edge_ready, 1)

            def indices(i, third, summed):
                g0 = third * PBANKS
                act.wait_ge(seg_done, summed)
                act.sem_inc(act_mark, 1)
                copy(src_now[:, 2 * g0:2 * (g0 + PBANKS)],
                     edge_src[:, bass.ds(i * PER + g0, PBANKS), :].rearrange("p g h -> p (g h)")
                     ).then_inc(src_copied, 1)

            act.wait_ge(edge_ready, 4)
            for third in range(PER // PBANKS):
                indices(0, third, PBANKS * (third + 1))
            with act.Fori(0, TILES) as i:
                act.wait_ge(xn_turned, i + 1)
                copy(xn_t.rearrange("p a b -> p (a b)"), bank[0][:, :]).then_inc(xn_t_ready, 1)
                indices(i + 1, 0, i * PER + (CREDIT_SEG + PBANKS))
                act.wait_ge(q_less, i + 2)
                act.activation(qkv_out[:, 0, :], qkv_out[:, 0, :], ACT.Exp).then_inc(q_exp, 1)
                indices(i + 1, 1, i * PER + (CREDIT_SEG + 2 * PBANKS))
                act.wait_ge(k_less, i + 1)
                act.activation(qkv_out[:, 1, :], qkv_out[:, 1, :], ACT.Exp).then_inc(k_exp, 1)
                indices(i + 1, 2, i * PER + (CREDIT_SEG + 3 * PBANKS))
                act.wait_ge(v_done, i + 1)
                act.wait_ge(qkv_free, i + 1)
                copy(qkv_out[:, 2, :], bank[3][:, :]).then_inc(v_ready, 1)

            act.wait_ge(seg_added, CREDIT_BANK + PAIRS)

            def hidden(t):
                wait_from(act, h_turned, t)
                act.sem_inc(act_mark, 1)
                copy(h_now, agg_tile(t)).then_inc(h_ready, 1)

            def relu(t):
                act.wait_ge(up_done, t + 1)
                act.wait_ge(gin_done, t + 1)
                for m in range(KC):
                    act.activation(h1_t[:, m, :], bank[1][:, m * P:(m + 1) * P], ACT.Relu,
                                   bias=b1_col[:, m:m + 1]).then_inc(up_act, 1)

            def turned_hidden(t):
                act.wait_ge(h_turned, t + 1)
                wait_from(act, up_done, t)
                copy(h_t.rearrange("p a b -> p (a b)"), bank[0][:, :]).then_inc(h_t_ready, 1)

            def k_exponent(t, b):
                act.wait_ge(k_shifted, t + 1)
                act.activation(kv_in[b][:, 0, :], kv_in[b][:, 0, :], ACT.Exp).then_inc(k_expd, 1)

            hidden(0)
            turned_hidden(0)
            k_exponent(0, 0)
            act.wait_ge(wgin_landed, 16 * WGIN)
            with act.Fori(0, (TILES - 1) // AHEAD) as g:
                for k in range(AHEAD):
                    t = g * AHEAD + (k + 1)
                    hidden(t)
                    relu(g * AHEAD + k)
                    turned_hidden(t)
                    k_exponent(t, (k + 1) % AHEAD)
            relu(TILES - 1)
            act.wait_ge(ctx_own, CTX_STEPS)
            act.wait_ge(mixw_done, KC)
            for hp in range(KC):
                copy(mix_w[:, hp, :], bank[4 + hp][:, :], scale=k_sum[:, hp:hp + 1]).then_inc(mixw_ready, 1)

            def turned_q(t):
                act.wait_ge(q_turned, t + 1)
                wait_from(act, att_done, t)
                copy(q_t.rearrange("p a b -> p (a b)"), bank[0][:, :]).then_inc(q_t_ready, 1)

            def turned_xm(t):
                act.wait_ge(xm_turned, t + 1)
                wait_from(act, lg_done, t)
                copy(xm_t.rearrange("p a b -> p (a b)"), bank[5][:, :]).then_inc(xm_t_ready, 1)

            def mixed(t):
                turned_q(t)
                turned_xm(t - 2)

            turned_q(0)
            turned_q(1)
            mixed(2)
            with act.Fori(3, TILES) as t:
                mixed(t)
            turned_xm(TILES - 2)
            turned_xm(TILES - 1)

            act.wait_ge(route_own, ROUTE_LESS)
            act.activation(expo, less, ACT.Exp).then_inc(expo_done, 1)

            act.wait_ge(wmix_landed, 16 * WMIX)
            act.wait_ge(lg_done, TILES)

            def shared_gelu(t, p):
                act.wait_ge(sh_up, t + 1)
                if not isinstance(t, int) or t >= 2:
                    act.wait_ge(sh_down, t - 1)
                for m in range(FC):
                    act.activation(hs_t[p][:, m, :], bank[SHARED_UP[p]][:, m * P:(m + 1) * P], ACT.Gelu,
                                   bias=bs1_col[:, m:m + 1]).then_inc(sh_act, 1)

            def shared(t, k, _):
                if not isinstance(t, int) or t >= 1:
                    shared_gelu(t - 1, (k + 1) % 2)
                act.wait_ge(xm_turned, t + (TILES + 1))
                wait_from(act, sh_up, t)
                copy(xm_t.rearrange("p a b -> p (a b)"), bank[5][:, :]).then_inc(xm_t_ready, 1)

            each_stage(act, shared)
            shared_gelu(TILES - 1, (TILES - 1) % 2)

            def turn_slot(j, k):
                act.wait_ge(sx_turned, j + 1)
                copy(sx_t[k % 2].rearrange("p a b -> p (a b)"), bank[k % 2][:, :]).then_inc(sx_t_ready, 1)

            def expert_gelu(j, k):
                act.wait_ge(e_biased, j + 1)
                act.activation(he[k % 2], he[k % 2], ACT.Gelu).then_inc(e_act, 1)

            def tokens(g, k):
                act.wait_ge(y_scattered[k % 2], g * (8 * UNROLL) + (Y_FROM + 16 * (k // 2 - 1)))
                act.sem_inc(act_mark, 1)
                copy(token_now[k], sx[k][:, D:D + 1]).then_inc(token_ready, 1)
                copy(gate_now[k], sx[k][:, D + 1 + bank_now:D + 2 + bank_now]).then_inc(token_ready, 1)

            def filled(g, k):
                expert_gelu(g * UNROLL + (k - 1), k + 1)
                turn_slot(g * UNROLL + k, k)
                tokens(g, k)

            for bank_now in range(BANKS):
                g0 = bank_now * BANK_TURNS
                if bank_now == 0:
                    turn_slot(0, 0)
                    tokens(0, 0)
                    for k in range(1, UNROLL):
                        filled(0, k)
                    g0 = 1
                with act.Fori(g0, (bank_now + 1) * BANK_TURNS) as g:
                    for k in range(UNROLL):
                        filled(g, k)
            expert_gelu(SLOT_TILES - 1, 1)

        @block.tensor
        def _(pe):
            def turn(to, tile, n=KC):
                for c in range(n):
                    last = pe.transpose(to[:, c * P:(c + 1) * P], tile[:, c * P:(c + 1) * P], ident[:, :])
                return last

            def product(to, stationary, moving):
                for c, (s, m) in enumerate(zip(stationary, moving)):
                    last = pe.matmul(to, s, m, start=c == 0, stop=c == len(stationary) - 1)
                return last

            pe.wait_ge(consts, CONSTS)
            pe.wait_ge(plan_own, PLAN_TOUCH)
            pe.matmul(bank[0][:, 0:2 * WSLOTS * TILES], ones32[0:WPARTS, :],
                      touch[0:WPARTS].rearrange("p a w n -> p (a w n)"), start=True, stop=True).then_inc(touch_summed, 1)
            pe.wait_ge(plan_own, PLAN_KNOWN)
            for j in range(SETS):
                last = pe.matmul(bank[1][0:1, j * P:(j + 1) * P], agg_off[:, j:j + 1], ident[:, :],
                                 start=True, stop=True)
            last.then_inc(at_summed, 1)
            pe.wait_ge(plan_own, PLAN_STEPS)
            for n, of in enumerate((local, off_tile)):
                for h in range(2):
                    for j in range(SETS):
                        last = pe.transpose(bank[2 + 2 * n + h][:, j * P:(j + 1) * P],
                                            of[:, j, h * P:(h + 1) * P], ident[:, :])
                    last.then_inc(edge_turned, 1)

            pe.wait_ge(wqkv_landed, 32)
            pe.wait_ge(edge_ready, 4)
            with pe.Fori(0, TILES) as i:
                def segment(u):
                    for h in range(2):
                        pe.wait_ge(row_in[2 * u + h], i * 16 + 16)
                    pe.wait_ge(pick_ready, i * PER + (u + 1))
                    pe.wait_ge(seg_added, i * PER + (u + 1))
                    to = bank[4 + u % PBANKS][:, :]
                    for h in range(2):
                        for half in range(2):
                            last = pe.matmul(to, pick[:, u, h, :], rows[:, 2 * u + h, half * D:(half + 1) * D],
                                             start=h + half == 0, stop=h + half == 2)
                    last.then_inc(seg_done, 1)

                pe.wait_ge(xn_ready, i + 1)
                turn(bank[0], xn_tile).then_inc(xn_turned, 1)
                for n, (free, done) in enumerate(((q_less, q_done), (k_ready, k_done), (v_ready, v_done))):
                    for u in range(n * PBANKS, (n + 1) * PBANKS):
                        segment(u)
                    if n == 0:
                        pe.wait_ge(xn_t_ready, i + 1)
                    pe.wait_ge(free, i + 1)
                    product(bank[1 + n][:, :], [xn_t[:, c, :] for c in range(KC)],
                            [wqkv_sb[:, c, n * D:(n + 1) * D] for c in range(KC)]).then_inc(done, 1)

            pe.wait_ge(k_max_done, TILES + 1)
            turn(bank[0], k_max).then_inc(k_max_turned, 1)
            pe.wait_ge(top_own, 1 + KC)
            for c in range(KC):
                last = pe.matmul(bank[1][:, c * P:(c + 1) * P], ones32[:, :], top_diag[:, c, :], start=True, stop=True)
            last.then_inc(top_spread, 1)
            pe.wait_ge(v_ready, TILES + 1)
            for b in (2, 3):
                pe.matmul(bank[b][:, :], zero16[:, 0:P], zero16[:, :], start=True, stop=True)
            def context(t, b):
                pe.wait_ge(k_expd, t + 1)
                for hp in range(KC):
                    cols = slice(hp * P, (hp + 1) * P)
                    ek, v = kv_in[b][:, 0, cols], kv_in[b][:, 1, cols]
                    pe.matmul(bank[2][:, cols], v, ek, start=False, stop=True, skip_group_check=True)
                    last = pe.matmul(bank[3][:, hp:hp + 1], ek, ones32[:, 0:1], start=False, stop=True,
                                     skip_group_check=True)
                last.then_inc(kv_used, 1)

            def turn_h(t):
                pe.wait_ge(h_ready, t + 1)
                wait_from(pe, h_t_ready, t)
                turn(bank[0], h_now).then_inc(h_turned, 1)

            def gin_up(t):
                pe.wait_ge(h_t_ready, t + 1)
                wait_from(pe, up_act, t * KC)
                for m in range(KC):
                    last = product(bank[1][:, m * P:(m + 1) * P], [w1_sb[:, c, m * P:(m + 1) * P] for c in range(KC)],
                                   [h_t[:, c, :] for c in range(KC)])
                last.then_inc(up_done, 1)

            def gin_down(t):
                pe.wait_ge(up_act, t * KC + KC)
                pe.wait_ge(gin_kept, t + 1)
                product(bank[4][:, :], [h1_t[:, c, :] for c in range(KC)],
                        [w2_sb[:, c, :] for c in range(KC)]).then_inc(gin_done, 1)

            pe.wait_ge(k_top_ready, 1)
            turn_h(0)
            pe.wait_ge(w1_landed, 16)
            gin_up(0)
            context(0, 0)
            pe.wait_ge(wgin_landed, 16 * WGIN)
            with pe.Fori(0, (TILES - 1) // AHEAD) as g:
                for k in range(AHEAD):
                    t = g * AHEAD + (k + 1)
                    turn_h(t)
                    gin_down(g * AHEAD + k)
                    gin_up(t)
                    context(t, (k + 1) % AHEAD)
            gin_down(TILES - 1)
            pe.wait_ge(ctx_own, CTX_STEPS)
            pe.wait_ge(gin_kept, TILES + 1)
            for hp in range(KC):
                pe.matmul(bank[4 + hp][:, :], ctx_t[:, hp, :], wproj_sb[:, hp, :],
                          start=True, stop=True).then_inc(mixw_done, 1)

            pe.wait_ge(wmix_landed, 16 * WMIX)
            pe.wait_ge(mixw_ready, KC)

            def turn_q(t):
                wait_from(pe, q_landed, t * 16)
                wait_from(pe, q_t_ready, t)
                turn(bank[0], q_in).then_inc(q_turned, 1)

            def attention(t):
                pe.wait_ge(q_t_ready, t + 1)
                wait_from(pe, xa_done, t)
                product(bank[3][:, :], [q_t[:, c, :] for c in range(KC)],
                        [mix_w[:, c, :] for c in range(KC)]).then_inc(att_done, 1)

            def turn_xm(t):
                pe.wait_ge(xm_ready, t + 1)
                wait_from(pe, xm_t_ready, t)
                turn(bank[5], xm_now).then_inc(xm_turned, 1)

            def router(t):
                pe.wait_ge(xm_t_ready, t + 1)
                wait_from(pe, lg_ready, t)
                product(bank[6][:, 0:EE], [xm_t[:, c, :] for c in range(KC)],
                        [wr_sb[:, c, :] for c in range(KC)]).then_inc(lg_done, 1)

            def mixed(t):
                turn_q(t)
                if not isinstance(t, int) or t >= 3:
                    router(t - 3)
                if not isinstance(t, int) or t >= 2:
                    turn_xm(t - 2)
                attention(t)

            for t in range(4):
                mixed(t)
            with pe.Fori(4, TILES) as t:
                mixed(t)
            router(TILES - 3)
            for t in (TILES - 2, TILES - 1):
                turn_xm(t)
                router(t)

            pe.wait_ge(route_own, ROUTE_HOT)
            half = TILES * EE // 2
            for n, by in enumerate((prefix16, ones16)):
                for h in range(2):
                    pe.matmul(bank[2 * n + h][:, 0:half], by[:, :], hot16[:, h * half:(h + 1) * half],
                              start=True, stop=True).then_inc(hot_summed, 1)

            pe.wait_ge(counts_read, 2)

            def shared_down(t, p):
                pe.wait_ge(sh_act, t * FC + FC)
                wait_from(pe, shared_added, t)
                product(bank[7][:, :], [hs_t[p][:, m, :] for m in range(FC)],
                        [ws2_sb[:, m, :] for m in range(FC)]).then_inc(sh_down, 1)

            def shared(t, k, _):
                pe.wait_ge(staged, t * 3 + 3)
                pe.wait_ge(xm_t_ready, t + TILES)
                turn(bank[5], stage[k][:, 0:D]).then_inc(xm_turned, 1)
                if not isinstance(t, int) or t >= 2:
                    shared_down(t - 2, k % 2)
                pe.wait_ge(xm_t_ready, t + (TILES + 1))
                for m in range(FC):
                    last = product(bank[SHARED_UP[k % 2]][:, m * P:(m + 1) * P],
                                   [ws1_sb[:, n, m * P:(m + 1) * P] for n in range(KC)],
                                   [xm_t[:, n, :] for n in range(KC)])
                last.then_inc(sh_up, 1)

            each_stage(pe, shared)
            for t in (TILES - 2, TILES - 1):
                shared_down(t, t % 2)

            pe.wait_ge(we_landed, 16 * 2 * E)
            pe.wait_ge(routed, 1)

            def turn_slot(j, k, landed):
                pe.wait_ge(sx_landed[k % UNROLL], landed)
                turn(bank[k % 2], sx[k % UNROLL][:, 0:D]).then_inc(sx_turned, 1)

            def weights(j):
                return pe.value_load(weight_at[0:1, bass.ds(j, 1)], min_val=0, max_val=(EE - 1) * EXPERT_W)

            def expert_up(j, k):
                at = weights(j)
                pe.wait_ge(sx_t_ready, j + 1)
                product(bank[2 + k % 2][:, 0:FF], [sx_t[k % 2][:, c, :] for c in range(KC)],
                        [arena[:, bass.ds(at + c * FF, FF)] for c in range(KC)]).then_inc(e_up, 1)

            def turn_hidden(j, k):
                pe.wait_ge(e_act, j + 1)
                turn(bank[4 + k % 2], he[k % 2], FC).then_inc(e_turned, 1)

            def expert_down(j, k):
                at = weights(j)
                pe.wait_ge(he_t_ready, j + 1)
                product(bank[6 + k % 2][:, :], [he_t[k % 2][:, m, :] for m in range(FC)],
                        [arena[:, bass.ds(at + (KC * FF + m * D), D)] for m in range(FC)]).then_inc(e_down, 1)

            def filled(g, k, last=False):
                j = g * UNROLL + k
                turn_hidden(j - 1, k + 1)
                expert_up(j, k)
                if not last:
                    turn_slot(j + 1, k + 1, g * 16 + 16 * (1 + (k + 1) // UNROLL))
                expert_down(j - 1, k + 1)

            turn_slot(0, 0, 16)
            expert_up(0, 0)
            turn_slot(1, 1, 16)
            for k in range(1, UNROLL):
                filled(0, k)
            with pe.Fori(1, BANK_TURNS) as g:
                for k in range(UNROLL):
                    filled(g, k)
            pe.wait_ge(we_landed, 16 * 2 * EE)
            with pe.Fori(BANK_TURNS, BANKS * BANK_TURNS - 1) as g:
                for k in range(UNROLL):
                    filled(g, k)
            for k in range(UNROLL):
                filled(BANKS * BANK_TURNS - 1, k, last=k == UNROLL - 1)
            turn_hidden(SLOT_TILES - 1, 1)
            expert_down(SLOT_TILES - 1, 1)

        @block.vector
        def _(dve):
            dve.memset(pad_src, 0).then_inc(pads_set, 1)
            dve.memset(pad_dst, NO_NODE).then_inc(pads_set, 1)
            dve.memset(agg[:, (TILES - 1) * D:], 0.0).then_inc(tail_zeroed, 1)
            dve.sem_inc(pair_free, CREDIT_PAIR)
            dve.sem_inc(seg_added, CREDIT_BANK)
            for s in (q_less, k_ready, v_ready, qkv_free, gin_done, gin_kept):
                dve.sem_inc(s, 1)
            dve.sem_inc(e_out, CREDIT_O)

            def normed(c):
                dve.wait_ge(x_ready, c + 1)
                dve.sem_inc(dve_mark, 1)
                for k in range(CHUNK):
                    dve.bn_stats(stats6[:, k, :], agg_tile(c * CHUNK + k)).then_inc(bn_own, 1)
                dve.wait_ge(bn_own, c * (2 * CHUNK) + CHUNK)
                dve.sem_inc(dve_mark, 1)
                for k in range(CHUNK):
                    dve.bn_aggr(moments[:, k, :], stats6[:, k, :]).then_inc(bn_own, 1)
                dve.wait_ge(std_done, c + 1)
                dve.reciprocal(rstd[:, :], std[:, :]).then_inc(rstd_done, 1)
                dve.wait_ge(rstd_done, c + 1)
                for k in range(CHUNK):
                    dve.tensor_scalar(agg_tile(c * CHUNK + k), agg_tile(c * CHUNK + k), moments[:, k, 0:1],
                                      rstd[:, k:k + 1], ALU.subtract, ALU.mult).then_inc(xn_done, 1)
                dve.wait_ge(xn_done, c * CHUNK + CHUNK)
                dve.sem_inc(dve_mark, 1)

            with dve.Fori(0, 2) as c:
                normed(c)

            plan = Steps(dve, plan_own)
            dve.wait_ge(consts, CONSTS)
            plan.done(dve.tensor_scalar(bounds[:, 0, :], count[:, 0:TILES], float(P), None, ALU.mult))
            plan.then(dve.tensor_scalar(bounds[:, 1, :], count[:, 0:TILES], float(P), float(P), ALU.mult, ALU.add))
            dve.wait_ge(ends_in, 16)
            for n, e in enumerate((WIN - 1, 0)):
                plan.done(dve.tensor_tensor(touch[0:WPARTS, n], spread(ends[0:WPARTS, :, e], TILES),
                                            repeat(bounds[0:WPARTS, n, :], WSLOTS), ALU.is_lt))
            assert plan.count == PLAN_TOUCH
            dve.wait_ge(touch_summed, 1)
            plan.then(dve.tensor_reduce(ab, bank[0][:, 0:2 * WSLOTS * TILES]
                                        .rearrange("p (a w n) -> p a n w", a=2, w=WSLOTS), X, ALU.add))
            plan.then(dve.tensor_tensor(pairs_of, ab[:, 1, :], ab[:, 0, :], ALU.subtract))
            plan.then(dve.tensor_scalar(pairs_of, pairs_of, 0.0, None, ALU.max))
            plan.then(dve.tensor_tensor_scan(pair_end, ones32[:, 0:TILES], pairs_of, 0.0, ALU.mult, ALU.add))
            plan.then(dve.tensor_tensor(shift, pairs_of, pair_end, ALU.subtract))
            plan.then(dve.tensor_tensor(shift, shift, ab[:, 0, :], ALU.add))
            plan.then(dve.tensor_tensor(cmp, repeat(pair_end, SETS), spread(pair_no[:, :], TILES), ALU.is_le))
            plan.then(dve.tensor_reduce(node_no, cmp, X, ALU.add))
            plan.then(dve.tensor_tensor(cmp, repeat(count[:, 0:TILES], SETS), spread(node_no, TILES), ALU.is_equal))
            plan.then(dve.tensor_tensor(cmp, cmp, repeat(shift, SETS), ALU.mult))
            plan.then(dve.tensor_reduce(win_no, cmp, X, ALU.add))
            plan.then(dve.tensor_tensor(win_no, win_no, pair_no[:, :], ALU.add))
            plan.done(dve.tensor_scalar(win_idx, win_no, float(WROWS - 1), None, ALU.min))
            plan.done(dve.tensor_scalar(minus_first, node_no, -float(P), None, ALU.mult))
            plan.then(dve.tensor_scalar(agg_off, node_no, float(TILES - 1), float(D), ALU.min, ALU.mult))
            assert plan.count == PLAN_KNOWN, plan.count
            dve.wait_ge(at_summed, 1)
            dve.tensor_copy(agg_at[0:1, :], bank[1][0:1, :]).then_inc(pads_set, 1)

            with dve.Fori(2, CHUNKS) as c:
                normed(c)

            dve.wait_ge(win_in, 16 * 2 * SETS)
            for j in range(SETS):
                plan.done(dve.tensor_scalar(local[:, j, :], win_dst[:, j, :], minus_first[:, j:j + 1], None, ALU.add))
            plan.wait()
            half = (P - 1) / 2
            plan.then(dve.tensor_scalar(off_tile, local, half, None, ALU.subtract))
            plan.then(dve.tensor_tensor(off_tile, off_tile, off_tile, ALU.mult))
            plan.then(dve.tensor_scalar(off_tile, off_tile, (half + 0.25) ** 2, float(NO_ROW), ALU.is_gt, ALU.mult))
            plan.then(dve.tensor_tensor(off_tile, off_tile, win_src, ALU.add))
            assert plan.count == PLAN_STEPS, plan.count
            dve.wait_ge(edge_turned, 4)
            for h in range(2):
                dve.tensor_copy(edge_node[:, :, h], bank[2 + h][:, :]).then_inc(edge_ready, 1)
            dve.wait_ge(edge_ready, 4)
            dve.wait_ge(pair_stored, 16 * CHUNKS)
            for third in range(PER // PBANKS):
                dve.memset(rows[:, 2 * PBANKS * third:2 * PBANKS * (third + 1), :].rearrange("p a b -> p (a b)"), 0.0
                           ).then_inc(soft_own, 1)
                dve.wait_ge(soft_own, third + 1)
                dve.sem_inc(seg_done, PBANKS)
            dve.memset(k_max, 0.0).then_inc(k_max_done, 1)

            def unpair():
                dve.tensor_tensor(xn_tile, pair_in[:, 0, :], pair_in[:, 1, :], ALU.add).then_inc(xn_ready, 1)

            def match(i, u):
                nodes = edge_node[:, bass.ds(i * PER + u, 1), :].rearrange("p a h -> p (a h)")
                dve.tensor_tensor(pick[:, u], repeat(node16[:, :], 2), spread(nodes, P), ALU.is_equal
                                  ).then_inc(pick_ready, 1)

            def add(i, u):
                at = dve.value_load(agg_at[0:1, bass.ds(i * PER + u, 1)], min_val=0, max_val=(TILES - 1) * D)
                dve.wait_ge(seg_done, i * PER + (CREDIT_SEG + u + 1))
                dve.wait_ge(seg_added, i * PER + (CREDIT_BANK + u))
                to = agg[:, bass.ds(at, D)]
                dve.tensor_tensor(to, bank[4 + u % PBANKS][:, :], to, ALU.add).then_inc(seg_added, 1)

            q3 = qkv_out[:, 0, :].rearrange("p (h d) -> p h d", h=HEADS)
            dve.wait_ge(pads_set, 3)
            dve.wait_ge(pair_landed, 16)
            unpair()
            for u in range(PER):
                match(0, u)
            with dve.Fori(0, TILES) as i:
                def pairs(us):
                    for u in us:
                        add(i, u)
                    for u in us:
                        match(i + 1, u)

                pairs(range(0, 3))
                dve.wait_ge(q_done, i + 1)
                dve.wait_ge(qkv_free, i + 1)
                dve.tensor_reduce(head[:, 0, :], bank[1][:, :].rearrange("p (h d) -> p h d", h=HEADS), X, ALU.max
                                  ).then_inc(soft_own, 1)
                dve.wait_ge(soft_own, i * 3 + 4)
                dve.tensor_tensor(q3, bank[1][:, :].rearrange("p (h d) -> p h d", h=HEADS), spread(head[:, 0, :], HD),
                                  ALU.subtract).then_inc(q_less, 1)
                pairs(range(3, 6))
                dve.wait_ge(q_exp, i + 1)
                dve.tensor_reduce(head[:, 1, :], q3, X, ALU.add).then_inc(soft_own, 1)
                dve.wait_ge(k_done, i + 1)
                dve.tensor_scalar(qkv_out[:, 1, :], bank[2][:, :], 0.0, None, ALU.min).then_inc(k_less, 1)
                dve.wait_ge(soft_own, i * 3 + 5)
                dve.reciprocal(head[:, 2, :], head[:, 1, :]).then_inc(soft_own, 1)
                dve.wait_ge(soft_own, i * 3 + 6)
                dve.tensor_tensor(q3, q3, spread(head[:, 2, :], HD), ALU.mult).then_inc(q_ready, 1)
                dve.wait_ge(pair_landed, i * 16 + 32)
                dve.wait_ge(xn_turned, i + 1)
                unpair()
                pairs(range(6, PER))
                dve.wait_ge(k_exp, i + 1)
                dve.scalar_tensor_tensor(out=qkv_out[:, 1, :], in0=bank[2][:, :], scalar=0.0, in1=qkv_out[:, 1, :],
                                         op0=ALU.max, op1=ALU.add).then_inc(k_ready, 1)
                dve.wait_ge(k_ready, i + 2)
                dve.wait_ge(k_max_done, i + 1)
                dve.tensor_tensor(k_max, k_max, qkv_out[:, 1, :], ALU.max).then_inc(k_max_done, 1)

            top_steps = Steps(dve, top_own)
            dve.wait_ge(k_max_turned, 1)
            top_steps.then(dve.tensor_reduce(k_top_col, bank[0][:, :].rearrange("p (c j) -> p c j", c=KC), X, ALU.max))
            for c in range(KC):
                top_steps.done(dve.tensor_scalar(top_diag[:, c, :], ident[:, :], k_top_col[:, c:c + 1], None, ALU.mult))
            dve.wait_ge(top_spread, 1)
            dve.tensor_copy(k_top, bank[1][:, :]).then_inc(k_top_ready, 1)
            dve.wait_ge(k_top_ready, 1)
            context = Steps(dve, ctx_own)
            context.then(dve.memset(ctx_t.rearrange("p a b -> p (a b)"), 0.0))

            def shift_k(b, turn):
                dve.wait_ge(kv_landed[b], turn * 16 + 16)
                dve.tensor_tensor(kv_in[b][:, 0, :], kv_in[b][:, 0, :], k_top, ALU.subtract).then_inc(k_shifted, 1)

            def keep_gin(t):
                dve.wait_ge(gin_done, t + 2)
                dve.tensor_tensor(agg_tile(t), bank[4][:, :], b2_row, ALU.add).then_inc(gin_kept, 1)

            shift_k(0, 0)
            dve.wait_ge(wgin_landed, 16 * WGIN)
            with dve.Fori(0, (TILES - 1) // AHEAD) as g:
                for k in range(AHEAD):
                    shift_k((k + 1) % AHEAD, g + (k + 1) // AHEAD)
                    keep_gin(g * AHEAD + k)
            keep_gin(TILES - 1)
            dve.wait_ge(kv_used, TILES)
            for h in range(2):
                side = slice(h * HD, (h + 1) * HD)
                context.done(dve.tensor_copy(ctx_t[side, :, side],
                                             bank[2][side, :].rearrange("p (a b) -> p a b", a=KC)[:, :, side]))
            context.done(dve.reciprocal(k_sum, bank[3][:, 0:KC]))
            assert context.count == CTX_STEPS

            dve.wait_ge(wmix_landed, 16 * WMIX)
            dve.wait_ge(gin_kept, TILES + 1)

            def residual(t):
                dve.wait_ge(att_done, t + 1)
                dve.wait_ge(xb_ready, t + 1)
                dve.tensor_tensor(xa, bank[3][:, :], x_b, ALU.add).then_inc(xa_done, 1)
                dve.wait_ge(xa_done, t + 1)
                dve.scalar_tensor_tensor(out=agg_tile(t), in0=agg_tile(t), scalar=0.0, in1=xa, op0=ALU.max, op1=ALU.add
                                         ).then_inc(x1_ready, 1)
                dve.wait_ge(x1_ready, t + 1)
                dve.sem_inc(dve_mark, 1)
                dve.bn_stats(st6, agg_tile(t)).then_inc(ln_own, 1)
                dve.wait_ge(ln_own, t * 3 + 1)
                dve.sem_inc(dve_mark, 1)
                dve.bn_aggr(mv2, st6).then_inc(ln_own, 1)
                dve.wait_ge(ln_own, t * 3 + 2)
                dve.tensor_scalar(var2, mv2[:, 1:2], EPS, None, ALU.add).then_inc(var_ready, 1)
                dve.tensor_copy(mean_all[:, bass.ds(t, 1)], mv2[:, 0:1]).then_inc(ln_own, 1)
                dve.wait_ge(rs_ready, t + 1)
                wait_from(dve, xm_turned, t)
                dve.tensor_scalar(xm_now, agg_tile(t), mv2[:, 0:1], rs_all[:, bass.ds(t, 1)], ALU.subtract, ALU.mult
                                  ).then_inc(xm_ready, 1)

            def keep_logits(t):
                dve.wait_ge(lg_done, t + 1)
                dve.tensor_tensor(logits[:, bass.ds(t * EE, EE)], bank[6][:, 0:EE], br_row, ALU.add
                                  ).then_inc(lg_ready, 1)

            for t in range(3):
                residual(t)
            with dve.Fori(3, TILES) as t:
                keep_logits(t - 3)
                residual(t)
            for t in range(TILES - 3, TILES):
                keep_logits(t)

            route = Steps(dve, route_own)
            dve.wait_ge(lg_ready, TILES)

            def by_expert(ap):
                return ap.rearrange("p (a e) -> p a e", e=E)

            def flat(ap):
                return ap.rearrange("p a e -> p (a e)")

            route.then(dve.tensor_reduce(top, by_expert(logits), X, ALU.max))
            route.done(dve.tensor_tensor(less, by_expert(logits), spread(top, E), ALU.subtract))
            assert route.count == ROUTE_LESS
            route.then(dve.tensor_scalar(first_best, count[:, 0:E], -1.0, float(E), ALU.mult, ALU.add))
            route.then(dve.tensor_scalar(key, less, 0.0, None, ALU.is_equal))
            route.then(dve.tensor_tensor(key, key, repeat(first_best, TB), ALU.mult))
            route.then(dve.tensor_reduce(top, key, X, ALU.max))
            route.then(dve.tensor_tensor(hot, key, spread(top, E), ALU.is_equal))
            route.done(dve.tensor_copy(hot16, flat(hot)))
            assert route.count == ROUTE_HOT
            dve.wait_ge(expo_done, 1)
            route.then(dve.tensor_reduce(gate, expo, X, ALU.add))
            route.then(dve.reciprocal(gate, gate))
            dve.wait_ge(hot_summed, 4)
            half = TILES * EE // 2
            for h in range(2):
                cols = slice(h * half, (h + 1) * half)
                route.done(dve.tensor_copy(before[:, cols], bank[h][:, 0:half]))
                route.done(dve.tensor_copy(tile_n[:, cols], bank[2 + h][:, 0:half]))
            route.wait()
            dve.sem_inc(counts_read, 2)
            def of_expert(ap, be):
                return ap.rearrange("p (t e) -> p e t", e=EE)[:, be, :]

            for be in range(EE):
                route.done(dve.tensor_tensor_scan(of_expert(tile_inc, be), ones32[:, 0:TILES], of_expert(tile_n, be),
                                                  0.0, ALU.mult, ALU.add))
            route.wait()
            total = tile_inc[:, (TILES - 1) * EE:]
            route.then(dve.tensor_scalar(tile_bound, count[:, 0:TILES], float(P), None, ALU.mult))
            fits = place.rearrange("p (e t) -> p e t", e=EE)
            route.then(dve.tensor_tensor(fits, spread(total, TILES), repeat(tile_bound, EE), ALU.is_gt))
            route.then(dve.tensor_reduce(n_tiles, fits, X, ALU.add))
            for b in range(BANKS):
                of = slice(b * E, (b + 1) * E)
                route.done(dve.tensor_tensor_scan(tile_end[:, of], ones32[:, 0:E], n_tiles[:, of],
                                                  float(b * BANK_TILES), ALU.mult, ALU.add))
            route.wait()
            route.then(dve.tensor_tensor(tile_row, tile_end, n_tiles, ALU.subtract))
            route.then(dve.tensor_scalar(tile_row, tile_row, float(P), None, ALU.mult))
            route.then(dve.tensor_tensor(place, before, tile_inc, ALU.add))
            route.then(dve.tensor_tensor(place, place, tile_n, ALU.subtract))
            route.then(dve.tensor_tensor(key, hot, by_expert(place), ALU.mult))
            route.then(dve.tensor_reduce(rank, key, X, ALU.add))
            route.then(dve.tensor_scalar(keep, rank, float(CAP), None, ALU.is_le))
            route.then(dve.tensor_tensor(gate, gate, keep, ALU.mult))
            route.then(dve.tensor_tensor(place.rearrange("p (t e) -> p t e", e=EE),
                                         place.rearrange("p (t e) -> p t e", e=EE), repeat(tile_row, TILES), ALU.add))
            route.then(dve.tensor_tensor(key, hot, by_expert(place), ALU.mult))
            route.then(dve.tensor_reduce(slot_f, key, X, ALU.add))
            route.then(dve.tensor_scalar(slot_i, slot_f, 1.0, None, ALU.subtract))
            route.done(dve.tensor_scalar(info[:, :, 0], tile_bound, pair_no[:, 0:1], None, ALU.add))
            route.done(dve.tensor_copy(info[:, :, 1:1 + BANKS], gate.rearrange("p (t b) -> p t b", b=BANKS)))
            route.wait()

            def stage_xm(t, k, before):
                dve.wait_ge(scattered[k], before * (16 * BANKS) + SCATTER_FROM)
                dve.tensor_scalar(stage[k][:, 0:D], agg_tile(t), mean_all[:, bass.ds(t, 1)], rs_all[:, bass.ds(t, 1)],
                                  ALU.subtract, ALU.mult).then_inc(staged, 1)
                dve.tensor_copy(slot_now[:, 2 * k:2 * k + 2], slot_i[:, bass.ds(t * BANKS, BANKS)]).then_inc(staged, 1)
                dve.tensor_copy(stage[k][:, D:ROW], info.rearrange("p t i -> p (t i)")
                                [:, bass.ds(t * (1 + BANKS), 1 + BANKS)]).then_inc(staged, 1)

            def keep_shared(t):
                dve.wait_ge(sh_down, t + 1)
                dve.tensor_tensor(agg_tile(t), bank[7][:, :], agg_tile(t), ALU.add).then_inc(shared_added, 1)

            def slot_tables():
                route.then(dve.tensor_tensor(wide, repeat(tile_end, SLOT_TILES), spread(count[:, 0:SLOT_TILES], EE),
                                             ALU.is_le))
                route.then(dve.tensor_reduce(expert_f, wide, X, ALU.add))
                for b in range(BANKS):
                    of = slice(b * BANK_TILES, (b + 1) * BANK_TILES)
                    last = float((b + 1) * E - 1)
                    route.done(dve.tensor_scalar(weight_at[:, of], expert_f[:, of], last, float(EXPERT_W), ALU.min,
                                                 ALU.mult))
                    route.done(dve.tensor_scalar(bias_at[:, of], expert_f[:, of], last, float(FF), ALU.min,
                                                 ALU.mult))
                    route.then(dve.tensor_scalar(expert_f[:, of], expert_f[:, of], last, float(b * E), ALU.min,
                                                 ALU.subtract))
                    route.done(dve.tensor_scalar(bias2_at[:, of], expert_f[:, of], float(D), None, ALU.mult))
                route.wait()
                dve.sem_inc(routed, 1)
                dve.memset(edge_node[:, :, :], 0.0).then_inc(o_set, 1)

            def shared(t, k, before):
                stage_xm(t, k, before)
                if isinstance(t, int) and t == 4:
                    slot_tables()
                if not isinstance(t, int) or t >= 3:
                    keep_shared(t - 3)

            each_stage(dve, shared)
            for t in range(TILES - 3, TILES):
                keep_shared(t)

            dve.wait_ge(b1_landed, 16 * BANKS)

            def add_bias(j, k):
                at = dve.value_load(bias_at[0:1, bass.ds(j, 1)], min_val=0, max_val=(EE - 1) * FF)
                dve.wait_ge(e_up, j + 1)
                dve.tensor_tensor(he[k % 2], bank[2 + k % 2][:, 0:FF], b1_all[:, bass.ds(at, FF)], ALU.add
                                  ).then_inc(e_biased, 1)

            def turn_hidden(j, k):
                dve.wait_ge(e_turned, j + 1)
                dve.tensor_copy(he_t[k % 2].rearrange("p a b -> p (a b)"), bank[4 + k % 2][:, 0:FF]
                                ).then_inc(he_t_ready, 1)

            def result(g, k, b):
                j = g * UNROLL + k
                at = dve.value_load(bias2_at[0:1, bass.ds(j, 1)], min_val=0, max_val=(E - 1) * D)
                dve.wait_ge(e_down, j + 1)
                dve.wait_ge(y_scattered[k % 2], g * (8 * UNROLL) + (Y_FROM + 16 * (k // 2)))
                dve.tensor_tensor(ye[k % 2], bank[6 + k % 2][:, :], b2_all[b][:, bass.ds(at, D)], ALU.add
                                  ).then_inc(e_own, 1)
                dve.wait_ge(o_landed[k % 2], g * (8 * UNROLL) + (Y_FROM + 16 * (k // 2 + 1)))
                dve.wait_ge(e_own, j + 1)
                dve.sem_inc(dve_mark, 1)
                dve.scalar_tensor_tensor(out=ye[k % 2], in0=ye[k % 2], scalar=gate_now[k % UNROLL], in1=o_in[k % 2],
                                         op0=ALU.mult, op1=ALU.add).then_inc(e_out, 1)

            def filled(g, k, b):
                turn_hidden(g * UNROLL + (k - 1), k + 1)
                add_bias(g * UNROLL + k, k)
                result(g, k - 1, b)

            for k in range(STAGES):
                dve.wait_ge(scattered[k], SCATTERED[k])
            add_bias(0, 0)
            dve.wait_ge(b2_landed, 16)
            for k in range(1, UNROLL):
                filled(0, k, 0)
            with dve.Fori(1, BANK_TURNS) as g:
                for k in range(UNROLL):
                    filled(g, k, 0)
            filled(BANK_TURNS, 0, 0)
            dve.wait_ge(b2_landed, 32)
            for k in range(1, UNROLL):
                filled(BANK_TURNS, k, 1)
            with dve.Fori(BANK_TURNS + 1, BANKS * BANK_TURNS) as g:
                for k in range(UNROLL):
                    filled(g, k, 1)
            turn_hidden(SLOT_TILES - 1, 1)
            result(BANKS * BANK_TURNS - 1, UNROLL - 1, 1)


_INS = ["x", "src", "dst", "L0_gnn_W1", "L0_gnn_b1", "L0_gnn_W2", "L0_gnn_b2", "L0_mix_w_qkv", "L0_mix_w_proj",
        "L0_mix_b_proj", "L0_ffn_Wr_sp", "L0_ffn_br_sp", "L0_ffn_Wr_fq", "L0_ffn_br_fq", "L0_ffn_Ws1", "L0_ffn_bs1",
        "L0_ffn_Ws2", "L0_ffn_bs2", "L0_ffn_W1_sp", "L0_ffn_b1_sp", "L0_ffn_W2_sp", "L0_ffn_b2_sp", "L0_ffn_W1_fq",
        "L0_ffn_b1_fq", "L0_ffn_W2_fq", "L0_ffn_b2_fq"]


def kernel(**inputs):
    import numpy as _np
    import concourse.bacc as _bacc
    from concourse import mybir as _mybir
    from concourse.bass_utils import run_bass_kernel_spmd as _run

    nc = _bacc.Bacc("TRN2", target_bir_lowering=False, num_devices=1)
    arrays, args = {}, []
    for name in _INS:
        a = _np.ascontiguousarray(inputs[name])
        arrays[f"in_{name}_dram"] = a
        args.append(nc.dram_tensor(f"in_{name}_dram", a.shape, _mybir.dt.from_np(a.dtype), kind="ExternalInput").ap())
    args.append(nc.dram_tensor("out_0_dram", (N, D), _mybir.dt.float32, kind="ExternalOutput").ap())
    gps_layer(nc, *args)
    r = _run(nc, [arrays], core_ids=[0])
    return r.results[0]["out_0_dram"]
```
